# Optimizing a Trainium2 kernel written in Bass

```python
import numpy as np
import jax
import jax.numpy as jnp

def _softmax(x, axis=-1):
    return jax.nn.softmax(x, axis=axis)

def _gelu(x):
    return jax.nn.gelu(x, approximate=True)

def _silu(x):
    return jax.nn.silu(x)

def _sigmoid(x):
    return jax.nn.sigmoid(x)

def _layernorm(x, axis=-1, eps=1e-05):
    m = jnp.mean(x, axis=axis, keepdims=True)
    v = jnp.var(x, axis=axis, keepdims=True)
    return (x - m) / jnp.sqrt(v + eps)

def _scatter_add(tgt, idx, src, axis=0):
    return tgt.at[idx].add(src)

def _segment_sum(src, seg, n):
    return jax.ops.segment_sum(src, seg, n)
kernel_name = 'mk_gnn_ffn_d2_gnn_r8_5c246f'

def setup_inputs(seed: int=0):
    np.random.seed(seed)
    _w = jnp.asarray

    def _rec_inputs():
        import jax
        import jax.numpy as jnp
        _gk = jax.random.key(seed)
        x = -0.0003713 + 1 * jax.random.normal(jax.random.fold_in(_gk, 1), (6250, 256), jnp.float32)
        _s = jax.random.randint(jax.random.fold_in(_gk, 2), (100000,), 0, 6250, jnp.int32)
        _d = jax.random.randint(jax.random.fold_in(_gk, 3), (100000,), 0, 6250, jnp.int32)
        _loop = jnp.arange(6250, dtype=jnp.int32)
        src = jnp.concatenate([_s, _d, _loop])
        dst = jnp.concatenate([_d, _s, _loop])
        _o = jnp.argsort(dst, stable=True)
        src = src[_o]
        dst = dst[_o]
        edge_weight = jax.random.uniform(jax.random.fold_in(_gk, 12), (206250,), jnp.float32, 0.0, 0.999998)
        return (x, src, dst, edge_weight)
    x, src, dst, edge_weight = _rec_inputs()

    def _L0_gnn_setup():
        import jax, jax.numpy as jnp
        import numpy as np
        N_NODES = 6250
        N_EDGES = 37500
        D_IN = 256
        D_OUT = 256
        key = jax.random.key(seed)
        k1, k2, k3, k4 = jax.random.split(key, 4)
        x = jax.random.normal(k1, (N_NODES, D_IN), dtype=jnp.float32)
        edge_index = jax.random.randint(k2, (2, N_EDGES), 0, N_NODES, dtype=jnp.int64)
        edge_weight = jax.random.uniform(k3, (N_EDGES,), dtype=jnp.float32)
        W = jax.random.normal(k4, (D_OUT, D_IN), dtype=jnp.float32) * (1.0 / np.sqrt(D_IN))
        return {'x': x, 'edge_index': edge_index, 'edge_weight': edge_weight, 'W': W}
    _L0_gnn_all = _L0_gnn_setup()
    _L0_gnn_in = {k: v for k, v in _L0_gnn_all.items() if k in ('W',)}
    del _L0_gnn_all

    def _L0_ffn_setup():
        import jax, jax.numpy as jnp
        import numpy as np
        E, D, H, TOP_K = (6, 256, 256, 2)
        ROUTER_H = D // 2
        key = jax.random.key(seed)
        ks = jax.random.split(key, 12)
        s = 1.0 / np.sqrt(D)
        sh = 1.0 / np.sqrt(H)
        sr = 1.0 / np.sqrt(ROUTER_H)
        return {'features': jax.random.normal(ks[0], (8, 512, D), dtype=jnp.float32), 'router_w1': jax.random.uniform(ks[1], (D, ROUTER_H), jnp.float32, -s, s), 'router_b1': jnp.zeros((ROUTER_H,), jnp.float32), 'router_w2': jax.random.uniform(ks[2], (ROUTER_H, E), jnp.float32, -sr, sr), 'router_b2': jnp.zeros((E,), jnp.float32), 'expert_w1': jax.random.uniform(ks[3], (E, D, H), jnp.float32, -s, s), 'expert_b1': jnp.zeros((E, H), jnp.float32), 'expert_w2': jax.random.uniform(ks[4], (E, H, H), jnp.float32, -sh, sh), 'expert_b2': jnp.zeros((E, H), jnp.float32), 'expert_w3': jax.random.uniform(ks[5], (E, H, D), jnp.float32, -sh, sh), 'expert_b3': jnp.zeros((E, D), jnp.float32)}
    _L0_ffn_all = _L0_ffn_setup()
    _L0_ffn_in = {k: v for k, v in _L0_ffn_all.items() if k in ('router_w1', 'router_b1', 'router_w2', 'router_b2', 'expert_w1', 'expert_b1', 'expert_w2', 'expert_b2', 'expert_w3', 'expert_b3')}
    del _L0_ffn_all

    def _L1_gnn_setup():
        import jax, jax.numpy as jnp
        import numpy as np
        N = 12500
        E = 200000
        C_IN = 256
        H = 2
        D = 128
        ALPHA = 0.2
        key = jax.random.key(seed)
        ks = jax.random.split(key, 5)
        x = jax.random.normal(ks[0], (N, C_IN), dtype=jnp.float32)
        edge_index = jax.random.randint(ks[1], (2, E), 0, N, dtype=jnp.int64)
        W = jax.random.normal(ks[2], (H, D, C_IN), dtype=jnp.float32) * 0.05
        b = jax.random.normal(ks[3], (H, D), dtype=jnp.float32) * 0.05
        a = jax.random.normal(ks[4], (H, 2 * D), dtype=jnp.float32) * 0.05
        return {'x': x, 'edge_index': edge_index, 'W': W, 'b': b, 'a': a, 'n': N}
    _L1_gnn_all = _L1_gnn_setup()
    _L1_gnn_in = {k: v for k, v in _L1_gnn_all.items() if k in ('W', 'b', 'a')}
    del _L1_gnn_all

    def _L1_ffn_setup():
        import jax, jax.numpy as jnp
        import numpy as np
        B, S, H, F, E, K = (8, 512, 256, 512, 16, 2)
        EPS = 1e-05
        key = jax.random.key(seed)
        ks = jax.random.split(key, 9)
        sc = 0.02
        return {'x': jax.random.normal(ks[0], (B, S, H), dtype=jnp.float32), 'gate_w': jax.random.normal(ks[1], (H, E), dtype=jnp.float32) * sc, 'gate_b': jnp.zeros((E,), dtype=jnp.float32), 'w1': jax.random.normal(ks[2], (E, H, F), dtype=jnp.float32) * sc, 'b1': jnp.zeros((E, F), dtype=jnp.float32), 'w2': jax.random.normal(ks[3], (E, F, H), dtype=jnp.float32) * sc, 'b2': jnp.zeros((E, H), dtype=jnp.float32), 'gamma': jnp.ones((H,), dtype=jnp.float32), 'beta': jnp.zeros((H,), dtype=jnp.float32)}
    _L1_ffn_all = _L1_ffn_setup()
    _L1_ffn_in = {k: v for k, v in _L1_ffn_all.items() if k in ('gate_w', 'gate_b', 'w1', 'b1', 'w2', 'b2', 'gamma', 'beta')}
    del _L1_ffn_all
    return {'x': x, 'src': src, 'dst': dst, 'edge_weight': edge_weight, 'L0_gnn_W': _L0_gnn_in['W'], 'L0_ffn_router_w1': _L0_ffn_in['router_w1'], 'L0_ffn_router_b1': _L0_ffn_in['router_b1'], 'L0_ffn_router_w2': _L0_ffn_in['router_w2'], 'L0_ffn_router_b2': _L0_ffn_in['router_b2'], 'L0_ffn_expert_w1': _L0_ffn_in['expert_w1'], 'L0_ffn_expert_b1': _L0_ffn_in['expert_b1'], 'L0_ffn_expert_w2': _L0_ffn_in['expert_w2'], 'L0_ffn_expert_b2': _L0_ffn_in['expert_b2'], 'L0_ffn_expert_w3': _L0_ffn_in['expert_w3'], 'L0_ffn_expert_b3': _L0_ffn_in['expert_b3'], 'L1_gnn_W': _L1_gnn_in['W'], 'L1_gnn_b': _L1_gnn_in['b'], 'L1_gnn_a': _L1_gnn_in['a'], 'L1_ffn_gate_w': _L1_ffn_in['gate_w'], 'L1_ffn_gate_b': _L1_ffn_in['gate_b'], 'L1_ffn_w1': _L1_ffn_in['w1'], 'L1_ffn_b1': _L1_ffn_in['b1'], 'L1_ffn_w2': _L1_ffn_in['w2'], 'L1_ffn_b2': _L1_ffn_in['b2'], 'L1_ffn_gamma': _L1_ffn_in['gamma'], 'L1_ffn_beta': _L1_ffn_in['beta']}

def reference(x, src, dst, edge_weight, L0_gnn_W, L0_ffn_router_w1, L0_ffn_router_b1, L0_ffn_router_w2, L0_ffn_router_b2, L0_ffn_expert_w1, L0_ffn_expert_b1, L0_ffn_expert_w2, L0_ffn_expert_b2, L0_ffn_expert_w3, L0_ffn_expert_b3, L1_gnn_W, L1_gnn_b, L1_gnn_a, L1_ffn_gate_w, L1_ffn_gate_b, L1_ffn_w1, L1_ffn_b1, L1_ffn_w2, L1_ffn_b2, L1_ffn_gamma, L1_ffn_beta):
    import jax
    import jax.numpy as jnp

    def _L0_gnn_ref(x, edge_index, edge_weight, W):
        import jax, jax.numpy as jnp
        import numpy as np
        N_NODES = 6250
        N_EDGES = 37500
        D_IN = 256
        D_OUT = 256
        x_proj = jnp.einsum('nd,od->no', x, W)
        dst = edge_index[0]
        src = edge_index[1]
        msgs = edge_weight[:, None] * x_proj[src]
        out = jax.ops.segment_sum(msgs, dst, num_segments=N_NODES)
        return out

    def _L0_ffn_ref(features, router_w1, router_b1, router_w2, router_b2, expert_w1, expert_b1, expert_w2, expert_b2, expert_w3, expert_b3):
        import jax, jax.numpy as jnp
        import numpy as np
        E, D, H, TOP_K = (6, 256, 256, 2)
        ROUTER_H = D // 2
        rh = jax.nn.relu(features @ router_w1 + router_b1)
        expert_logits = jax.nn.softmax(rh @ router_w2 + router_b2, axis=-1)
        top_w, top_i = jax.lax.top_k(expert_logits, TOP_K)
        routing_weights = jax.nn.softmax(top_w, axis=-1)
        h1 = jax.nn.relu(jnp.einsum('bsd,edh->bseh', features, expert_w1) + expert_b1)
        h2 = jax.nn.relu(jnp.einsum('bseh,ehf->bsef', h1, expert_w2) + expert_b2)
        expert_out = jnp.einsum('bsef,efo->bseo', h2, expert_w3) + expert_b3
        sel = jnp.take_along_axis(expert_out, top_i[:, :, :, None], axis=2)
        combined = jnp.sum(sel * routing_weights[..., None], axis=2)
        return combined

    def _L1_gnn_ref(x, edge_index, W, b, a, n):
        import jax, jax.numpy as jnp
        import numpy as np
        N = 12500
        E = 200000
        C_IN = 256
        H = 2
        D = 128
        ALPHA = 0.2
        src = edge_index[0]
        dst = edge_index[1]

        def head(Wh, bh, ah):
            h = x @ Wh.T + bh
            s_src = h @ ah[:D]
            s_dst = h @ ah[D:]
            score = s_src[src] + s_dst[dst]
            lrelu = jnp.where(score > 0, score, ALPHA * score)
            e = jnp.exp(-lrelu)
            row_sum = jax.ops.segment_sum(e, src, num_segments=n)
            num = jax.ops.segment_sum(e[:, None] * h[dst], src, num_segments=n)
            h_prime = num / row_sum[:, None]
            return jax.nn.elu(h_prime)
        outs = jax.vmap(head)(W, b, a)
        return jnp.moveaxis(outs, 0, 1).reshape(x.shape[0], H * D)

    def _L1_ffn_ref(x, gate_w, gate_b, w1, b1, w2, b2, gamma, beta):
        import jax, jax.numpy as jnp
        import numpy as np
        B, S, H, F, E, K = (8, 512, 256, 512, 16, 2)
        EPS = 1e-05
        gate_logits = x @ gate_w + gate_b
        topk_vals, topk_idx = jax.lax.top_k(gate_logits, K)
        topk_w = jax.nn.softmax(topk_vals, axis=-1)
        h = jax.nn.relu(jnp.einsum('bsh,ehf->bsef', x, w1) + b1)
        expert_out = jnp.einsum('bsef,efh->bseh', h, w2) + b2
        sel = jnp.take_along_axis(expert_out, topk_idx[:, :, :, None], axis=2)
        moe = jnp.sum(topk_w[..., None] * sel, axis=2)
        y = x + moe
        mu = jnp.mean(y, axis=-1, keepdims=True)
        var = jnp.var(y, axis=-1, keepdims=True)
        return (y - mu) / jnp.sqrt(var + EPS) * gamma + beta
    edge_index = jnp.stack([src, dst])
    x = x + _L0_gnn_ref(_layernorm(x, axis=-1), edge_index, edge_weight, L0_gnn_W)
    x = x + _L0_ffn_ref(_layernorm(x, axis=-1)[None], L0_ffn_router_w1, L0_ffn_router_b1, L0_ffn_router_w2, L0_ffn_router_b2, L0_ffn_expert_w1, L0_ffn_expert_b1, L0_ffn_expert_w2, L0_ffn_expert_b2, L0_ffn_expert_w3, L0_ffn_expert_b3)[0]
    x = x + _L1_gnn_ref(_layernorm(x, axis=-1), edge_index, L1_gnn_W, L1_gnn_b, L1_gnn_a, 6250)
    x = x + _L1_ffn_ref(_layernorm(x, axis=-1)[None], L1_ffn_gate_w, L1_ffn_gate_b, L1_ffn_w1, L1_ffn_b1, L1_ffn_w2, L1_ffn_b2, L1_ffn_gamma, L1_ffn_beta)[0]
    return x

_drawn_inputs = setup_inputs


def setup_inputs(seed=0):
    import zlib

    import numpy as np

    out = dict(_drawn_inputs(seed))
    spreads = {'L0_ffn_router_b1': (0.0, 0.686),
     'L0_ffn_router_b2': (0.0, 0.458),
     'L0_ffn_expert_b1': (0.0, 0.8),
     'L0_ffn_expert_b2': (0.0, 0.8),
     'L0_ffn_expert_b3': (0.0, 0.37),
     'L1_ffn_gate_b': (0.0, 0.585),
     'L1_ffn_b1': (0.0, 0.8),
     'L1_ffn_b2': (0.0, 0.491),
     'L1_ffn_gamma': (1.0, 0.2),
     'L1_ffn_beta': (0.0, 0.375)}
    factors = {'L0_ffn_expert_w1': 3.554,
     'L0_ffn_expert_w2': 3.21,
     'L1_gnn_b': 4.471,
     'L1_gnn_a': 4.812,
     'L1_ffn_w1': 4.088,
     'L1_ffn_w2': 3.25}
    for name, (base, spread) in spreads.items():
        noise = np.random.default_rng([zlib.crc32(name.encode()), seed]).standard_normal(out[name].shape)
        drawn = base * np.exp(spread * noise) if base else spread * noise
        out[name] = jnp.asarray(drawn.astype(out[name].dtype))
    for name, factor in factors.items():
        out[name] = (out[name] * factor).astype(out[name].dtype)
    return out
```

```python
from contextlib import ExitStack, contextmanager

import concourse.bass as bass
from concourse import mybir

ALU = mybir.AluOpType
ACT = mybir.ActivationFunctionType
AX = mybir.AxisListType
F32 = mybir.dt.float32
BF16 = mybir.dt.bfloat16
I32 = mybir.dt.int32

P = 128
EPS = 1e-5
SLOPE = 0.2

N, D, EDGES = 6250, 256, 206250
NT = -(-N // P)
LAST = N - (NT - 1) * P
KD = D // P

LANE = -(-EDGES // P)
LANE_LAST = EDGES - (P - 1) * LANE
CHUNK = 26
NCHUNK = LANE // CHUNK
BUCKETS = NT + 1
assert NCHUNK * CHUNK == LANE and NCHUNK % 2 == 0

GROUP = 512
GB = GROUP // P
RING = 4
NGROUP = -(-(((EDGES + NT * (GROUP - 1)) // GROUP)) // RING) * RING
SLOTS = NGROUP * GROUP
REC = 3
assert P * (LANE + 0) - EDGES <= P

HD = D // 2
HW = HD + 1
ROW1 = 2 * HW + 2


class Count:

    def __init__(self):
        self.n, self.i, self.k = 0, None, 0

    def enter(self, i, per, start=0):
        self.i, self.per, self.k, self.start = i, per, 0, start

    def next(self):
        if self.i is None:
            self.n += 1
            return self.n
        self.k += 1
        return self.i * self.per + (self.n + self.k - self.start * self.per)

    def leave(self, count):
        assert self.k == self.per, (self.k, self.per)
        self.n += self.per * count
        self.i = None


def peeled(engine, count, body):
    body(0, True)
    with engine.Fori(1, count) as i:
        body(i, False)


@contextmanager
def stage(nc, kept):
    own = []

    def sem(name):
        own.append(nc.alloc_semaphore(name=name))
        return own[-1]

    yield sem, kept
    nc.clear_and_free_semaphores(own)
    nc.all_engine_barrier()


def tile_rows(dram, t):
    return dram[bass.ds(t * P, P), :]


def spread(ap, n):
    return ap.unsqueeze(1).to_broadcast([ap.shape[0], n, ap.shape[1]])


def widen(ap, n):
    return ap.unsqueeze(2).to_broadcast([ap.shape[0], ap.shape[1], n])


def sort_and_project(nc, sem, bank, c, a, dram):
    with ExitStack() as ctx, stage(nc, sem) as (sem, pool_sem):
        sb = lambda n, s, d: ctx.enter_context(nc.sbuf_tensor(n, s, d))
        X, ident, tri, ones, iota = c["X"], c["ident"], c["tri"], c["ones"], c["iota"]
        lane_src = sb("lane_src", [P, LANE], I32)
        lane_dst = sb("lane_dst", [P, LANE], I32)
        lane_w = sb("lane_w", [P, LANE], F32)
        tile_i = sb("tile_i", [P, LANE], I32)
        tile_f = sb("tile_f", [P, LANE], F32)
        rec = sb("rec", [P, LANE, REC], I32)
        rec_f = rec[:, :, :].bitcast(F32)
        hits = sb("hits", [P, LANE], BF16)
        fill = sb("fill", [P, SLOTS // P // 8, REC], F32)
        bucket_iota = sb("bucket_iota", [P, BUCKETS, CHUNK], F32)
        carry_mask = sb("carry_mask", [P, BUCKETS, CHUNK], F32)
        member = sb("member", [P, BUCKETS, CHUNK], F32)
        ranks = sb("ranks", [P, BUCKETS, CHUNK], F32)
        own = sb("own", [P, BUCKETS, CHUNK], F32)
        first_col = sb("first_col", [P, BUCKETS], F32)
        run = sb("run", [P, BUCKETS], F32)
        lane_count = sb("lane_count", [P, BUCKETS], F32)
        groups_i = sb("groups_i", [P, 2, BUCKETS], I32)
        groups = sb("groups", [P, BUCKETS], F32)
        group_end = sb("group_end", [P, BUCKETS], F32)
        group_start = sb("group_start", [P, BUCKETS], F32)
        NQ = -(-NGROUP // P)
        group_no = sb("group_no", [P, NQ], F32)
        past = sb("past", [P, NQ, NT], F32)
        tid_f = sb("tid_f", [P, NQ], F32)
        tid_i = sb("tid_i", [P, NQ], I32)
        pos_f = sb("pos_f", [P, CHUNK], F32)
        pos_ring = sb("pos_ring", [P, 2, CHUNK], I32)
        rec_ring = sb("rec_ring", [P, 2, CHUNK, REC], I32)
        Wn = sb("Wn", [P, KD, D], F32)
        WT = sb("WT", [P, KD, D], F32)
        stats = sb("stats", [P, 2, 6], F32)
        moments = sb("moments", [P, 2, 2], F32)
        dev = sb("dev", [P, 2], F32)
        rstd = sb("rstd", [P, 2], F32)
        xn = sb("xn", [P, 2, D], F32)
        xT = sb("xT", [P, 2, KD, P], F32)
        xp = sb("xp", [P, 2, D], F32)

        zeros = sb("zeros", [P, D], F32)
        cleared = sem("a_cleared")
        pads_set = sem("a_pads_set")
        fill_set = sem("a_fill_set")
        consts_set = sem("a_consts_set")
        edges_in = sem("a_edges_in")
        x_in = sem("a_x_in")
        w_in = sem("a_w_in")
        filled = sem("a_filled")
        w_turned = sem("a_w_turned")
        w_ready = sem("a_w_ready")
        dve_done = sem("a_dve_done")
        counted = sem("a_counted")
        summed = sem("a_summed")
        ranked = sem("a_ranked")
        scattered = [pool_sem(f"a_scattered{s}") for s in range(2)]
        var_ready = sem("a_var_ready")
        dev_ready = sem("a_dev_ready")
        xn_ready = sem("a_xn_ready")
        x_turned = sem("a_x_turned")
        xT_ready = sem("a_xT_ready")
        projected = sem("a_projected")
        xp_ready = sem("a_xp_ready")
        stored = [sem(f"a_stored{s}") for s in range(2)]
        tid_ready = sem("a_tid_ready")
        tid_out = sem("a_tid_out")
        tid_in = sem("a_tid_in")
        turn = sem("a_turn")
        pool_done = sem("a_pool_done")

        psW = bank[0][:, :].rearrange("p (k o) -> p k o", k=KD)
        psC = bank[1]
        psT = [bank[2 + s][:, 0:D].rearrange("p (k n) -> p k n", k=KD) for s in range(2)]
        psP = [bank[4 + s][:, 0:D] for s in range(2)]

        table = dram["table0"]
        sorted_edges = dram["sorted_edges"]

        with nc.Block() as block:

            @block.sync
            def _(sp):
                sp.wait_ge(pads_set, 4)
                cut = (P - 1) // 16 * 16
                for name, lanes in (("src", lane_src), ("dst", lane_dst), ("edge_weight", lane_w)):
                    flat = a[name]
                    for lo, hi in ((0, cut), (cut, P - 1)):
                        sp.dma_start(lanes[lo:hi, :], flat[lo * LANE:hi * LANE].rearrange(
                            "(p t) -> p t", t=LANE)).then_inc(edges_in, 16)
                    sp.dma_start(lanes[P - 1:P, 0:LANE_LAST], flat[(P - 1) * LANE:EDGES].rearrange(
                        "(p t) -> p t", p=1)).then_inc(edges_in, 16)
                full = (NT - 1) * P
                sp.dma_start(X[:, 0:NT - 1, :], a["x"][0:full, :].rearrange(
                    "(t p) d -> p t d", p=P)).then_inc(x_in, 16)
                sp.dma_start(X[0:LAST, NT - 1, :], a["x"][full:N, :]).then_inc(x_in, 16)
                sp.dma_start(Wn[:, :, :], a["L0_gnn_W"].rearrange("(k p) d -> p k d", p=P)).then_inc(w_in, 16)
                sp.wait_ge(fill_set, 3)
                part = SLOTS // 8
                for q in range(8):
                    sp.dma_start(sorted_edges[q * part:(q + 1) * part, :].rearrange(
                        "(p s) c -> p s c", p=P), fill[:, :, :].bitcast(I32)).then_inc(filled, 16)
                sp.dma_start(dram["sent"].rearrange("(p r) d -> p r d", p=P),
                             zeros[:, :].unsqueeze(1).to_broadcast([P, BLOCKS_MAX, D])).then_inc(cleared, 16)
                sp.wait_ge(tid_ready, 1)
                sp.dma_start(dram["group_tile"][0:NQ * P].rearrange("(p q) -> p q", p=P),
                             tid_i[:, :]).then_inc(tid_out, 16)
                sp.wait_ge(tid_out, 16)
                sp.dma_start(c["tid"][0:1, :], dram["group_tile"][0:NGROUP].rearrange(
                    "(p g) -> p g", p=1)).then_inc(tid_in, 16)
                with sp.Fori(0, NT // 2) as i:
                    for s in range(2):
                        sp.wait_ge(xp_ready, i * 2 + s + 1)
                        sp.dma_start(tile_rows(table, i * 2 + s), xp[:, s, :]).then_inc(stored[s], 16)
                sp.wait_ge(xp_ready, NT)
                sp.dma_start(tile_rows(table, NT - 1), xp[:, 0, :]).then_inc(stored[0], 16)
                sp.wait_ge(stored[0], 16 * (NT - NT // 2))
                sp.wait_ge(stored[1], 16 * (NT // 2))
                sp.wait_ge(tid_in, 16)
                sp.wait_ge(cleared, 16)

            @block.gpsimd
            def _(pool):
                nc.gpsimd.iota(bucket_iota[:, :, :], pattern=[[1, BUCKETS], [0, CHUNK]], base=0,
                               channel_multiplier=0, allow_small_or_imprecise_dtypes=True).then_inc(consts_set, 1)
                nc.gpsimd.iota(group_no[:, :], pattern=[[1, NQ]], base=0, channel_multiplier=NQ,
                               allow_small_or_imprecise_dtypes=True).then_inc(consts_set, 1)
                nc.gpsimd.iota(iota[:, :], pattern=[[1, P]], base=0, channel_multiplier=0,
                               allow_small_or_imprecise_dtypes=True).then_inc(consts_set, 1)
                nc.gpsimd.memset(ident[:, :], 0.0).then_inc(pool_done, 1)
                nc.gpsimd.memset(tri[:, :], 1.0).then_inc(pool_done, 1)
                nc.gpsimd.memset(ones[:, :], 1.0).then_inc(consts_set, 1)
                pool.wait_ge(pool_done, 2)
                nc.gpsimd.affine_select(out=ident[:, :], in_=ident[:, :], compare_op=ALU.not_equal, fill=1.0,
                                        base=0, pattern=[[-1, P]], channel_multiplier=1).then_inc(consts_set, 1)
                nc.gpsimd.affine_select(out=tri[:, :], in_=tri[:, :], compare_op=ALU.is_gt, fill=0.0,
                                        base=0, pattern=[[1, P]], channel_multiplier=-1).then_inc(consts_set, 1)
                pool.wait_ge(filled, 16 * 8)

                with pool.Fori(0, NCHUNK // 2) as i:
                    for s in range(2):
                        pool.wait_ge(ranked, i * 2 + s + 1)
                        pool.sem_inc(turn, 1)
                        for t in range(CHUNK):
                            nc.gpsimd.indirect_dma_start(
                                sorted_edges[:, :], bass.IndirectOffsetOnAxis(pos_ring[:, s, t:t + 1], 0),
                                rec_ring[:, s, t, :], None).then_inc(scattered[s], 16)
                for s in range(2):
                    pool.wait_ge(scattered[s], NCHUNK // 2 * CHUNK * 16)

            @block.vector
            def _(dve):
                steps = Count()

                def link(ins):
                    ins.then_inc(dve_done, 1)
                    dve.wait_ge(dve_done, steps.next())

                nc.vector.memset(lane_src[96:P, LANE_LAST:LANE], NT * P).then_inc(pads_set, 1)
                nc.vector.memset(lane_dst[96:P, LANE_LAST:LANE], 0).then_inc(pads_set, 1)
                nc.vector.memset(lane_w[96:P, LANE_LAST:LANE], 0.0).then_inc(pads_set, 1)
                nc.vector.memset(X[:, NT - 1, :], 0.0).then_inc(pads_set, 1)
                nc.vector.memset(zeros[:, :], 0.0).then_inc(fill_set, 1)
                nc.vector.memset(fill[:, :, 0], -1.0).then_inc(fill_set, 1)
                nc.vector.memset(fill[:, :, 1:REC], 0.0).then_inc(fill_set, 1)
                link(nc.vector.memset(carry_mask[:, :, :], 1.0))
                nc.vector.memset(carry_mask[:, :, 0], 0.0)
                dve.wait_ge(edges_in, 16 * 9)
                link(nc.vector.tensor_scalar(tile_i[:, :], lane_src[:, :], 7, None, ALU.arith_shift_right))
                link(nc.vector.tensor_copy(tile_f[:, :], tile_i[:, :]))
                link(nc.vector.tensor_scalar(tile_i[:, :], lane_src[:, :], P - 1, None, ALU.bitwise_and))
                nc.vector.tensor_copy(rec_f[:, :, 0], tile_i[:, :])
                nc.vector.tensor_copy(rec_f[:, :, 1], lane_w[:, :])
                nc.vector.tensor_copy(rec[:, :, 2], lane_dst[:, :])
                for b in range(BUCKETS):
                    link(nc.vector.tensor_scalar(hits[:, :], tile_f[:, :], float(b), None, ALU.is_equal,
                                                 ALU.add, accum_out=lane_count[:, b:b + 1]))
                dve.sem_inc(counted, 1)
                dve.wait_ge(summed, 1)
                link(nc.vector.tensor_scalar(groups_i[:, 0, :], psC[:, BUCKETS:2 * BUCKETS], float(GROUP - 1), None,
                                             ALU.add))
                link(nc.vector.tensor_scalar(groups_i[:, 1, :], groups_i[:, 0, :], GROUP.bit_length() - 1, None,
                                             ALU.arith_shift_right))
                link(nc.vector.tensor_copy(groups[:, :], groups_i[:, 1, :]))
                dve.wait_ge(consts_set, 6)
                link(nc.vector.tensor_tensor_scan(group_end[:, :], ones[:, 0:BUCKETS], groups[:, :], 0.0,
                                                  ALU.mult, ALU.add))
                link(nc.vector.tensor_tensor(group_start[:, :], group_end[:, :], groups[:, :], ALU.subtract))
                link(nc.vector.memset(group_start[:, NT:NT + 1], float(NGROUP)))
                link(nc.vector.scalar_tensor_tensor(run[:, :], group_start[:, :], float(GROUP), psC[:, 0:BUCKETS],
                                                    ALU.mult, ALU.add))
                link(nc.vector.tensor_tensor(past[:, :, :], spread(group_end[:, 0:NT], NQ),
                                             widen(group_no[:, :], NT), ALU.is_le))
                link(nc.vector.tensor_reduce(tid_f[:, :], past[:, :, :], AX.X, ALU.add))
                nc.vector.tensor_scalar(tid_i[:, :], tid_f[:, :], float(NT - 1), None, ALU.min).then_inc(tid_ready, 1)

                def rank(t0, s, wait_slot):
                    link(nc.vector.tensor_tensor(member[:, :, :], bucket_iota[:, :, :],
                                                 spread(tile_f[:, bass.ds(t0, CHUNK)], BUCKETS), ALU.is_equal))
                    link(nc.vector.tensor_copy(first_col[:, :], member[:, :, 0]))
                    link(nc.vector.tensor_tensor(member[:, :, 0], member[:, :, 0], run[:, :], ALU.add))
                    link(nc.vector.tensor_tensor_scan(ranks[:, :, :].rearrange("p b t -> p (b t)"),
                                                      carry_mask[:, :, :].rearrange("p b t -> p (b t)"),
                                                      member[:, :, :].rearrange("p b t -> p (b t)"), 0.0,
                                                      ALU.mult, ALU.add))
                    link(nc.vector.tensor_copy(member[:, :, 0], first_col[:, :]))
                    nc.vector.tensor_copy(run[:, :], ranks[:, :, CHUNK - 1])
                    link(nc.vector.tensor_tensor(own[:, :, :], member[:, :, :], ranks[:, :, :], ALU.mult))
                    link(nc.vector.tensor_reduce(pos_f[:, :], own[:, :, :].rearrange("p b t -> p t b"), AX.X,
                                                 ALU.add))
                    wait_slot()
                    nc.vector.tensor_scalar(pos_ring[:, s, :], pos_f[:, :], -1.0, None, ALU.add)
                    nc.vector.tensor_copy(rec_ring[:, s, :, :], rec[:, bass.ds(t0, CHUNK), :]).then_inc(ranked, 1)

                RANK_LINKS = 7

                dve.wait_ge(x_in, 32)

                def step(i, first):
                    steps.enter(i, 2 * RANK_LINKS + 2 * 3 + 2, 0 if first else 1)
                    for s in range(2):
                        def slot_free(s=s):
                            if not first:
                                dve.wait_ge(scattered[s], i * (16 * CHUNK))
                        rank((i * 2 + s) * CHUNK, s, slot_free)
                        link(nc.vector.bn_stats(stats[:, s, :], X[:, i * 2 + s, :]))
                        dve.sem_inc(turn, 1)
                        link(nc.vector.bn_aggr(moments[:, s, :], stats[:, s, :]))
                        link(nc.vector.tensor_scalar(moments[:, s, 1:2], moments[:, s, 1:2], EPS, None, ALU.add))
                        nc.vector.tensor_copy(dev[:, s:s + 1], moments[:, s, 1:2]).then_inc(var_ready, 1)
                        dve.wait_ge(dev_ready, i * 2 + s + 1)
                        link(nc.vector.reciprocal(rstd[:, s:s + 1], dev[:, s:s + 1]))
                        if not first:
                            dve.wait_ge(x_turned, i * 2 + s - 1)
                        nc.vector.tensor_scalar(xn[:, s, :], X[:, i * 2 + s, :], moments[:, s, 0:1],
                                                rstd[:, s:s + 1], ALU.subtract, ALU.mult).then_inc(xn_ready, 1)

                step(0, True)
                steps.leave(1)
                with dve.Fori(1, NT // 2) as i:
                    step(i, False)
                steps.leave(NT // 2 - 1)
                t = NT - 1
                link(nc.vector.bn_stats(stats[:, 0, :], X[:, t, :]))
                link(nc.vector.bn_aggr(moments[:, 0, :], stats[:, 0, :]))
                link(nc.vector.tensor_scalar(moments[:, 0, 1:2], moments[:, 0, 1:2], EPS, None, ALU.add))
                nc.vector.tensor_copy(dev[:, 0:1], moments[:, 0, 1:2]).then_inc(var_ready, 1)
                dve.wait_ge(dev_ready, NT)
                link(nc.vector.reciprocal(rstd[:, 0:1], dev[:, 0:1]))
                dve.wait_ge(x_turned, NT - 2)
                nc.vector.tensor_scalar(xn[:, 0, :], X[:, t, :], moments[:, 0, 0:1],
                                        rstd[:, 0:1], ALU.subtract, ALU.mult).then_inc(xn_ready, 1)
                with dve.Fori(NT // 2, NCHUNK // 2) as i:
                    steps.enter(i, 2 * RANK_LINKS, NT // 2)
                    for s in range(2):
                        rank((i * 2 + s) * CHUNK, s, lambda s=s: dve.wait_ge(scattered[s], i * (16 * CHUNK)))

            @block.scalar
            def _(act):
                act.wait_ge(w_turned, 1)
                nc.scalar.activation(WT[:, :, :], psW, ACT.Copy).then_inc(w_ready, 1)

                def step(t, s, first, i):
                    act.wait_ge(var_ready, t + 1)
                    nc.scalar.activation(dev[:, s:s + 1], dev[:, s:s + 1], ACT.Sqrt).then_inc(dev_ready, 1)
                    act.wait_ge(x_turned, t + 1)
                    if not first:
                        act.wait_ge(projected, t - 1)
                    nc.scalar.activation(xT[:, s, :, :], psT[s], ACT.Copy).then_inc(xT_ready, 1)
                    act.wait_ge(projected, t + 1)
                    if not first:
                        act.wait_ge(stored[s], i * 16)
                    nc.scalar.activation(xp[:, s, :], psP[s], ACT.Copy).then_inc(xp_ready, 1)

                for s in range(2):
                    step(s, s, True, 0)
                with act.Fori(1, NT // 2) as i:
                    for s in range(2):
                        step(i * 2 + s, s, False, i)
                step(NT - 1, 0, False, NT // 2)

            @block.tensor
            def _(pe):
                pe.wait_ge(consts_set, 6)
                pe.wait_ge(w_in, 16)
                for k in range(KD):
                    for o in range(KD):
                        last = nc.tensor.transpose(psW[:, k, o * P:(o + 1) * P], Wn[:, o, k * P:(k + 1) * P],
                                                   ident[:, :])
                last.then_inc(w_turned, 1)
                pe.wait_ge(counted, 1)
                nc.tensor.matmul(psC[:, 0:BUCKETS], tri[:, :], lane_count[:, :], start=True, stop=True)
                nc.tensor.matmul(psC[:, BUCKETS:2 * BUCKETS], ones[:, :], lane_count[:, :], start=True,
                                 stop=True).then_inc(summed, 1)
                pe.wait_ge(w_ready, 1)

                def step(t, s, first):
                    pe.wait_ge(xn_ready, t + 1)
                    if not first:
                        pe.wait_ge(xT_ready, t - 1)
                    for k in range(KD):
                        last = nc.tensor.transpose(psT[s][:, k, :], xn[:, s, k * P:(k + 1) * P], ident[:, :])
                    last.then_inc(x_turned, 1)
                    pe.wait_ge(xT_ready, t + 1)
                    if not first:
                        pe.wait_ge(xp_ready, t - 1)
                    for k in range(KD):
                        last = nc.tensor.matmul(psP[s], xT[:, s, k, :], WT[:, k, :], start=(k == 0),
                                                stop=(k == KD - 1))
                    last.then_inc(projected, 1)

                for s in range(2):
                    step(s, s, True)
                with pe.Fori(1, NT // 2) as i:
                    for s in range(2):
                        step(i * 2 + s, s, False)
                step(NT - 1, 0, False)


def gather_sum0(nc, sem, bank, c, dram):
    with ExitStack() as ctx, stage(nc, sem) as (sem, pool_sem):
        sb = lambda n, s, d: ctx.enter_context(nc.sbuf_tensor(n, s, d))
        X, iota, tid = c["X"], c["iota"], c["tid"]
        rec = sb("b_rec", [P, RING, GB, REC], I32)
        rec_f = rec[:, :, :, :].bitcast(F32)
        rows = sb("b_rows", [P, RING, GB, D], F32)
        spot = sb("b_spot", [P, RING, GB, P], F32)
        rec_in = [sem(f"b_rec_in{k}") for k in range(RING)]
        rows_in = [[pool_sem(f"b_rows_in{k}_{e}") for e in range(GB)] for k in range(RING)]
        spot_ready = sem("b_spot_ready")
        summed = sem("b_summed")
        added = sem("b_added")
        turn = sem("b_turn")
        ITER = NGROUP // RING

        with nc.Block() as block:

            @block.sync
            def _(sp):
                def body(i, first):
                    for k in range(RING):
                        if not first:
                            sp.wait_ge(summed, i * RING + (k + 1 - RING))
                        sp.dma_start(rec[:, k, :, :].rearrange("p e c -> p (e c)"),
                                     dram["sorted_edges"][bass.ds((i * RING + k) * GROUP, GROUP), :].rearrange(
                                         "(p e) c -> p (e c)", p=P)).then_inc(rec_in[k], 16)
                peeled(sp, ITER, body)

            @block.gpsimd
            def _(pool):
                with pool.Fori(0, ITER) as i:
                    for k in range(RING):
                        pool.wait_ge(rec_in[k], i * 16 + 16)
                        pool.sem_inc(turn, 1)
                        for e in range(GB):
                            nc.gpsimd.indirect_dma_start(
                                rows[:, k, e, :], None, dram["table0"][:, :],
                                bass.IndirectOffsetOnAxis(rec[:, k, e, 2:3], 0)).then_inc(rows_in[k][e], 16)

            @block.vector
            def _(dve):
                def build(i, k):
                    dve.wait_ge(rec_in[k], i * 16 + 16)
                    for e in range(GB):
                        last = nc.vector.tensor_scalar(spot[:, k, e, :], iota[:, :], rec_f[:, k, e, 0:1],
                                                       rec_f[:, k, e, 1:2], ALU.is_equal, ALU.mult)
                    last.then_inc(spot_ready, 1)

                def add(i, k, first):
                    dve.wait_ge(summed, i * RING + (k + 1))
                    if not (first and k == 0):
                        dve.wait_ge(added, i * RING + k)
                    dve.sem_inc(turn, 1)
                    t = dve.value_load(tid[0:1, bass.ds(i * RING + k, 1)], min_val=0, max_val=NT - 1)
                    nc.vector.tensor_tensor(X[:, bass.ds(t, 1), :].rearrange("p a d -> p (a d)"),
                                            X[:, bass.ds(t, 1), :].rearrange("p a d -> p (a d)"),
                                            bank[k][:, 0:D], ALU.add).then_inc(added, 1)

                def body(i, first):
                    build(i, 0)
                    for k in range(1, RING):
                        build(i, k)
                        add(i, k - 1, first)
                    add(i, RING - 1, first)
                peeled(dve, ITER, body)

            @block.tensor
            def _(pe):
                def body(i, first):
                    for k in range(RING):
                        pe.wait_ge(spot_ready, i * RING + (k + 1))
                        if not first:
                            pe.wait_ge(added, i * RING + (k + 1 - RING))
                        for e in range(GB):
                            pe.wait_ge(rows_in[k][e], i * 16 + 16)
                            last = nc.tensor.matmul(bank[k][:, 0:D], spot[:, k, e, :], rows[:, k, e, :],
                                                    start=(e == 0), stop=(e == GB - 1))
                        last.then_inc(summed, 1)
                peeled(pe, ITER, body)


def blocks_of(experts):
    n = (2 * NT * P + experts * (P - 1)) // P
    return n + n % 2


MOE = [
    {"E": 6, "widths": [D, 256, 256, D], "blocks": blocks_of(6), "softmax": True,
     "router_w1": "L0_ffn_router_w1", "router_b1": "L0_ffn_router_b1", "router_w2": "L0_ffn_router_w2",
     "router_b2": "L0_ffn_router_b2", "w": ["L0_ffn_expert_w1", "L0_ffn_expert_w2", "L0_ffn_expert_w3"],
     "b": ["L0_ffn_expert_b1", "L0_ffn_expert_b2"], "b_last": "L0_ffn_expert_b3"},
    {"E": 16, "widths": [D, 512, D], "blocks": blocks_of(16), "softmax": False,
     "router_w2": "L1_ffn_gate_w", "router_b2": "L1_ffn_gate_b", "w": ["L1_ffn_w1", "L1_ffn_w2"],
     "b": ["L1_ffn_b1"], "b_last": "L1_ffn_b2"},
]
BLOCKS_MAX = max(m["blocks"] for m in MOE)
LOT = 7
NLOT = NT // LOT
assert NLOT * LOT == NT


def before(s, ring):
    same = [q for q in range(LOT) if q % ring == s % ring]
    return s - ring if s >= ring else same[-1] - LOT


def norm_all(nc, dve, link, steps, turn, X, stats, moments, mr, var_ready, dev_ready):
    with dve.Fori(0, NLOT) as i:
        steps.enter(i, 3)
        for s in range(LOT):
            last = nc.vector.bn_stats(stats[:, s, :], X[:, i * LOT + s, :])
        link(last)
        dve.sem_inc(turn, 1)
        for s in range(LOT):
            last = nc.vector.bn_aggr(moments[:, s, :], stats[:, s, :])
        link(last)
        dve.sem_inc(turn, 1)
        link(nc.vector.tensor_copy(mr[:, bass.ds(i * LOT, LOT), :], moments[:, :, :]))
        dve.sem_inc(turn, 1)
    steps.leave(NLOT)
    nc.vector.tensor_scalar(mr[:, :, 1], mr[:, :, 1], EPS, None, ALU.add).then_inc(var_ready, 1)
    dve.wait_ge(dev_ready, 1)
    link(nc.vector.reciprocal(mr[:, :, 1], mr[:, :, 1]))


def route(nc, sem, bank, c, a, dram, layer, m):
    E = m["E"]
    L = layer
    hidden = "router_w1" in m
    with ExitStack() as ctx, stage(nc, sem) as (sem, pool_sem):
        sb = lambda n, s, d: ctx.enter_context(nc.sbuf_tensor(f"r{L}_{n}", s, d))
        X, ident, tri, ones = c["X"], c["ident"], c["tri"], c["ones"]
        gates, gates_by, pos, eid = m["gates"], m["gates_by"], m["pos"], m["eid"]
        stats = sb("stats", [P, LOT, 6], F32)
        moments = sb("moments", [P, LOT, 2], F32)
        mr = sb("mr", [P, NT, 2], F32)
        xn = sb("xn", [P, LOT, D], F32)
        xT = sb("xT", [P, LOT, KD, P], F32)
        w1 = sb("w1", [P, KD, P], F32)
        b1 = sb("b1", [P, 1], F32)
        w2 = sb("w2", [P, KD, E], F32)
        b2 = sb("b2", [P, E], F32)
        rh = sb("rh", [P, LOT, P], F32)
        logits = sb("logits", [P, NT, E], F32)
        tmp = sb("tmp", [P, NT, E], F32)
        hot = [sb(f"hot{k}", [P, NT, E], F32) for k in range(2)]
        eno = sb("eno", [P, NT, E], F32)
        top = sb("top", [P, 4, NT], F32)
        member = sb("member", [P, E, 2 * NT], F32)
        ranks = sb("ranks", [P, E, 2 * NT], F32)
        carry_mask = sb("carry_mask", [P, E, 2 * NT], F32)
        run = sb("run", [P, 6, E], F32)
        blocks_i = sb("blocks_i", [P, 2, E], I32)
        block_no = sb("block_no", [P, 1], F32)
        past = sb("past", [P, E], F32)
        eid_f = sb("eid_f", [P, 1], F32)
        eid_i = sb("eid_i", [P, 1], I32)

        consts_set = sem(f"r{L}_consts_set")
        w_in = sem(f"r{L}_w_in")
        var_ready = sem(f"r{L}_var_ready")
        dev_ready = sem(f"r{L}_dev_ready")
        dve_done = sem(f"r{L}_dve_done")
        turn = sem(f"r{L}_turn")
        xn_ready = sem(f"r{L}_xn_ready")
        xn_out = [sem(f"r{L}_xn_out{s}") for s in range(LOT)]
        x_turned = sem(f"r{L}_x_turned")
        xT_ready = sem(f"r{L}_xT_ready")
        h_summed = sem(f"r{L}_h_summed")
        rh_ready = sem(f"r{L}_rh_ready")
        l_summed = sem(f"r{L}_l_summed")
        l_ready = sem(f"r{L}_l_ready")
        exp_asked = sem(f"r{L}_exp_asked")
        exp_ready = sem(f"r{L}_exp_ready")
        counted = sem(f"r{L}_counted")
        summed = sem(f"r{L}_summed")
        eid_ready = sem(f"r{L}_eid_ready")
        eid_out = sem(f"r{L}_eid_out")
        eid_in = sem(f"r{L}_eid_in")

        RT, RH = 3, 2
        psT = [bank[r][:, 0:D].rearrange("p (k n) -> p k n", k=KD) for r in range(RT)]
        psH = [bank[3 + r][:, 0:P] for r in range(RH)]
        psL = [bank[5 + r][:, 0:E] for r in range(RH)]
        psC = bank[7]
        NW = 4 if hidden else 2

        with nc.Block() as block:

            @block.sync
            def _(sp):
                if hidden:
                    sp.dma_start(w1[:, :, :], a[m["router_w1"]].rearrange("(k p) h -> p k h", p=P)).then_inc(w_in, 16)
                    with nc.allow_non_contiguous_dma(reason="a bias of 128 features, one on each partition"):
                        sp.dma_start(b1[:, :], a[m["router_b1"]].rearrange("(p o) -> p o", o=1)).then_inc(w_in, 16)
                    sp.dma_start(w2[:, 0, :], a[m["router_w2"]]).then_inc(w_in, 16)
                else:
                    sp.dma_start(w2[:, :, :], a[m["router_w2"]].rearrange("(k p) e -> p k e", p=P)).then_inc(w_in, 16)
                sp.dma_start(b2[:, :], a[m["router_b2"]].rearrange("(o e) -> o e", o=1).to_broadcast([P, E])
                             ).then_inc(w_in, 16)
                with sp.Fori(0, NLOT) as i:
                    for s in range(LOT):
                        sp.wait_ge(xn_ready, i * LOT + (s + 1))
                        sp.dma_start(tile_rows(dram["xn"], i * LOT + s), xn[:, s, :]).then_inc(xn_out[s], 16)
                sp.wait_ge(eid_ready, 1)
                sp.dma_start(dram["eid"].rearrange("(p o) -> p o", o=1), eid_i[:, :]).then_inc(eid_out, 16)
                sp.wait_ge(eid_out, 16)
                sp.dma_start(eid[0:1, :], dram["eid"].rearrange("(o g) -> o g", o=1)).then_inc(eid_in, 16)
                sp.wait_ge(eid_in, 16)
                for s in range(LOT):
                    sp.wait_ge(xn_out[s], 16 * NLOT)

            @block.gpsimd
            def _(pool):
                nc.gpsimd.iota(eno[:, :, :], pattern=[[0, NT], [1, E]], base=-1000, channel_multiplier=0,
                               allow_small_or_imprecise_dtypes=True).then_inc(consts_set, 1)
                nc.gpsimd.iota(block_no[:, :], pattern=[[0, 1]], base=0, channel_multiplier=1,
                               allow_small_or_imprecise_dtypes=True).then_inc(consts_set, 1)

            @block.vector
            def _(dve):
                steps = Count()

                def link(ins):
                    ins.then_inc(dve_done, 1)
                    dve.wait_ge(dve_done, steps.next())

                norm_all(nc, dve, link, steps, turn, X, stats, moments, mr, var_ready, dev_ready)

                def norm(i, s, first):
                    if not first:
                        dve.wait_ge(xn_out[s], i * 16)
                        dve.wait_ge(x_turned, i * LOT + (s + 1 - LOT))
                        dve.sem_inc(turn, 1)
                    nc.vector.tensor_scalar(xn[:, s, :], X[:, i * LOT + s, :], mr[:, bass.ds(i * LOT + s, 1), 0],
                                            mr[:, bass.ds(i * LOT + s, 1), 1], ALU.subtract,
                                            ALU.mult).then_inc(xn_ready, 1)

                def logit(i, s):
                    dve.wait_ge(l_summed, i * LOT + (s + 1))
                    dve.sem_inc(turn, 1)
                    nc.vector.tensor_tensor(logits[:, bass.ds(i * LOT + s, 1), :].rearrange("p a e -> p (a e)"),
                                            psL[s % RH], b2[:, :], ALU.add).then_inc(l_ready, 1)

                dve.wait_ge(w_in, 16 * NW)

                def body(i, first):
                    for s in range(LOT + 2):
                        if s < LOT:
                            norm(i, s, first)
                        if s >= 2:
                            logit(i, s - 2)
                peeled(dve, NLOT, body)
                dve.wait_ge(l_ready, NT)
                dve.wait_ge(consts_set, 2)
                v = logits
                if m["softmax"]:
                    link(nc.vector.tensor_reduce(top[:, 0, :], logits[:, :, :], AX.X, ALU.max))
                    nc.vector.tensor_tensor(tmp[:, :, :], logits[:, :, :], widen(top[:, 0, :], E),
                                            ALU.subtract).then_inc(exp_asked, 1)
                    dve.wait_ge(exp_ready, 1)
                    link(nc.vector.tensor_reduce(top[:, 0, :], tmp[:, :, :], AX.X, ALU.add))
                    link(nc.vector.reciprocal(top[:, 1, :], top[:, 0, :]))
                    link(nc.vector.tensor_tensor(logits[:, :, :], tmp[:, :, :], widen(top[:, 1, :], E), ALU.mult))
                for k in range(2):
                    link(nc.vector.tensor_reduce(top[:, k, :], v[:, :, :], AX.X, ALU.max))
                    link(nc.vector.tensor_tensor(tmp[:, :, :], v[:, :, :], widen(top[:, k, :], E), ALU.is_equal))
                    link(nc.vector.tensor_tensor(tmp[:, :, :], tmp[:, :, :], eno[:, :, :], ALU.mult))
                    link(nc.vector.tensor_reduce(top[:, 2, :], tmp[:, :, :], AX.X, ALU.min))
                    link(nc.vector.tensor_tensor(hot[k][:, :, :], eno[:, :, :], widen(top[:, 2, :], E), ALU.is_equal))
                    if k == 0:
                        link(nc.vector.scalar_tensor_tensor(v[:, :, :], hot[0][:, :, :], -3.0e38, v[:, :, :],
                                                            ALU.mult, ALU.add))
                nc.vector.tensor_tensor(top[:, 2, :], top[:, 1, :], top[:, 0, :], ALU.subtract).then_inc(exp_asked, 1)
                dve.wait_ge(exp_ready, 2 if m["softmax"] else 1)
                link(nc.vector.tensor_scalar(top[:, 3, :], top[:, 2, :], 1.0, None, ALU.add))
                link(nc.vector.reciprocal(gates[:, 0, :], top[:, 3, :]))
                link(nc.vector.tensor_tensor(gates[:, 1, :], gates[:, 0, :], top[:, 2, :], ALU.mult))
                link(nc.vector.tensor_tensor(tmp[:, :, :], hot[0][:, :, :], widen(gates[:, 0, :], E), ALU.mult))
                link(nc.vector.tensor_tensor(gates_by[:, :, :], hot[1][:, :, :], widen(gates[:, 1, :], E), ALU.mult))
                link(nc.vector.tensor_tensor(gates_by[:, :, :], gates_by[:, :, :], tmp[:, :, :], ALU.add))
                for k in range(2):
                    link(nc.vector.tensor_copy(member[:, :, k * NT:(k + 1) * NT],
                                               hot[k][:, :, :].rearrange("p t e -> p e t")))
                link(nc.vector.tensor_reduce(run[:, 0, :], member[:, :, :], AX.X, ALU.add))
                dve.sem_inc(counted, 1)
                link(nc.vector.memset(carry_mask[:, :, :], 1.0))
                link(nc.vector.memset(carry_mask[:, :, 0], 0.0))
                dve.wait_ge(summed, 1)
                link(nc.vector.tensor_scalar(blocks_i[:, 0, :], psC[:, E:2 * E], float(P - 1), None, ALU.add))
                link(nc.vector.tensor_scalar(blocks_i[:, 1, :], blocks_i[:, 0, :], 7, None, ALU.arith_shift_right))
                link(nc.vector.tensor_copy(run[:, 1, :], blocks_i[:, 1, :]))
                link(nc.vector.tensor_tensor_scan(run[:, 2, :], ones[:, 0:E], run[:, 1, :], 0.0, ALU.mult, ALU.add))
                link(nc.vector.tensor_tensor(run[:, 3, :], run[:, 2, :], run[:, 1, :], ALU.subtract))
                link(nc.vector.scalar_tensor_tensor(run[:, 4, :], run[:, 3, :], float(P), psC[:, 0:E], ALU.mult, ALU.add))
                link(nc.vector.tensor_scalar(past[:, :], run[:, 2, :], block_no[:, :], None, ALU.is_le))
                link(nc.vector.tensor_reduce(eid_f[:, :], past[:, :], AX.X, ALU.add))
                nc.vector.tensor_scalar(eid_i[:, :], eid_f[:, :], float(E - 1), None, ALU.min).then_inc(eid_ready, 1)
                link(nc.vector.tensor_copy(run[:, 5, :], member[:, :, 0]))
                link(nc.vector.tensor_tensor(member[:, :, 0], member[:, :, 0], run[:, 4, :], ALU.add))
                link(nc.vector.tensor_tensor_scan(ranks[:, :, :].rearrange("p e t -> p (e t)"),
                                                  carry_mask[:, :, :].rearrange("p e t -> p (e t)"),
                                                  member[:, :, :].rearrange("p e t -> p (e t)"), 0.0,
                                                  ALU.mult, ALU.add))
                link(nc.vector.tensor_copy(member[:, :, 0], run[:, 5, :]))
                link(nc.vector.tensor_tensor(member[:, :, :], member[:, :, :], ranks[:, :, :], ALU.mult))
                link(nc.vector.tensor_reduce(ranks[:, 0, :], member[:, :, :].rearrange("p e t -> p t e"), AX.X, ALU.add))
                link(nc.vector.tensor_scalar(pos[:, :], ranks[:, 0, :], -1.0, None, ALU.add))

            @block.scalar
            def _(act):
                act.wait_ge(var_ready, 1)
                nc.scalar.activation(mr[:, :, 1], mr[:, :, 1], ACT.Sqrt).then_inc(dev_ready, 1)
                if hidden:
                    act.wait_ge(w_in, 16 * NW)

                def turned(i, s, first):
                    act.wait_ge(x_turned, i * LOT + (s + 1))
                    if not first:
                        act.wait_ge(h_summed if hidden else l_summed, i * LOT + (s + 1 - LOT))
                    nc.scalar.activation(xT[:, s, :, :], psT[s % RT], ACT.Copy).then_inc(xT_ready, 1)

                def relu(i, s, first):
                    act.wait_ge(h_summed, i * LOT + (s + 1))
                    if not first:
                        act.wait_ge(l_summed, i * LOT + (s + 1 - LOT))
                    nc.scalar.activation(rh[:, s, :], psH[s % RH], ACT.Relu, bias=b1[:, 0:1]).then_inc(rh_ready, 1)

                def body(i, first):
                    for s in range(LOT + 1):
                        if s < LOT:
                            turned(i, s, first)
                        if s >= 1 and hidden:
                            relu(i, s - 1, first)
                peeled(act, NLOT, body)
                for n in range(2 if m["softmax"] else 1):
                    act.wait_ge(exp_asked, n + 1)
                    t = tmp[:, :, :] if n == 0 and m["softmax"] else top[:, 2, :]
                    nc.scalar.activation(t, t, ACT.Exp).then_inc(exp_ready, 1)

            @block.tensor
            def _(pe):
                pe.wait_ge(w_in, 16 * NW)

                def wait_past(sm, i, s, ring, first):
                    q = before(s, ring)
                    if q >= 0 or not first:
                        pe.wait_ge(sm, i * LOT + (q + 1))

                def turn_x(i, s, first):
                    pe.wait_ge(xn_ready, i * LOT + (s + 1))
                    wait_past(xT_ready, i, s, RT, first)
                    for k in range(KD):
                        last = nc.tensor.transpose(psT[s % RT][:, k, :], xn[:, s, k * P:(k + 1) * P], ident[:, :])
                    last.then_inc(x_turned, 1)

                def sum_h(i, s, first):
                    pe.wait_ge(xT_ready, i * LOT + (s + 1))
                    wait_past(rh_ready, i, s, RH, first)
                    for k in range(KD):
                        last = nc.tensor.matmul(psH[s % RH], w1[:, k, :], xT[:, s, k, :], start=(k == 0),
                                                stop=(k == KD - 1))
                    last.then_inc(h_summed, 1)

                def sum_l(i, s, first):
                    pe.wait_ge(rh_ready if hidden else xT_ready, i * LOT + (s + 1))
                    wait_past(l_ready, i, s, RH, first)
                    if hidden:
                        nc.tensor.matmul(psL[s % RH], rh[:, s, :], w2[:, 0, :], start=True,
                                         stop=True).then_inc(l_summed, 1)
                    else:
                        for k in range(KD):
                            last = nc.tensor.matmul(psL[s % RH], xT[:, s, k, :], w2[:, k, :], start=(k == 0),
                                                    stop=(k == KD - 1))
                        last.then_inc(l_summed, 1)

                def body(i, first):
                    for s in range(LOT + 2):
                        if s < LOT:
                            turn_x(i, s, first)
                        if 1 <= s <= LOT and hidden:
                            sum_h(i, s - 1, first)
                        if s >= 2:
                            sum_l(i, s - 2, first)
                peeled(pe, NLOT, body)
                pe.wait_ge(counted, 1)
                nc.tensor.matmul(psC[:, 0:E], tri[:, :], run[:, 0, :], start=True, stop=True)
                nc.tensor.matmul(psC[:, E:2 * E], ones[:, :], run[:, 0, :], start=True,
                                 stop=True).then_inc(summed, 1)


def experts(nc, sem, bank, c, a, dram, layer, m):
    E, widths = m["E"], m["widths"]
    NL = len(widths) - 1
    L = layer
    BLOCKS = m["blocks"]
    with ExitStack() as ctx, stage(nc, sem) as (sem, pool_sem):
        sb = lambda n, s, d: ctx.enter_context(nc.sbuf_tensor(f"e{L}_{n}", s, d))
        ident, pos, eid = c["ident"], m["pos"], m["eid"]
        W = [sb(f"W{n}", [P, E, widths[n] // P, widths[n + 1]], F32) for n in range(NL)]
        B = [sb(f"B{n}", [P, E, widths[n + 1] // P], F32) for n in range(NL - 1)]
        NB = [E * widths[n + 1] // P for n in range(NL - 1)]
        brow = [sb(f"brow{n}", [NB[n], P], F32) for n in range(NL - 1)]
        xr = sb("xr", [P, LOT, D], F32)
        pos_ring = sb("pos_ring", [P, LOT, 2], I32)
        xb = sb("xb", [P, 2, D], F32)
        widest = max(widths)
        hT = sb("hT", [P, 2, widest // P, P], F32)
        z = sb("z", [P, 2, max(widths[1:-1])], F32)
        y = sb("y", [P, 2, D], F32)

        w_in = [sem(f"e{L}_w_in{n}") for n in range(NL)]
        b_in = sem(f"e{L}_b_in")
        b_turned = sem(f"e{L}_b_turned")
        b_ready = sem(f"e{L}_b_ready")
        xr_in = [sem(f"e{L}_xr_in{s}") for s in range(LOT)]
        pos_ready = sem(f"e{L}_pos_ready")
        sent = [pool_sem(f"e{L}_sent{s}") for s in range(LOT)]
        all_sent = sem(f"e{L}_all_sent")
        xb_in = [sem(f"e{L}_xb_in{s}") for s in range(2)]
        turned = sem(f"e{L}_turned")
        hT_ready = sem(f"e{L}_hT_ready")
        summed = sem(f"e{L}_summed")
        z_ready = sem(f"e{L}_z_ready")
        y_out = [sem(f"e{L}_y_out{s}") for s in range(2)]
        turn = sem(f"e{L}_turn")
        psT = [bank[s] for s in range(2)]
        psZ = [bank[2 + s] for s in range(2)]
        psB = [bank[4 + n] for n in range(2)]
        ITER = BLOCKS // 2
        assert ITER * 2 == BLOCKS

        with nc.Block() as block:

            @block.sync
            def _(sp):
                for n in range(NL - 1):
                    sp.dma_start(brow[n][:, :], a[m["b"][n]].rearrange("e (k p) -> (e k) p", p=P)).then_inc(b_in, 16)
                with sp.Fori(0, NLOT) as i:
                    for s in range(LOT):
                        sp.wait_ge(pos_ready, i * LOT + (s + 1))
                        sp.dma_start(xr[:, s, :], tile_rows(dram["xn"], i * LOT + s)).then_inc(xr_in[s], 16)
                sp.wait_ge(all_sent, 1)

                def load(b, s):
                    sp.dma_start(xb[:, s, :], tile_rows(dram["sent"], b)).then_inc(xb_in[s], 16)

                def store(i, s):
                    sp.wait_ge(z_ready, i * (2 * NL) + (2 * (NL - 1) + s + 1))
                    sp.dma_start(tile_rows(dram["made"], i * 2 + s), y[:, s, :]).then_inc(y_out[s], 16)

                for s in range(2):
                    load(s, s)
                with sp.Fori(0, ITER - 1) as i:
                    for s in range(2):
                        sp.wait_ge(turned, i * (2 * NL) + (s + 1))
                        load(i * 2 + (2 + s), s)
                    for s in range(2):
                        store(i, s)
                for s in range(2):
                    store(ITER - 1, s)
                for s in range(2):
                    sp.wait_ge(y_out[s], 16 * ITER)

            @block.gpsimd
            def _(pool):
                with pool.Fori(0, NLOT) as i:
                    for s in range(LOT):
                        pool.wait_ge(xr_in[s], i * 16 + 16)
                        pool.sem_inc(turn, 1)
                        for k in range(2):
                            nc.gpsimd.indirect_dma_start(
                                dram["sent"][:, :], bass.IndirectOffsetOnAxis(pos_ring[:, s, k:k + 1], 0),
                                xr[:, s, :], None).then_inc(sent[s], 16)
                for s in range(LOT):
                    pool.wait_ge(sent[s], 32 * NLOT)
                pool.sem_inc(all_sent, 1)

            @block.vector
            def _(dve):
                pos_by_tile = pos[:, :].rearrange("p (k t) -> p t k", k=2)

                def places(i, first):
                    for s in range(LOT):
                        if not first:
                            dve.wait_ge(sent[s], i * 32)
                            dve.sem_inc(turn, 1)
                        nc.vector.tensor_copy(pos_ring[:, s, :], pos_by_tile[:, bass.ds(i * LOT + s, 1), :].rearrange(
                            "p a k -> p (a k)")).then_inc(pos_ready, 1)
                peeled(dve, NLOT, places)

                def body(i, first):
                    for n in range(NL):
                        for s in range(2):
                            dve.wait_ge(summed, i * (2 * NL) + (2 * n + s + 1))
                            if n == NL - 1 and not first:
                                dve.wait_ge(y_out[s], i * 16)
                            out = y[:, s, :] if n == NL - 1 else z[:, s, 0:widths[n + 1]]
                            nc.vector.tensor_copy(out, psZ[s][:, 0:widths[n + 1]]).then_inc(z_ready, 1)
                peeled(dve, ITER, body)

            @block.scalar
            def _(act):
                for n in range(NL):
                    act.dma_start(W[n][:, :, :, :], a[m["w"][n]].rearrange("e (k p) f -> p e k f", p=P)
                                  ).then_inc(w_in[n], 16)
                for n in range(NL - 1):
                    act.wait_ge(b_turned, n + 1)
                    nc.scalar.activation(B[n][:, :, :].rearrange("p e k -> p (e k)"), psB[n][:, 0:NB[n]],
                                         ACT.Copy).then_inc(b_ready, 1)
                act.wait_ge(b_ready, NL - 1)

                def body(i, first):
                    es = [act.value_load(eid[0:1, bass.ds(i * 2 + s, 1)], min_val=0, max_val=E - 1) for s in range(2)]
                    for n in range(NL):
                        for s in range(2):
                            act.wait_ge(turned, i * (2 * NL) + (2 * n + s + 1))
                            if n == 0:
                                if not first:
                                    act.wait_ge(summed, i * (2 * NL) + (s + 1 - 2))
                                nc.scalar.activation(hT[:, s, 0:KD, :], psT[s][:, 0:D].rearrange(
                                    "p (k n) -> p k n", k=KD), ACT.Copy).then_inc(hT_ready, 1)
                            else:
                                act.sem_inc(turn, 1)
                                for k in range(widths[n] // P):
                                    last = nc.scalar.activation(
                                        hT[:, s, k, :], psT[s][:, k * P:(k + 1) * P], ACT.Relu,
                                        bias=B[n - 1][:, bass.ds(es[s], 1), k])
                                last.then_inc(hT_ready, 1)
                peeled(act, ITER, body)

            @block.tensor
            def _(pe):
                pe.wait_ge(b_in, 16 * (NL - 1))
                for n in range(NL - 1):
                    nc.tensor.transpose(psB[n][:, 0:NB[n]], brow[n][:, :],
                                        ident[0:NB[n], 0:NB[n]]).then_inc(b_turned, 1)
                for n in range(NL):
                    pe.wait_ge(w_in[n], 16)

                def body(i, first):
                    es = [pe.value_load(eid[0:1, bass.ds(i * 2 + s, 1)], min_val=0, max_val=E - 1) for s in range(2)]
                    for n in range(NL):
                        for s in range(2):
                            if n == 0:
                                pe.wait_ge(xb_in[s], i * 16 + 16)
                            else:
                                pe.wait_ge(z_ready, i * (2 * NL) + (2 * (n - 1) + s + 1))
                            src = xb[:, s, :] if n == 0 else z[:, s, :]
                            for k in range(widths[n] // P):
                                last = nc.tensor.transpose(psT[s][:, k * P:(k + 1) * P], src[:, k * P:(k + 1) * P],
                                                           ident[:, :])
                            last.then_inc(turned, 1)
                        for s in range(2):
                            pe.wait_ge(hT_ready, i * (2 * NL) + (2 * n + s + 1))
                            if n == 0 and not first:
                                pe.wait_ge(z_ready, i * (2 * NL) + (s + 1 - 2))
                            K = widths[n] // P
                            for k in range(K):
                                last = nc.tensor.matmul(psZ[s][:, 0:widths[n + 1]], hT[:, s, k, :],
                                                        W[n][:, bass.ds(es[s], 1), k, :].rearrange("p a f -> p (a f)"),
                                                        start=(k == 0), stop=(k == K - 1))
                            last.then_inc(summed, 1)
                peeled(pe, ITER, body)


def combine(nc, sem, bank, c, a, dram, layer, m, out=None):
    E = m["E"]
    L = layer
    final = out is not None
    with ExitStack() as ctx, stage(nc, sem) as (sem, pool_sem):
        sb = lambda n, s, d: ctx.enter_context(nc.sbuf_tensor(f"c{L}_{n}", s, d))
        X, ident = c["X"], c["ident"]
        gates, gates_by, pos = m["gates"], m["gates_by"], m["pos"]
        pos_ring = sb("pos_ring", [P, LOT, 2], I32)
        yr = sb("yr", [P, LOT, 2, D], F32)
        bl = sb("bl", [E, D], F32)
        gT = sb("gT", [E, LOT, P], F32)
        gs = sb("gs", [P, LOT, E], F32)
        if final:
            y = sb("y", [P, LOT, D], F32)
            gamma = sb("gamma", [P, D], F32)
            beta = sb("beta", [P, D], F32)
            stats = sb("stats", [P, LOT, 6], F32)
            moments = sb("moments", [P, LOT, 2], F32)
            rstd = sb("rstd", [P, LOT], F32)
        w_in = sem(f"c{L}_w_in")
        xn_in = sem(f"c{L}_xn_in")
        pos_ready = sem(f"c{L}_pos_ready")
        rows_in = [pool_sem(f"c{L}_rows_in{s}") for s in range(LOT)]
        gs_ready = sem(f"c{L}_gs_ready")
        turned = sem(f"c{L}_turned")
        gT_ready = sem(f"c{L}_gT_ready")
        summed = sem(f"c{L}_summed")
        added = sem(f"c{L}_added")
        var_ready = sem(f"c{L}_var_ready")
        dev_ready = sem(f"c{L}_dev_ready")
        dve_done = sem(f"c{L}_dve_done")
        lot_done = sem(f"c{L}_lot_done")
        stored = sem(f"c{L}_stored")
        turn = sem(f"c{L}_turn")
        psG = [bank[r] for r in range(2)]
        psB = [bank[2 + r][:, 0:D] for r in range(2)]

        with nc.Block() as block:

            @block.sync
            def _(sp):
                sp.dma_start(bl[:, :], a[m["b_last"]]).then_inc(w_in, 16)
                if final:
                    for t, name in ((gamma, "L1_ffn_gamma"), (beta, "L1_ffn_beta")):
                        sp.dma_start(t[:, :], a[name].rearrange("(o d) -> o d", o=1).to_broadcast([P, D])
                                     ).then_inc(w_in, 16)

                    def body(i, first):
                        if not first:
                            sp.wait_ge(lot_done, i * 1)
                        sp.dma_start(y[:, :, :], dram["xn"][bass.ds(i * (LOT * P), LOT * P), :].rearrange(
                            "(t p) d -> p t d", p=P)).then_inc(xn_in, 16)
                        if not first:
                            sp.dma_start(out[bass.ds((i - 1) * (LOT * P), LOT * P), :].rearrange(
                                "(t p) d -> p t d", p=P), X[:, bass.ds((i - 1) * LOT, LOT), :]).then_inc(stored, 16)
                    peeled(sp, NLOT, body)
                    sp.wait_ge(lot_done, NLOT)
                    start = (NT - LOT) * P
                    full = (NT - 1) * P
                    sp.dma_start(out[start:full, :].rearrange("(t p) d -> p t d", p=P),
                                 X[:, NT - LOT:NT - 1, :]).then_inc(stored, 16)
                    sp.dma_start(out[full:N, :], X[0:LAST, NT - 1, :]).then_inc(stored, 16)
                    sp.wait_ge(stored, 16 * (NLOT + 1))

            @block.gpsimd
            def _(pool):
                with pool.Fori(0, NLOT) as i:
                    for s in range(LOT):
                        pool.wait_ge(pos_ready, i * LOT + (s + 1))
                        pool.sem_inc(turn, 1)
                        for k in range(2):
                            nc.gpsimd.indirect_dma_start(
                                yr[:, s, k, :], None, dram["made"][:, :],
                                bass.IndirectOffsetOnAxis(pos_ring[:, s, k:k + 1], 0)).then_inc(rows_in[s], 16)

            @block.vector
            def _(dve):
                steps = Count()
                pos_by_tile = pos[:, :].rearrange("p (k t) -> p t k", k=2)

                def link(ins):
                    ins.then_inc(dve_done, 1)
                    dve.wait_ge(dve_done, steps.next())

                def place(t, s):
                    nc.vector.tensor_copy(pos_ring[:, s, :], pos_by_tile[:, bass.ds(t, 1), :].rearrange(
                        "p a k -> p (a k)")).then_inc(pos_ready, 1)

                for s in range(LOT):
                    place(s, s)
                if final:
                    dve.wait_ge(w_in, 48)

                def body(i, first, last_turn):
                    if final:
                        dve.wait_ge(xn_in, i * 16 + 16)
                    for s in range(LOT):
                        t = i * LOT + s
                        x = y[:, s, :] if final else X[:, bass.ds(t, 1), :].rearrange("p a d -> p (a d)")
                        dve.wait_ge(rows_in[s], i * 32 + 32)
                        dve.sem_inc(turn, 1)
                        for k in range(2):
                            link(nc.vector.scalar_tensor_tensor(x, yr[:, s, k, :], gates[:, k, bass.ds(t, 1)], x,
                                                                ALU.mult, ALU.add))
                            dve.sem_inc(turn, 1)
                        if not last_turn:
                            place(t + LOT, s)
                        dve.wait_ge(summed, t + 1)
                        nc.vector.tensor_tensor(x, psB[s % 2], x, ALU.add).then_inc(added, 1)
                    if final:
                        dve.wait_ge(added, i * LOT + LOT)
                        for s in range(LOT):
                            ins = nc.vector.bn_stats(stats[:, s, :], y[:, s, :])
                        link(ins)
                        dve.sem_inc(turn, 1)
                        for s in range(LOT):
                            ins = nc.vector.bn_aggr(moments[:, s, :], stats[:, s, :])
                        link(ins)
                        nc.vector.tensor_scalar(rstd[:, :], moments[:, :, 1], EPS, None,
                                                ALU.add).then_inc(var_ready, 1)
                        dve.wait_ge(dev_ready, i * 1 + 1)
                        link(nc.vector.reciprocal(rstd[:, :], rstd[:, :]))
                        for s in range(LOT):
                            ins = nc.vector.tensor_scalar(y[:, s, :], y[:, s, :], moments[:, s, 0:1],
                                                          rstd[:, s:s + 1], ALU.subtract, ALU.mult)
                        link(ins)
                        link(nc.vector.tensor_tensor(y[:, :, :], y[:, :, :], spread(gamma[:, :], LOT), ALU.mult))
                        link(nc.vector.tensor_tensor(y[:, :, :], y[:, :, :], spread(beta[:, :], LOT), ALU.add))
                        dve.sem_inc(turn, 1)
                        xs = X[:, bass.ds(i * LOT, LOT), :]
                        nc.vector.tensor_tensor(xs, y[:, :, :], xs, ALU.add).then_inc(lot_done, 1)

                PER = 2 * LOT + (6 if final else 0)
                steps.enter(0, PER)
                body(0, True, False)
                steps.leave(1)
                with dve.Fori(1, NLOT - 1) as i:
                    steps.enter(i, PER, 1)
                    body(i, False, False)
                steps.leave(NLOT - 2)
                body(NLOT - 1, False, True)

            @block.scalar
            def _(act):
                def body(i, first):
                    nc.scalar.activation(gs[:, :, :], gates_by[:, bass.ds(i * LOT, LOT), :],
                                         ACT.Copy).then_inc(gs_ready, 1)
                    for s in range(LOT):
                        act.wait_ge(turned, i * LOT + (s + 1))
                        if not first:
                            act.wait_ge(summed, i * LOT + (s + 1 - LOT))
                        nc.scalar.activation(gT[:, s, :], psG[s % 2][0:E, 0:P], ACT.Copy).then_inc(gT_ready, 1)
                    if final:
                        act.wait_ge(var_ready, i * 1 + 1)
                        nc.scalar.activation(rstd[:, :], rstd[:, :], ACT.Sqrt).then_inc(dev_ready, 1)
                peeled(act, NLOT, body)

            @block.tensor
            def _(pe):
                pe.wait_ge(w_in, 48 if final else 16)

                def body(i, first):
                    pe.wait_ge(gs_ready, i * 1 + 1)
                    for s in range(LOT):
                        q = before(s, 2)
                        if q >= 0 or not first:
                            pe.wait_ge(gT_ready, i * LOT + (q + 1))
                        nc.tensor.transpose(psG[s % 2][0:E, 0:P], gs[:, s, :], ident[:, :]).then_inc(turned, 1)
                        pe.wait_ge(gT_ready, i * LOT + (s + 1))
                        if q >= 0 or not first:
                            pe.wait_ge(added, i * LOT + (q + 1))
                        nc.tensor.matmul(psB[s % 2], gT[:, s, :], bl[:, :], start=True, stop=True).then_inc(summed, 1)
                peeled(pe, NLOT, body)


def project_heads(nc, sem, bank, c, a, dram):
    with ExitStack() as ctx, stage(nc, sem) as (sem, pool_sem):
        sb = lambda n, s, d: ctx.enter_context(nc.sbuf_tensor(f"h_{n}", s, d))
        X, ident, ones = c["X"], c["ident"], c["ones"]
        W = sb("W", [HD, 2, D], F32)
        arow = sb("arow", [4, HD], F32)
        aT = sb("aT", [HD, 4], F32)
        brow = sb("brow", [2, HD], F32)
        bT = sb("bT", [HD, 2], F32)
        WIDE = ROW1 + 2
        WX = sb("WX", [P, KD, WIDE], F32)
        bias = sb("bias", [1, WIDE], F32)
        stats = sb("stats", [P, LOT, 6], F32)
        moments = sb("moments", [P, LOT, 2], F32)
        mr = sb("mr", [P, NT, 2], F32)
        xn = sb("xn", [P, LOT, D], F32)
        xT = sb("xT", [P, LOT, KD, P], F32)
        row = sb("row", [P, LOT, ROW1], F32)
        ss = sb("ss", [2, LOT, P], F32)
        w_in = sem("h_w_in")
        b_set = sem("h_b_set")
        a_turned = sem("h_a_turned")
        b_turned = sem("h_b_turned")
        w_turned = sem("h_w_turned")
        a_ready = sem("h_a_ready")
        ab_summed = sem("h_ab_summed")
        w_ready = sem("h_w_ready")
        dve_done = sem("h_dve_done")
        turn = sem("h_turn")
        var_ready = sem("h_var_ready")
        dev_ready = sem("h_dev_ready")
        xn_ready = sem("h_xn_ready")
        x_turned = sem("h_x_turned")
        xT_ready = sem("h_xT_ready")
        summed = sem("h_summed")
        row_ready = sem("h_row_ready")
        s_summed = sem("h_s_summed")
        ss_ready = sem("h_ss_ready")
        row_out = [sem(f"h_row_out{s}") for s in range(LOT)]
        psT = [bank[r][:, 0:D].rearrange("p (k n) -> p k n", k=KD) for r in range(3)]
        psR = [bank[3 + r][:, 0:WIDE] for r in range(2)]
        psS = [bank[5 + r][0:2, 0:P] for r in range(2)]
        psX = bank[7]

        with nc.Block() as block:

            @block.sync
            def _(sp):
                sp.dma_start(W[:, :, :], a["L1_gnn_W"].rearrange("h d f -> d h f")).then_inc(w_in, 16)
                sp.dma_start(arow[:, :], a["L1_gnn_a"].rearrange("h (s d) -> (h s) d", s=2)).then_inc(w_in, 16)
                sp.dma_start(brow[:, :], a["L1_gnn_b"]).then_inc(w_in, 16)
                sp.wait_ge(b_set, 1)
                for h in range(2):
                    sp.dma_start(bias[0:1, h * HW:h * HW + HD], a["L1_gnn_b"][h:h + 1, :]).then_inc(w_in, 16)

                def body(i, first):
                    for s in range(LOT):
                        sp.wait_ge(row_ready, i * LOT + (s + 1))
                        sp.dma_start(tile_rows(dram["table1"], i * LOT + s), row[:, s, :]).then_inc(row_out[s], 16)
                        sp.wait_ge(ss_ready, i * LOT + (s + 1))
                        sp.dma_start(dram["source_score"][bass.ds(i * LOT + s, 1), :].rearrange(
                            "t (h n) -> (t h) n", h=2), ss[:, s, :]).then_inc(row_out[s], 16)
                peeled(sp, NLOT, body)
                for s in range(LOT):
                    sp.wait_ge(row_out[s], 32 * NLOT)

            @block.vector
            def _(dve):
                steps = Count()

                def link(ins):
                    ins.then_inc(dve_done, 1)
                    dve.wait_ge(dve_done, steps.next())

                nc.vector.memset(bias[:, :], 1.0).then_inc(b_set, 1)
                link(nc.vector.memset(WX[:, :, :], 0.0))
                dve.wait_ge(a_turned, 1)
                nc.vector.tensor_copy(aT[:, :], psX[:, 0:4]).then_inc(a_ready, 1)
                dve.wait_ge(b_turned, 1)
                nc.vector.tensor_copy(bT[:, :], psX[:, 0:2]).then_inc(a_ready, 1)
                dve.wait_ge(w_in, 16 * 5)
                for h in range(2):
                    dve.wait_ge(ab_summed, h + 1)
                    for which, col in ((1, ROW1 - 2), (0, ROW1)):
                        nc.vector.tensor_copy(bias[0:1, col + h:col + h + 1], psX[0:1, which:which + 1])
                        for k in range(KD):
                            last = nc.vector.tensor_copy(WX[:, k, col + h:col + h + 1],
                                                         psX[:, 16 * (k + 1) + which:16 * (k + 1) + which + 1])
                    last.then_inc(w_ready, 1)
                for h in range(2):
                    dve.wait_ge(w_turned, h + 1)
                    nc.vector.tensor_copy(WX[:, :, h * HW:h * HW + HD], psX[:, 0:D].rearrange(
                        "p (k n) -> p k n", k=KD)).then_inc(w_ready, 1)
                norm_all(nc, dve, link, steps, turn, X, stats, moments, mr, var_ready, dev_ready)

                def body(i, first):
                    for s in range(LOT + 2):
                        if s < LOT:
                            if not first:
                                dve.wait_ge(x_turned, i * LOT + (s + 1 - LOT))
                                dve.sem_inc(turn, 1)
                            nc.vector.tensor_scalar(xn[:, s, :], X[:, i * LOT + s, :],
                                                    mr[:, bass.ds(i * LOT + s, 1), 0],
                                                    mr[:, bass.ds(i * LOT + s, 1), 1], ALU.subtract,
                                                    ALU.mult).then_inc(xn_ready, 1)
                        if s >= 2:
                            q = s - 2
                            dve.wait_ge(s_summed, i * LOT + (q + 1))
                            if not first:
                                dve.wait_ge(row_out[q], i * 32)
                            nc.vector.tensor_copy(ss[:, q, :], psS[q % 2]).then_inc(ss_ready, 1)
                peeled(dve, NLOT, body)

            @block.scalar
            def _(act):
                act.wait_ge(var_ready, 1)
                nc.scalar.activation(mr[:, :, 1], mr[:, :, 1], ACT.Sqrt).then_inc(dev_ready, 1)

                def body(i, first):
                    for s in range(LOT + 1):
                        if s < LOT:
                            act.wait_ge(x_turned, i * LOT + (s + 1))
                            if not first:
                                act.wait_ge(s_summed, i * LOT + (s + 1 - LOT))
                            nc.scalar.activation(xT[:, s, :, :], psT[s % 3], ACT.Copy).then_inc(xT_ready, 1)
                        if s >= 1:
                            q = s - 1
                            act.wait_ge(summed, i * LOT + (q + 1))
                            if not first:
                                act.wait_ge(row_out[q], i * 32)
                            nc.scalar.activation(row[:, q, :], psR[q % 2][:, 0:ROW1], ACT.Copy).then_inc(row_ready, 1)
                peeled(act, NLOT, body)

            @block.tensor
            def _(pe):
                pe.wait_ge(w_in, 16 * 5)
                nc.tensor.transpose(psX[:, 0:4], arow[:, :], ident[0:4, 0:4]).then_inc(a_turned, 1)
                pe.wait_ge(a_ready, 1)
                nc.tensor.transpose(psX[:, 0:2], brow[:, :], ident[0:2, 0:2]).then_inc(b_turned, 1)
                pe.wait_ge(a_ready, 2)
                for h in range(2):
                    if h:
                        pe.wait_ge(w_ready, h)
                    nc.tensor.matmul(psX[0:1, 0:2], bT[:, h:h + 1], aT[:, 2 * h:2 * h + 2], start=True, stop=True)
                    for k in range(KD):
                        last = nc.tensor.matmul(psX[:, 16 * (k + 1):16 * (k + 1) + 2], W[:, h, k * P:(k + 1) * P],
                                                aT[:, 2 * h:2 * h + 2], start=True, stop=True)
                    last.then_inc(ab_summed, 1)
                for h in range(2):
                    pe.wait_ge(w_ready, 2 + h)
                    for k in range(KD):
                        last = nc.tensor.transpose(psX[:, k * P:(k + 1) * P], W[:, h, k * P:(k + 1) * P], ident[:, :])
                    last.then_inc(w_turned, 1)
                pe.wait_ge(w_ready, 4)

                def wait_past(sm, i, s, ring, first):
                    q = before(s, ring)
                    if q >= 0 or not first:
                        pe.wait_ge(sm, i * LOT + (q + 1))

                def body(i, first):
                    for s in range(LOT + 1):
                        if s < LOT:
                            pe.wait_ge(xn_ready, i * LOT + (s + 1))
                            wait_past(xT_ready, i, s, 3, first)
                            for k in range(KD):
                                last = nc.tensor.transpose(psT[s % 3][:, k, :], xn[:, s, k * P:(k + 1) * P],
                                                           ident[:, :])
                            last.then_inc(x_turned, 1)
                        if s >= 1:
                            q = s - 1
                            pe.wait_ge(xT_ready, i * LOT + (q + 1))
                            wait_past(row_ready, i, q, 2, first)
                            for k in range(KD):
                                nc.tensor.matmul(psR[q % 2], xT[:, q, k, :], WX[:, k, :], start=(k == 0), stop=False)
                            nc.tensor.matmul(psR[q % 2], ones[0:1, :], bias[0:1, :], start=False,
                                             stop=True).then_inc(summed, 1)
                            wait_past(ss_ready, i, q, 2, first)
                            for k in range(KD):
                                nc.tensor.matmul(psS[q % 2], WX[:, k, ROW1:WIDE], xT[:, q, k, :], start=(k == 0),
                                                 stop=False)
                            nc.tensor.matmul(psS[q % 2], bias[0:1, ROW1:WIDE], ones[0:1, :], start=False,
                                             stop=True).then_inc(s_summed, 1)
                peeled(pe, NLOT, body)


def gather_heads(nc, sem, bank, c, dram, acc):
    with ExitStack() as ctx, stage(nc, sem) as (sem, pool_sem):
        sb = lambda n, s, d: ctx.enter_context(nc.sbuf_tensor(f"g_{n}", s, d))
        iota, tid, ones = c["iota"], c["tid"], c["ones"]
        rec = sb("rec", [P, RING, GB, REC], I32)
        rec_f = rec[:, :, :, :].bitcast(F32)
        rows = sb("rows", [P, RING, GB, ROW1], F32)
        spot = sb("spot", [P, RING, GB, P], F32)
        scaled = sb("scaled", [P, RING, GB, 2, P], F32)
        ss = sb("ss", [P, RING, 2, P], F32)
        junk = sb("junk", [P, GB * 2, P], F32)
        own = sb("own", [P, RING, GB, 2], F32)
        score = sb("score", [P, RING, GB, 2], F32)
        leaky = sb("leaky", [P, RING, GB, 2], F32)
        e_ = sb("e", [P, RING, GB, 2], F32)
        last_rows = sb("last_rows", [P, 1], F32)
        rec_in = [sem(f"g_rec_in{k}") for k in range(RING)]
        ss_in = [sem(f"g_ss_in{k}") for k in range(RING)]
        rows_in = [[pool_sem(f"g_rows_in{k}_{e}") for e in range(GB)] for k in range(RING)]
        pad_set = sem("g_pad_set")
        acc_set = sem("g_acc_set")
        spot_ready = sem("g_spot_ready")
        dve_done = sem("g_dve_done")
        leaky_ready = sem("g_leaky_ready")
        e_ready = sem("g_e_ready")
        scaled_ready = sem("g_scaled_ready")
        summed = sem("g_summed")
        added = sem("g_added")
        turn = sem("g_turn")
        ITER = NGROUP // RING

        with nc.Block() as block:

            @block.sync
            def _(sp):
                def body(i, first):
                    for k in range(RING):
                        if not first:
                            sp.wait_ge(summed, i * RING + (k + 1 - RING))
                        sp.dma_start(rec[:, k, :, :].rearrange("p e c -> p (e c)"),
                                     dram["sorted_edges"][bass.ds((i * RING + k) * GROUP, GROUP), :].rearrange(
                                         "(p e) c -> p (e c)", p=P)).then_inc(rec_in[k], 16)
                        t = sp.value_load(tid[0:1, bass.ds(i * RING + k, 1)], min_val=0, max_val=NT - 1)
                        sp.dma_start(ss[:, k, :, :].rearrange("p h n -> p (h n)"),
                                     dram["source_score"][bass.ds(t, 1), :].to_broadcast([P, 2 * P])
                                     ).then_inc(ss_in[k], 16)
                peeled(sp, ITER, body)

            @block.gpsimd
            def _(pool):
                nc.gpsimd.memset(last_rows[:, :], 1.0).then_inc(pad_set, 1)
                pool.wait_ge(pad_set, 1)
                nc.gpsimd.affine_select(out=last_rows[:, :], in_=last_rows[:, :], compare_op=ALU.is_ge, fill=0.0,
                                        base=-LAST, pattern=[[0, 1]], channel_multiplier=1).then_inc(pad_set, 1)
                with pool.Fori(0, ITER) as i:
                    for k in range(RING):
                        pool.wait_ge(rec_in[k], i * 16 + 16)
                        pool.sem_inc(turn, 1)
                        for e in range(GB):
                            nc.gpsimd.indirect_dma_start(
                                rows[:, k, e, :], None, dram["table1"][:, :],
                                bass.IndirectOffsetOnAxis(rec[:, k, e, 2:3], 0)).then_inc(rows_in[k][e], 16)

            @block.vector
            def _(dve):
                steps = Count()

                def link(ins):
                    ins.then_inc(dve_done, 1)
                    dve.wait_ge(dve_done, steps.next())

                link(nc.vector.memset(acc[:, :, :], 0.0))
                dve.wait_ge(pad_set, 2)
                for h in range(2):
                    link(nc.vector.tensor_copy(acc[:, NT - 1, h * HW + HD:h * HW + HW], last_rows[:, :]))

                def build(i, k):
                    dve.wait_ge(rec_in[k], i * 16 + 16)
                    for e in range(GB):
                        last = nc.vector.tensor_scalar(spot[:, k, e, :], iota[:, :], rec_f[:, k, e, 0:1], None,
                                                       ALU.is_equal)
                    last.then_inc(spot_ready, 1)
                    dve.wait_ge(spot_ready, i * RING + (k + 1))
                    dve.wait_ge(ss_in[k], i * 16 + 16)
                    for e in range(GB):
                        for h in range(2):
                            last = nc.vector.tensor_tensor_reduce(junk[:, e * 2 + h, :], spot[:, k, e, :],
                                                                  ss[:, k, h, :], 1.0, 0.0, ALU.mult, ALU.add,
                                                                  own[:, k, e, h:h + 1])
                    link(last)

                def leak(i, k):
                    for e in range(GB):
                        dve.wait_ge(rows_in[k][e], i * 16 + 16)
                    link(nc.vector.tensor_tensor(score[:, k, :, :], own[:, k, :, :],
                                                 rows[:, k, :, ROW1 - 2:ROW1], ALU.add))
                    nc.vector.scalar_tensor_tensor(leaky[:, k, :, :], score[:, k, :, :], SLOPE, score[:, k, :, :],
                                                   ALU.mult, ALU.max).then_inc(leaky_ready, 1)

                def add(i, k, first):
                    dve.wait_ge(summed, i * RING + (k + 1))
                    if not (first and k == 0):
                        dve.wait_ge(added, i * RING + k)
                    dve.sem_inc(turn, 1)
                    t = dve.value_load(tid[0:1, bass.ds(i * RING + k, 1)], min_val=0, max_val=NT - 1)
                    at = acc[:, bass.ds(t, 1), :].rearrange("p a d -> p (a d)")
                    nc.vector.tensor_tensor(at, at, bank[k][:, 0:2 * HW], ALU.add).then_inc(added, 1)

                def body(i, first):
                    build(i, 0)
                    for k in range(RING):
                        if k + 1 < RING:
                            build(i, k + 1)
                        leak(i, k)
                        if k:
                            add(i, k - 1, first)
                    add(i, RING - 1, first)
                steps.enter(0, 2 * RING)
                body(0, True)
                steps.leave(1)
                with dve.Fori(1, ITER) as i:
                    steps.enter(i, 2 * RING, 1)
                    body(i, False)

            @block.scalar
            def _(act):
                def body(i, first):
                    for k in range(RING):
                        act.wait_ge(leaky_ready, i * RING + (k + 1))
                        nc.scalar.activation(e_[:, k, :, :], leaky[:, k, :, :], ACT.Exp, scale=-1.0).then_inc(e_ready, 1)
                        act.wait_ge(e_ready, i * RING + (k + 1))
                        for e in range(GB):
                            for h in range(2):
                                last = nc.scalar.activation(scaled[:, k, e, h, :], spot[:, k, e, :], ACT.Copy,
                                                            scale=e_[:, k, e, h:h + 1])
                        last.then_inc(scaled_ready, 1)
                peeled(act, ITER, body)

            @block.tensor
            def _(pe):
                def body(i, first):
                    for k in range(RING):
                        pe.wait_ge(scaled_ready, i * RING + (k + 1))
                        if not first:
                            pe.wait_ge(added, i * RING + (k + 1 - RING))
                        for e in range(GB):
                            pe.wait_ge(rows_in[k][e], i * 16 + 16)
                            for h in range(2):
                                last = nc.tensor.matmul(bank[k][:, h * HW:(h + 1) * HW], scaled[:, k, e, h, :],
                                                        rows[:, k, e, h * HW:(h + 1) * HW], start=(e == 0 and h == 0),
                                                        stop=(e == GB - 1), skip_group_check=True)
                        last.then_inc(summed, 1)
                peeled(pe, ITER, body)


def finish_heads(nc, sem, c, acc):
    with ExitStack() as ctx, stage(nc, sem) as (sem, pool_sem):
        sb = lambda n, s, d: ctx.enter_context(nc.sbuf_tensor(f"f_{n}", s, d))
        X = c["X"]
        by_head = acc[:, :, :].rearrange("p t (h w) -> p t h w", h=2)
        inv = sb("inv", [P, LOT, 2], F32)
        mean = sb("mean", [P, 2, LOT, 2, HD], F32)
        low = sb("low", [P, 2, LOT, 2, HD], F32)
        dve_done = sem("f_dve_done")
        turn = sem("f_turn")
        low_ready = sem("f_low_ready")
        exp_ready = sem("f_exp_ready")

        with nc.Block() as block:

            @block.vector
            def _(dve):
                steps = Count()

                def link(ins):
                    ins.then_inc(dve_done, 1)
                    dve.wait_ge(dve_done, steps.next())

                def divide(i, s):
                    link(nc.vector.reciprocal(inv[:, :, :], by_head[:, bass.ds(i * LOT, LOT), :, HD]))
                    dve.sem_inc(turn, 1)
                    for t in range(LOT):
                        last = nc.vector.tensor_tensor(mean[:, s, t, :, :], by_head[:, i * LOT + t, :, 0:HD],
                                                       widen(inv[:, t, :], HD), ALU.mult)
                    link(last)
                    nc.vector.tensor_scalar(low[:, s, :, :, :], mean[:, s, :, :, :], 0.0, None,
                                            ALU.min).then_inc(low_ready, 1)

                def grow(i, s):
                    dve.wait_ge(exp_ready, i + 1)
                    link(nc.vector.scalar_tensor_tensor(mean[:, s, :, :, :].rearrange("p t h n -> p (t h n)"),
                                                        mean[:, s, :, :, :].rearrange("p t h n -> p (t h n)"), 0.0,
                                                        low[:, s, :, :, :].rearrange("p t h n -> p (t h n)"),
                                                        ALU.max, ALU.add))
                    dve.sem_inc(turn, 1)
                    xs = X[:, bass.ds(i * LOT, LOT), :].rearrange("p t d -> p (t d)")
                    link(nc.vector.scalar_tensor_tensor(xs, mean[:, s, :, :, :].rearrange("p t h n -> p (t h n)"), -1.0,
                                                        xs, ALU.add, ALU.add))

                for i in range(NLOT):
                    divide(i, i % 2)
                    if i:
                        grow(i - 1, (i - 1) % 2)
                grow(NLOT - 1, (NLOT - 1) % 2)

            @block.scalar
            def _(act):
                for i in range(NLOT):
                    act.wait_ge(low_ready, i + 1)
                    nc.scalar.activation(low[:, i % 2, :, :, :], low[:, i % 2, :, :, :], ACT.Exp).then_inc(exp_ready, 1)


def build(nc, a, out):
    with ExitStack() as ctx:
        def sb(name, shape, dt):
            return ctx.enter_context(nc.sbuf_tensor(name, shape, dt))

        def sem(name):
            return ctx.enter_context(nc.semaphore(name))

        bank = [ctx.enter_context(nc.psum_tensor(f"bank{b}", [P, 512], F32)) for b in range(8)]
        dram = {
            "sorted_edges": nc.dram_tensor("sorted_edges", (SLOTS + P, REC), I32).ap(),
            "table0": nc.dram_tensor("table0", (NT * P, D), F32).ap(),
            "table1": nc.dram_tensor("table1", (NT * P, ROW1), F32).ap(),
            "source_score": nc.dram_tensor("source_score", (NT, 2 * P), F32).ap(),
            "xn": nc.dram_tensor("dram_xn", (NT * P, D), F32).ap(),
            "sent": nc.dram_tensor("dram_sent", (BLOCKS_MAX * P, D), F32).ap(),
            "eid": nc.dram_tensor("dram_eid", (P,), I32).ap(),
            "group_tile": nc.dram_tensor("group_tile", (-(-NGROUP // P) * P,), I32).ap(),
        }
        c = {
            "X": sb("X", [P, NT, D], F32),
            "ident": sb("ident", [P, P], F32),
            "tri": sb("tri", [P, P], F32),
            "ones": sb("ones", [P, P], F32),
            "iota": sb("iota", [P, P], F32),
            "tid": sb("tid", [1, NGROUP], I32),
        }
        sort_and_project(nc, sem, bank, c, a, dram)
        gather_sum0(nc, sem, bank, c, dram)
        for layer in range(2):
            if layer == 1:
                project_heads(nc, sem, bank, c, a, dram)
                with nc.sbuf_tensor("acc", [P, NT, 2 * HW], F32) as acc:
                    gather_heads(nc, sem, bank, c, dram, acc)
                    finish_heads(nc, sem, c, acc)
            with ExitStack() as inner:
                m = dict(MOE[layer])
                tensor = lambda n, s, d: inner.enter_context(nc.sbuf_tensor(f"m{layer}_{n}", s, d))
                dram["made"] = nc.dram_tensor(f"dram_made{layer}", (m["blocks"] * P, D), F32).ap()
                m["gates"] = tensor("gates", [P, 2, NT], F32)
                m["gates_by"] = tensor("gates_by", [P, NT, m["E"]], F32)
                m["pos"] = tensor("pos", [P, 2 * NT], I32)
                m["eid"] = tensor("eid", [1, P], I32)
                route(nc, sem, bank, c, a, dram, layer, m)
                experts(nc, sem, bank, c, a, dram, layer, m)
                combine(nc, sem, bank, c, a, dram, layer, m, out if layer == 1 else None)


_INS = ['x', 'src', 'dst', 'edge_weight', 'L0_gnn_W', 'L0_ffn_router_w1', 'L0_ffn_router_b1', 'L0_ffn_router_w2',
        'L0_ffn_router_b2', 'L0_ffn_expert_w1', 'L0_ffn_expert_b1', 'L0_ffn_expert_w2', 'L0_ffn_expert_b2',
        'L0_ffn_expert_w3', 'L0_ffn_expert_b3', 'L1_gnn_W', 'L1_gnn_b', 'L1_gnn_a', 'L1_ffn_gate_w',
        'L1_ffn_gate_b', 'L1_ffn_w1', 'L1_ffn_b1', 'L1_ffn_w2', 'L1_ffn_b2', 'L1_ffn_gamma', 'L1_ffn_beta']


def kernel(**inputs):
    import numpy as _np
    import concourse.bacc as _bacc
    from concourse import mybir as _mybir
    from concourse.bass_utils import run_bass_kernel_spmd as _run

    nc = _bacc.Bacc("TRN2", target_bir_lowering=False, num_devices=1)
    arrays, args = {}, {}
    for name in _INS:
        v = _np.ascontiguousarray(inputs[name])
        arrays[f"in_{name}_dram"] = v
        args[name] = nc.dram_tensor(f"in_{name}_dram", v.shape, _mybir.dt.from_np(v.dtype), kind="ExternalInput").ap()
    out = nc.dram_tensor("out_0_dram", (N, D), _mybir.dt.float32, kind="ExternalOutput").ap()
    build(nc, args, out)
    r = _run(nc, [arrays], core_ids=[0])
    return r.results[0]["out_0_dram"]
```

```python
from contextlib import ExitStack, contextmanager

import concourse.bass as bass
from concourse import mybir

ALU = mybir.AluOpType
ACT = mybir.ActivationFunctionType
AX = mybir.AxisListType
F32 = mybir.dt.float32
BF16 = mybir.dt.bfloat16
I32 = mybir.dt.int32

P = 128
EPS = 1e-5
SLOPE = 0.2

N, D, EDGES = 6250, 256, 206250
NT = -(-N // P)
LAST = N - (NT - 1) * P
KD = D // P

LANE = -(-EDGES // P)
LANE_LAST = EDGES - (P - 1) * LANE
CHUNK = 26
NCHUNK = LANE // CHUNK
BUCKETS = NT + 1
assert NCHUNK * CHUNK == LANE and NCHUNK % 2 == 0

GROUP = 256
GB = GROUP // P
RING = 8
NGROUP = (EDGES + NT * (GROUP - 1)) // GROUP
SLOTS = NGROUP * GROUP
FILLS = 8
FILL = -(-(SLOTS + P) // (FILLS * P))
REC = 3
assert P * LANE - EDGES <= P

HD = D // 2
HW = HD + 1
ROW1 = 2 * HW + 2


class Count:

    def __init__(self):
        self.n, self.i, self.k = 0, None, 0

    def enter(self, i, per, start=0):
        self.i, self.per, self.k, self.start = i, per, 0, start

    def next(self):
        if self.i is None:
            self.n += 1
            return self.n
        self.k += 1
        return self.i * self.per + (self.n + self.k - self.start * self.per)

    def leave(self, count):
        assert self.k == self.per, (self.k, self.per)
        self.n += self.per * count
        self.i = None


def peeled(engine, count, body):
    body(0, True)
    with engine.Fori(1, count) as i:
        body(i, False)


def each_group(engine, step):
    for k in range(RING):
        step(0, k, True)
    with engine.Fori(1, NGROUP // RING) as i:
        for k in range(RING):
            step(i, k, False)
    for k in range(NGROUP % RING):
        step(NGROUP // RING, k, False)


@contextmanager
def stage(nc, kept):
    own = []

    def sem(name):
        own.append(nc.alloc_semaphore(name=name))
        return own[-1]

    yield sem, kept
    nc.clear_and_free_semaphores(own)
    nc.all_engine_barrier()


def tile_rows(dram, t):
    return dram[bass.ds(t * P, P), :]


def spread(ap, n):
    return ap.unsqueeze(1).to_broadcast([ap.shape[0], n, ap.shape[1]])


def widen(ap, n):
    return ap.unsqueeze(2).to_broadcast([ap.shape[0], ap.shape[1], n])


def sort_and_project(nc, sem, bank, c, a, dram):
    with ExitStack() as ctx, stage(nc, sem) as (sem, pool_sem):
        sb = lambda n, s, d: ctx.enter_context(nc.sbuf_tensor(n, s, d))
        X, ident, tri, ones, iota = c["X"], c["ident"], c["tri"], c["ones"], c["iota"]
        lane_src = sb("lane_src", [P, LANE], I32)
        lane_dst = sb("lane_dst", [P, LANE], I32)
        lane_w = sb("lane_w", [P, LANE], F32)
        tile_i = sb("tile_i", [P, LANE], I32)
        tile_f = sb("tile_f", [P, LANE], F32)
        rec = sb("rec", [P, LANE, REC], I32)
        rec_f = rec[:, :, :].bitcast(F32)
        hits = sb("hits", [P, LANE], BF16)
        fill = sb("fill", [P, FILL, REC], F32)
        bucket_iota = sb("bucket_iota", [P, BUCKETS, CHUNK], F32)
        carry_mask = sb("carry_mask", [P, BUCKETS, CHUNK], F32)
        member = sb("member", [P, BUCKETS, CHUNK], F32)
        ranks = sb("ranks", [P, BUCKETS, CHUNK], F32)
        own = sb("own", [P, BUCKETS, CHUNK], F32)
        first_col = sb("first_col", [P, BUCKETS], F32)
        run = sb("run", [P, BUCKETS], F32)
        lane_count = sb("lane_count", [P, BUCKETS], F32)
        groups_i = sb("groups_i", [P, 2, BUCKETS], I32)
        groups = sb("groups", [P, BUCKETS], F32)
        group_end = sb("group_end", [P, BUCKETS], F32)
        group_start = sb("group_start", [P, BUCKETS], F32)
        NQ = -(-NGROUP // P)
        group_no = sb("group_no", [P, NQ], F32)
        past = sb("past", [P, NQ, NT], F32)
        tid_f = sb("tid_f", [P, NQ], F32)
        tid_i = sb("tid_i", [P, NQ], I32)
        pos_f = sb("pos_f", [P, CHUNK], F32)
        pos_ring = sb("pos_ring", [P, 2, CHUNK], I32)
        rec_ring = sb("rec_ring", [P, 2, CHUNK, REC], I32)
        Wn = sb("Wn", [P, KD, D], F32)
        WT = sb("WT", [P, KD, D], F32)
        stats = sb("stats", [P, 2, 6], F32)
        moments = sb("moments", [P, 2, 2], F32)
        dev = sb("dev", [P, 2], F32)
        rstd = sb("rstd", [P, 2], F32)
        xn = sb("xn", [P, 2, D], F32)
        xT = sb("xT", [P, 2, KD, P], F32)
        xp = sb("xp", [P, 2, D], F32)

        zeros = sb("zeros", [P, D], F32)
        cleared = sem("a_cleared")
        pads_set = sem("a_pads_set")
        fill_set = sem("a_fill_set")
        consts_set = sem("a_consts_set")
        edges_in = sem("a_edges_in")
        x_in = sem("a_x_in")
        w_in = sem("a_w_in")
        filled = sem("a_filled")
        w_turned = sem("a_w_turned")
        w_ready = sem("a_w_ready")
        dve_done = sem("a_dve_done")
        counted = sem("a_counted")
        summed = sem("a_summed")
        ranked = sem("a_ranked")
        scattered = [pool_sem(f"a_scattered{s}") for s in range(2)]
        var_ready = sem("a_var_ready")
        dev_ready = sem("a_dev_ready")
        xn_ready = sem("a_xn_ready")
        x_turned = sem("a_x_turned")
        xT_ready = sem("a_xT_ready")
        projected = sem("a_projected")
        xp_ready = sem("a_xp_ready")
        stored = [sem(f"a_stored{s}") for s in range(2)]
        tid_ready = sem("a_tid_ready")
        tid_out = sem("a_tid_out")
        tid_in = sem("a_tid_in")
        turn = sem("a_turn")
        pool_done = sem("a_pool_done")

        psW = bank[0][:, :].rearrange("p (k o) -> p k o", k=KD)
        psC = bank[1]
        psT = [bank[2 + s][:, 0:D].rearrange("p (k n) -> p k n", k=KD) for s in range(2)]
        psP = [bank[4 + s][:, 0:D] for s in range(2)]

        table = dram["table0"]
        sorted_edges = dram["sorted_edges"]

        with nc.Block() as block:

            @block.sync
            def _(sp):
                sp.wait_ge(pads_set, 4)
                cut = (P - 1) // 16 * 16
                for name, lanes in (("src", lane_src), ("dst", lane_dst), ("edge_weight", lane_w)):
                    flat = a[name]
                    for lo, hi in ((0, cut), (cut, P - 1)):
                        sp.dma_start(lanes[lo:hi, :], flat[lo * LANE:hi * LANE].rearrange(
                            "(p t) -> p t", t=LANE)).then_inc(edges_in, 16)
                    sp.dma_start(lanes[P - 1:P, 0:LANE_LAST], flat[(P - 1) * LANE:EDGES].rearrange(
                        "(p t) -> p t", p=1)).then_inc(edges_in, 16)
                full = (NT - 1) * P
                sp.dma_start(X[:, 0:NT - 1, :], a["x"][0:full, :].rearrange(
                    "(t p) d -> p t d", p=P)).then_inc(x_in, 16)
                sp.dma_start(X[0:LAST, NT - 1, :], a["x"][full:N, :]).then_inc(x_in, 16)
                sp.dma_start(Wn[:, :, :], a["L0_gnn_W"].rearrange("(k p) d -> p k d", p=P)).then_inc(w_in, 16)
                sp.wait_ge(fill_set, 3)
                for q in range(FILLS):
                    sp.dma_start(sorted_edges[q * P * FILL:(q + 1) * P * FILL, :].rearrange(
                        "(p s) c -> p s c", p=P), fill[:, :, :].bitcast(I32)).then_inc(filled, 16)
                sp.dma_start(dram["sent"].rearrange("(p r) d -> p r d", p=P),
                             zeros[:, :].unsqueeze(1).to_broadcast([P, BLOCKS_MAX, D])).then_inc(cleared, 16)
                sp.wait_ge(tid_ready, 1)
                sp.dma_start(dram["group_tile"][0:NQ * P].rearrange("(p q) -> p q", p=P),
                             tid_i[:, :]).then_inc(tid_out, 16)
                sp.wait_ge(tid_out, 16)
                sp.dma_start(c["tid"][0:1, :], dram["group_tile"][0:NGROUP].rearrange(
                    "(p g) -> p g", p=1)).then_inc(tid_in, 16)
                with sp.Fori(0, NT // 2) as i:
                    for s in range(2):
                        sp.wait_ge(xp_ready, i * 2 + s + 1)
                        sp.dma_start(tile_rows(table, i * 2 + s), xp[:, s, :]).then_inc(stored[s], 16)
                sp.wait_ge(xp_ready, NT)
                sp.dma_start(tile_rows(table, NT - 1), xp[:, 0, :]).then_inc(stored[0], 16)
                sp.wait_ge(stored[0], 16 * (NT - NT // 2))
                sp.wait_ge(stored[1], 16 * (NT // 2))
                sp.wait_ge(tid_in, 16)
                sp.wait_ge(cleared, 16)

            @block.gpsimd
            def _(pool):
                nc.gpsimd.iota(bucket_iota[:, :, :], pattern=[[1, BUCKETS], [0, CHUNK]], base=0,
                               channel_multiplier=0, allow_small_or_imprecise_dtypes=True).then_inc(consts_set, 1)
                nc.gpsimd.iota(group_no[:, :], pattern=[[1, NQ]], base=0, channel_multiplier=NQ,
                               allow_small_or_imprecise_dtypes=True).then_inc(consts_set, 1)
                nc.gpsimd.iota(iota[:, :], pattern=[[1, P]], base=0, channel_multiplier=0,
                               allow_small_or_imprecise_dtypes=True).then_inc(consts_set, 1)
                nc.gpsimd.memset(ident[:, :], 0.0).then_inc(pool_done, 1)
                nc.gpsimd.memset(tri[:, :], 1.0).then_inc(pool_done, 1)
                nc.gpsimd.memset(ones[:, :], 1.0).then_inc(consts_set, 1)
                pool.wait_ge(pool_done, 2)
                nc.gpsimd.affine_select(out=ident[:, :], in_=ident[:, :], compare_op=ALU.not_equal, fill=1.0,
                                        base=0, pattern=[[-1, P]], channel_multiplier=1).then_inc(consts_set, 1)
                nc.gpsimd.affine_select(out=tri[:, :], in_=tri[:, :], compare_op=ALU.is_gt, fill=0.0,
                                        base=0, pattern=[[1, P]], channel_multiplier=-1).then_inc(consts_set, 1)
                pool.wait_ge(filled, 16 * FILLS)

                with pool.Fori(0, NCHUNK // 2) as i:
                    for s in range(2):
                        pool.wait_ge(ranked, i * 2 + s + 1)
                        pool.sem_inc(turn, 1)
                        for t in range(CHUNK):
                            nc.gpsimd.indirect_dma_start(
                                sorted_edges[:, :], bass.IndirectOffsetOnAxis(pos_ring[:, s, t:t + 1], 0),
                                rec_ring[:, s, t, :], None).then_inc(scattered[s], 16)
                for s in range(2):
                    pool.wait_ge(scattered[s], NCHUNK // 2 * CHUNK * 16)

            @block.vector
            def _(dve):
                steps = Count()

                def link(ins):
                    ins.then_inc(dve_done, 1)
                    dve.wait_ge(dve_done, steps.next())

                nc.vector.memset(lane_src[96:P, LANE_LAST:LANE], NT * P).then_inc(pads_set, 1)
                nc.vector.memset(lane_dst[96:P, LANE_LAST:LANE], 0).then_inc(pads_set, 1)
                nc.vector.memset(lane_w[96:P, LANE_LAST:LANE], 0.0).then_inc(pads_set, 1)
                nc.vector.memset(X[:, NT - 1, :], 0.0).then_inc(pads_set, 1)
                nc.vector.memset(zeros[:, :], 0.0).then_inc(fill_set, 1)
                nc.vector.memset(fill[:, :, 0], -1.0).then_inc(fill_set, 1)
                nc.vector.memset(fill[:, :, 1:REC], 0.0).then_inc(fill_set, 1)
                link(nc.vector.memset(carry_mask[:, :, :], 1.0))
                nc.vector.memset(carry_mask[:, :, 0], 0.0)
                dve.wait_ge(edges_in, 16 * 9)
                link(nc.vector.tensor_scalar(tile_i[:, :], lane_src[:, :], 7, None, ALU.arith_shift_right))
                link(nc.vector.tensor_copy(tile_f[:, :], tile_i[:, :]))
                link(nc.vector.tensor_scalar(tile_i[:, :], lane_src[:, :], P - 1, None, ALU.bitwise_and))
                nc.vector.tensor_copy(rec_f[:, :, 0], tile_i[:, :])
                nc.vector.tensor_copy(rec_f[:, :, 1], lane_w[:, :])
                nc.vector.tensor_copy(rec[:, :, 2], lane_dst[:, :])
                for b in range(BUCKETS):
                    link(nc.vector.tensor_scalar(hits[:, :], tile_f[:, :], float(b), None, ALU.is_equal,
                                                 ALU.add, accum_out=lane_count[:, b:b + 1]))
                dve.sem_inc(counted, 1)
                dve.wait_ge(summed, 1)
                link(nc.vector.tensor_scalar(groups_i[:, 0, :], psC[:, BUCKETS:2 * BUCKETS], float(GROUP - 1), None,
                                             ALU.add))
                link(nc.vector.tensor_scalar(groups_i[:, 1, :], groups_i[:, 0, :], GROUP.bit_length() - 1, None,
                                             ALU.arith_shift_right))
                link(nc.vector.tensor_copy(groups[:, :], groups_i[:, 1, :]))
                dve.wait_ge(consts_set, 6)
                link(nc.vector.tensor_tensor_scan(group_end[:, :], ones[:, 0:BUCKETS], groups[:, :], 0.0,
                                                  ALU.mult, ALU.add))
                link(nc.vector.tensor_tensor(group_start[:, :], group_end[:, :], groups[:, :], ALU.subtract))
                link(nc.vector.memset(group_start[:, NT:NT + 1], float(NGROUP)))
                link(nc.vector.scalar_tensor_tensor(run[:, :], group_start[:, :], float(GROUP), psC[:, 0:BUCKETS],
                                                    ALU.mult, ALU.add))
                link(nc.vector.tensor_tensor(past[:, :, :], spread(group_end[:, 0:NT], NQ),
                                             widen(group_no[:, :], NT), ALU.is_le))
                link(nc.vector.tensor_reduce(tid_f[:, :], past[:, :, :], AX.X, ALU.add))
                nc.vector.tensor_scalar(tid_i[:, :], tid_f[:, :], float(NT - 1), None, ALU.min).then_inc(tid_ready, 1)

                def rank(t0, s, wait_slot):
                    link(nc.vector.tensor_tensor(member[:, :, :], bucket_iota[:, :, :],
                                                 spread(tile_f[:, bass.ds(t0, CHUNK)], BUCKETS), ALU.is_equal))
                    link(nc.vector.tensor_copy(first_col[:, :], member[:, :, 0]))
                    link(nc.vector.tensor_tensor(member[:, :, 0], member[:, :, 0], run[:, :], ALU.add))
                    link(nc.vector.tensor_tensor_scan(ranks[:, :, :].rearrange("p b t -> p (b t)"),
                                                      carry_mask[:, :, :].rearrange("p b t -> p (b t)"),
                                                      member[:, :, :].rearrange("p b t -> p (b t)"), 0.0,
                                                      ALU.mult, ALU.add))
                    link(nc.vector.tensor_copy(member[:, :, 0], first_col[:, :]))
                    nc.vector.tensor_copy(run[:, :], ranks[:, :, CHUNK - 1])
                    link(nc.vector.tensor_tensor(own[:, :, :], member[:, :, :], ranks[:, :, :], ALU.mult))
                    link(nc.vector.tensor_reduce(pos_f[:, :], own[:, :, :].rearrange("p b t -> p t b"), AX.X,
                                                 ALU.add))
                    wait_slot()
                    nc.vector.tensor_scalar(pos_ring[:, s, :], pos_f[:, :], -1.0, None, ALU.add)
                    nc.vector.tensor_copy(rec_ring[:, s, :, :], rec[:, bass.ds(t0, CHUNK), :]).then_inc(ranked, 1)

                RANK_LINKS = 7

                dve.wait_ge(x_in, 32)

                def step(i, first):
                    steps.enter(i, 2 * RANK_LINKS + 2 * 3 + 2, 0 if first else 1)
                    for s in range(2):
                        def slot_free(s=s):
                            if not first:
                                dve.wait_ge(scattered[s], i * (16 * CHUNK))
                        rank((i * 2 + s) * CHUNK, s, slot_free)
                        link(nc.vector.bn_stats(stats[:, s, :], X[:, i * 2 + s, :]))
                        dve.sem_inc(turn, 1)
                        link(nc.vector.bn_aggr(moments[:, s, :], stats[:, s, :]))
                        link(nc.vector.tensor_scalar(moments[:, s, 1:2], moments[:, s, 1:2], EPS, None, ALU.add))
                        nc.vector.tensor_copy(dev[:, s:s + 1], moments[:, s, 1:2]).then_inc(var_ready, 1)
                        dve.wait_ge(dev_ready, i * 2 + s + 1)
                        link(nc.vector.reciprocal(rstd[:, s:s + 1], dev[:, s:s + 1]))
                        if not first:
                            dve.wait_ge(x_turned, i * 2 + s - 1)
                        nc.vector.tensor_scalar(xn[:, s, :], X[:, i * 2 + s, :], moments[:, s, 0:1],
                                                rstd[:, s:s + 1], ALU.subtract, ALU.mult).then_inc(xn_ready, 1)

                step(0, True)
                steps.leave(1)
                with dve.Fori(1, NT // 2) as i:
                    step(i, False)
                steps.leave(NT // 2 - 1)
                t = NT - 1
                link(nc.vector.bn_stats(stats[:, 0, :], X[:, t, :]))
                link(nc.vector.bn_aggr(moments[:, 0, :], stats[:, 0, :]))
                link(nc.vector.tensor_scalar(moments[:, 0, 1:2], moments[:, 0, 1:2], EPS, None, ALU.add))
                nc.vector.tensor_copy(dev[:, 0:1], moments[:, 0, 1:2]).then_inc(var_ready, 1)
                dve.wait_ge(dev_ready, NT)
                link(nc.vector.reciprocal(rstd[:, 0:1], dev[:, 0:1]))
                dve.wait_ge(x_turned, NT - 2)
                nc.vector.tensor_scalar(xn[:, 0, :], X[:, t, :], moments[:, 0, 0:1],
                                        rstd[:, 0:1], ALU.subtract, ALU.mult).then_inc(xn_ready, 1)
                with dve.Fori(NT // 2, NCHUNK // 2) as i:
                    steps.enter(i, 2 * RANK_LINKS, NT // 2)
                    for s in range(2):
                        rank((i * 2 + s) * CHUNK, s, lambda s=s: dve.wait_ge(scattered[s], i * (16 * CHUNK)))

            @block.scalar
            def _(act):
                act.wait_ge(w_turned, 1)
                nc.scalar.activation(WT[:, :, :], psW, ACT.Copy).then_inc(w_ready, 1)

                def step(t, s, first, i):
                    act.wait_ge(var_ready, t + 1)
                    nc.scalar.activation(dev[:, s:s + 1], dev[:, s:s + 1], ACT.Sqrt).then_inc(dev_ready, 1)
                    act.wait_ge(x_turned, t + 1)
                    if not first:
                        act.wait_ge(projected, t - 1)
                    nc.scalar.activation(xT[:, s, :, :], psT[s], ACT.Copy).then_inc(xT_ready, 1)
                    act.wait_ge(projected, t + 1)
                    if not first:
                        act.wait_ge(stored[s], i * 16)
                    nc.scalar.activation(xp[:, s, :], psP[s], ACT.Copy).then_inc(xp_ready, 1)

                for s in range(2):
                    step(s, s, True, 0)
                with act.Fori(1, NT // 2) as i:
                    for s in range(2):
                        step(i * 2 + s, s, False, i)
                step(NT - 1, 0, False, NT // 2)

            @block.tensor
            def _(pe):
                pe.wait_ge(consts_set, 6)
                pe.wait_ge(w_in, 16)
                for k in range(KD):
                    for o in range(KD):
                        last = nc.tensor.transpose(psW[:, k, o * P:(o + 1) * P], Wn[:, o, k * P:(k + 1) * P],
                                                   ident[:, :])
                last.then_inc(w_turned, 1)
                pe.wait_ge(counted, 1)
                nc.tensor.matmul(psC[:, 0:BUCKETS], tri[:, :], lane_count[:, :], start=True, stop=True)
                nc.tensor.matmul(psC[:, BUCKETS:2 * BUCKETS], ones[:, :], lane_count[:, :], start=True,
                                 stop=True).then_inc(summed, 1)
                pe.wait_ge(w_ready, 1)

                def step(t, s, first):
                    pe.wait_ge(xn_ready, t + 1)
                    if not first:
                        pe.wait_ge(xT_ready, t - 1)
                    for k in range(KD):
                        last = nc.tensor.transpose(psT[s][:, k, :], xn[:, s, k * P:(k + 1) * P], ident[:, :])
                    last.then_inc(x_turned, 1)
                    pe.wait_ge(xT_ready, t + 1)
                    if not first:
                        pe.wait_ge(xp_ready, t - 1)
                    for k in range(KD):
                        last = nc.tensor.matmul(psP[s], xT[:, s, k, :], WT[:, k, :], start=(k == 0),
                                                stop=(k == KD - 1))
                    last.then_inc(projected, 1)

                for s in range(2):
                    step(s, s, True)
                with pe.Fori(1, NT // 2) as i:
                    for s in range(2):
                        step(i * 2 + s, s, False)
                step(NT - 1, 0, False)


def gather_sum0(nc, sem, bank, c, dram):
    with ExitStack() as ctx, stage(nc, sem) as (sem, pool_sem):
        sb = lambda n, s, d: ctx.enter_context(nc.sbuf_tensor(n, s, d))
        X, iota, tid = c["X"], c["iota"], c["tid"]
        rec = sb("b_rec", [P, RING, GB, REC], I32)
        rec_f = rec[:, :, :, :].bitcast(F32)
        rows = sb("b_rows", [P, RING, GB, D], F32)
        spot = sb("b_spot", [P, RING, GB, P], F32)
        rec_in = [sem(f"b_rec_in{k}") for k in range(RING)]
        rows_in = [pool_sem(f"b_rows_in{k}") for k in range(RING)]
        spot_ready = sem("b_spot_ready")
        summed = sem("b_summed")
        added = sem("b_added")
        turn = sem("b_turn")
        LAG = 4

        with nc.Block() as block:

            @block.sync
            def _(sp):
                def load(i, k, first):
                    if not first:
                        sp.wait_ge(summed, i * RING + (k + 1 - RING))
                    sp.dma_start(rec[:, k, :, :].rearrange("p e c -> p (e c)"),
                                 dram["sorted_edges"][bass.ds((i * RING + k) * GROUP, GROUP), :].rearrange(
                                     "(p e) c -> p (e c)", p=P)).then_inc(rec_in[k], 16)
                each_group(sp, load)

            @block.gpsimd
            def _(pool):
                def gather(i, k, first):
                    pool.wait_ge(rec_in[k], i * 16 + 16)
                    pool.sem_inc(turn, 1)
                    for e in range(GB):
                        nc.gpsimd.indirect_dma_start(
                            rows[:, k, e, :], None, dram["table0"][:, :],
                            bass.IndirectOffsetOnAxis(rec[:, k, e, 2:3], 0)).then_inc(rows_in[k], 16)
                each_group(pool, gather)

            @block.vector
            def _(dve):
                def build(i, k):
                    dve.wait_ge(rec_in[k], i * 16 + 16)
                    for e in range(GB):
                        last = nc.vector.tensor_scalar(spot[:, k, e, :], iota[:, :], rec_f[:, k, e, 0:1],
                                                       rec_f[:, k, e, 1:2], ALU.is_equal, ALU.mult)
                    last.then_inc(spot_ready, 1)

                def add(i, k, very_first=False):
                    dve.wait_ge(summed, i * RING + (k + 1))
                    if not very_first:
                        dve.wait_ge(added, i * RING + k)
                    dve.sem_inc(turn, 1)
                    t = dve.value_load(tid[0:1, bass.ds(i * RING + k, 1)], min_val=0, max_val=NT - 1)
                    nc.vector.tensor_tensor(X[:, bass.ds(t, 1), :].rearrange("p a d -> p (a d)"),
                                            X[:, bass.ds(t, 1), :].rearrange("p a d -> p (a d)"),
                                            bank[k % RING][:, 0:D], ALU.add).then_inc(added, 1)

                def step(i, k, first):
                    build(i, k)
                    if not first or k >= LAG:
                        add(i, k - LAG, first and k == LAG)
                each_group(dve, step)
                for k in range(NGROUP % RING - LAG, NGROUP % RING):
                    add(NGROUP // RING, k)

            @block.tensor
            def _(pe):
                def total(i, k, first):
                    pe.wait_ge(spot_ready, i * RING + (k + 1))
                    if not first:
                        pe.wait_ge(added, i * RING + (k + 1 - RING))
                    pe.wait_ge(rows_in[k], (i + 1) * (16 * GB))
                    for e in range(GB):
                        last = nc.tensor.matmul(bank[k][:, 0:D], spot[:, k, e, :], rows[:, k, e, :],
                                                start=(e == 0), stop=(e == GB - 1))
                    last.then_inc(summed, 1)
                each_group(pe, total)


def blocks_of(experts, ring):
    n = (2 * NT * P + experts * (P - 1)) // P
    return -(-n // ring) * ring


MOE = [
    {"E": 6, "widths": [D, 256, 256, D], "ring": 4, "ahead": 2, "blocks": blocks_of(6, 4), "softmax": True,
     "router_w1": "L0_ffn_router_w1", "router_b1": "L0_ffn_router_b1", "router_w2": "L0_ffn_router_w2",
     "router_b2": "L0_ffn_router_b2", "w": ["L0_ffn_expert_w1", "L0_ffn_expert_w2", "L0_ffn_expert_w3"],
     "b": ["L0_ffn_expert_b1", "L0_ffn_expert_b2"], "b_last": "L0_ffn_expert_b3"},
    {"E": 16, "widths": [D, 512, D], "ring": 3, "ahead": 1, "blocks": blocks_of(16, 3), "softmax": False,
     "router_w2": "L1_ffn_gate_w", "router_b2": "L1_ffn_gate_b", "w": ["L1_ffn_w1", "L1_ffn_w2"],
     "b": ["L1_ffn_b1"], "b_last": "L1_ffn_b2"},
]
BLOCKS_MAX = max(m["blocks"] for m in MOE)
LOT = 7
NLOT = NT // LOT
assert NLOT * LOT == NT


def before(s, ring):
    same = [q for q in range(LOT) if q % ring == s % ring]
    return s - ring if s >= ring else same[-1] - LOT


def after(engine, sem, count):
    if not isinstance(count, int) or count > 0:
        engine.wait_ge(sem, count)


def each_tile(engine, jobs):
    def lot(i):
        for s in range(LOT):
            for job, lag in jobs:
                if not isinstance(i, int) or i * LOT + s >= lag:
                    job(i, s - lag)
    lot(0)
    lot(1)
    with engine.Fori(2, NLOT) as i:
        lot(i)
    for s in range(max(lag for _, lag in jobs)):
        for job, lag in jobs:
            if s < lag:
                job(NLOT, s - lag)


def norm_all(nc, dve, link, steps, turn, X, stats, moments, mr, var_ready, dev_ready):
    with dve.Fori(0, NLOT) as i:
        steps.enter(i, 3)
        for s in range(LOT):
            last = nc.vector.bn_stats(stats[:, s, :], X[:, i * LOT + s, :])
        link(last)
        dve.sem_inc(turn, 1)
        for s in range(LOT):
            last = nc.vector.bn_aggr(moments[:, s, :], stats[:, s, :])
        link(last)
        dve.sem_inc(turn, 1)
        link(nc.vector.tensor_copy(mr[:, bass.ds(i * LOT, LOT), :], moments[:, :, :]))
        dve.sem_inc(turn, 1)
    steps.leave(NLOT)
    nc.vector.tensor_scalar(mr[:, :, 1], mr[:, :, 1], EPS, None, ALU.add).then_inc(var_ready, 1)
    dve.wait_ge(dev_ready, 1)
    link(nc.vector.reciprocal(mr[:, :, 1], mr[:, :, 1]))


def route(nc, sem, bank, c, a, dram, layer, m):
    E = m["E"]
    L = layer
    hidden = "router_w1" in m
    with ExitStack() as ctx, stage(nc, sem) as (sem, pool_sem):
        sb = lambda n, s, d: ctx.enter_context(nc.sbuf_tensor(f"r{L}_{n}", s, d))
        X, ident, tri, ones = c["X"], c["ident"], c["tri"], c["ones"]
        gates, gates_by, pos, eid = m["gates"], m["gates_by"], m["pos"], m["eid"]
        stats = sb("stats", [P, LOT, 6], F32)
        moments = sb("moments", [P, LOT, 2], F32)
        mr = sb("mr", [P, NT, 2], F32)
        xn = sb("xn", [P, LOT, D], F32)
        xT = sb("xT", [P, LOT, KD, P], F32)
        w1 = sb("w1", [P, KD, P], F32)
        b1 = sb("b1", [P, 1], F32)
        w2 = sb("w2", [P, KD, E], F32)
        b2 = sb("b2", [P, E], F32)
        rh = sb("rh", [P, LOT, P], F32)
        logits = sb("logits", [P, NT, E], F32)
        tmp = sb("tmp", [P, NT, E], F32)
        hot = [sb(f"hot{k}", [P, NT, E], F32) for k in range(2)]
        eno = sb("eno", [P, NT, E], F32)
        top = sb("top", [P, 4, NT], F32)
        member = sb("member", [P, E, 2 * NT], F32)
        ranks = sb("ranks", [P, E, 2 * NT], F32)
        carry_mask = sb("carry_mask", [P, E, 2 * NT], F32)
        run = sb("run", [P, 6, E], F32)
        blocks_i = sb("blocks_i", [P, 2, E], I32)
        block_no = sb("block_no", [P, 1], F32)
        past = sb("past", [P, E], F32)
        eid_f = sb("eid_f", [P, 1], F32)
        eid_i = sb("eid_i", [P, 1], I32)

        consts_set = sem(f"r{L}_consts_set")
        w_in = sem(f"r{L}_w_in")
        var_ready = sem(f"r{L}_var_ready")
        dev_ready = sem(f"r{L}_dev_ready")
        dve_done = sem(f"r{L}_dve_done")
        turn = sem(f"r{L}_turn")
        xn_ready = sem(f"r{L}_xn_ready")
        xn_out = [sem(f"r{L}_xn_out{s}") for s in range(LOT)]
        x_turned = sem(f"r{L}_x_turned")
        xT_ready = sem(f"r{L}_xT_ready")
        h_summed = sem(f"r{L}_h_summed")
        rh_ready = sem(f"r{L}_rh_ready")
        l_summed = sem(f"r{L}_l_summed")
        l_ready = sem(f"r{L}_l_ready")
        exp_asked = sem(f"r{L}_exp_asked")
        exp_ready = sem(f"r{L}_exp_ready")
        counted = sem(f"r{L}_counted")
        summed = sem(f"r{L}_summed")
        eid_ready = sem(f"r{L}_eid_ready")
        eid_out = sem(f"r{L}_eid_out")
        eid_in = sem(f"r{L}_eid_in")

        RT, RH = 3, 2
        psT = [bank[r][:, 0:D].rearrange("p (k n) -> p k n", k=KD) for r in range(RT)]
        psH = [bank[3 + r][:, 0:P] for r in range(RH)]
        psL = [bank[5 + r][:, 0:E] for r in range(RH)]
        psC = bank[7]
        NW = 4 if hidden else 2
        H_LAG, LOGIT_LAG = 1, (3 if hidden else 2)

        with nc.Block() as block:

            @block.sync
            def _(sp):
                if hidden:
                    sp.dma_start(w1[:, :, :], a[m["router_w1"]].rearrange("(k p) h -> p k h", p=P)).then_inc(w_in, 16)
                    with nc.allow_non_contiguous_dma(reason="a bias of 128 features, one on each partition"):
                        sp.dma_start(b1[:, :], a[m["router_b1"]].rearrange("(p o) -> p o", o=1)).then_inc(w_in, 16)
                    sp.dma_start(w2[:, 0, :], a[m["router_w2"]]).then_inc(w_in, 16)
                else:
                    sp.dma_start(w2[:, :, :], a[m["router_w2"]].rearrange("(k p) e -> p k e", p=P)).then_inc(w_in, 16)
                sp.dma_start(b2[:, :], a[m["router_b2"]].rearrange("(o e) -> o e", o=1).to_broadcast([P, E])
                             ).then_inc(w_in, 16)
                with sp.Fori(0, NLOT) as i:
                    for s in range(LOT):
                        sp.wait_ge(xn_ready, i * LOT + (s + 1))
                        sp.dma_start(tile_rows(dram["xn"], i * LOT + s), xn[:, s, :]).then_inc(xn_out[s], 16)
                sp.wait_ge(eid_ready, 1)
                sp.dma_start(dram["eid"].rearrange("(p o) -> p o", o=1), eid_i[:, :]).then_inc(eid_out, 16)
                sp.wait_ge(eid_out, 16)
                sp.dma_start(eid[0:1, :], dram["eid"].rearrange("(o g) -> o g", o=1)).then_inc(eid_in, 16)
                sp.wait_ge(eid_in, 16)
                for s in range(LOT):
                    sp.wait_ge(xn_out[s], 16 * NLOT)

            @block.gpsimd
            def _(pool):
                nc.gpsimd.iota(eno[:, :, :], pattern=[[0, NT], [1, E]], base=-1000, channel_multiplier=0,
                               allow_small_or_imprecise_dtypes=True).then_inc(consts_set, 1)
                nc.gpsimd.iota(block_no[:, :], pattern=[[0, 1]], base=0, channel_multiplier=1,
                               allow_small_or_imprecise_dtypes=True).then_inc(consts_set, 1)

            @block.vector
            def _(dve):
                steps = Count()

                def link(ins):
                    ins.then_inc(dve_done, 1)
                    dve.wait_ge(dve_done, steps.next())

                norm_all(nc, dve, link, steps, turn, X, stats, moments, mr, var_ready, dev_ready)

                def norm(i, s):
                    after(dve, xn_out[s], i * 16)
                    after(dve, x_turned, i * LOT + (s + 1 - LOT))
                    dve.sem_inc(turn, 1)
                    nc.vector.tensor_scalar(xn[:, s, :], X[:, i * LOT + s, :], mr[:, bass.ds(i * LOT + s, 1), 0],
                                            mr[:, bass.ds(i * LOT + s, 1), 1], ALU.subtract,
                                            ALU.mult).then_inc(xn_ready, 1)

                def logit(i, s):
                    dve.wait_ge(l_summed, i * LOT + (s + 1))
                    dve.sem_inc(turn, 1)
                    nc.vector.tensor_tensor(logits[:, bass.ds(i * LOT + s, 1), :].rearrange("p a e -> p (a e)"),
                                            psL[s % LOT % RH], b2[:, :], ALU.add).then_inc(l_ready, 1)

                dve.wait_ge(w_in, 16 * NW)
                each_tile(dve, [(norm, 0), (logit, LOGIT_LAG + 1)])
                dve.wait_ge(l_ready, NT)
                dve.wait_ge(consts_set, 2)
                v = logits
                if m["softmax"]:
                    link(nc.vector.tensor_reduce(top[:, 0, :], logits[:, :, :], AX.X, ALU.max))
                    nc.vector.tensor_tensor(tmp[:, :, :], logits[:, :, :], widen(top[:, 0, :], E),
                                            ALU.subtract).then_inc(exp_asked, 1)
                    dve.wait_ge(exp_ready, 1)
                    link(nc.vector.tensor_reduce(top[:, 0, :], tmp[:, :, :], AX.X, ALU.add))
                    link(nc.vector.reciprocal(top[:, 1, :], top[:, 0, :]))
                    link(nc.vector.tensor_tensor(logits[:, :, :], tmp[:, :, :], widen(top[:, 1, :], E), ALU.mult))
                for k in range(2):
                    link(nc.vector.tensor_reduce(top[:, k, :], v[:, :, :], AX.X, ALU.max))
                    link(nc.vector.tensor_tensor(tmp[:, :, :], v[:, :, :], widen(top[:, k, :], E), ALU.is_equal))
                    link(nc.vector.tensor_tensor(tmp[:, :, :], tmp[:, :, :], eno[:, :, :], ALU.mult))
                    link(nc.vector.tensor_reduce(top[:, 2, :], tmp[:, :, :], AX.X, ALU.min))
                    link(nc.vector.tensor_tensor(hot[k][:, :, :], eno[:, :, :], widen(top[:, 2, :], E), ALU.is_equal))
                    if k == 0:
                        link(nc.vector.scalar_tensor_tensor(v[:, :, :], hot[0][:, :, :], -3.0e38, v[:, :, :],
                                                            ALU.mult, ALU.add))
                nc.vector.tensor_tensor(top[:, 2, :], top[:, 1, :], top[:, 0, :], ALU.subtract).then_inc(exp_asked, 1)
                dve.wait_ge(exp_ready, 2 if m["softmax"] else 1)
                link(nc.vector.tensor_scalar(top[:, 3, :], top[:, 2, :], 1.0, None, ALU.add))
                link(nc.vector.reciprocal(gates[:, 0, :], top[:, 3, :]))
                link(nc.vector.tensor_tensor(gates[:, 1, :], gates[:, 0, :], top[:, 2, :], ALU.mult))
                link(nc.vector.tensor_tensor(tmp[:, :, :], hot[0][:, :, :], widen(gates[:, 0, :], E), ALU.mult))
                link(nc.vector.tensor_tensor(gates_by[:, :, :], hot[1][:, :, :], widen(gates[:, 1, :], E), ALU.mult))
                link(nc.vector.tensor_tensor(gates_by[:, :, :], gates_by[:, :, :], tmp[:, :, :], ALU.add))
                for k in range(2):
                    link(nc.vector.tensor_copy(member[:, :, k * NT:(k + 1) * NT],
                                               hot[k][:, :, :].rearrange("p t e -> p e t")))
                link(nc.vector.tensor_reduce(run[:, 0, :], member[:, :, :], AX.X, ALU.add))
                dve.sem_inc(counted, 1)
                link(nc.vector.memset(carry_mask[:, :, :], 1.0))
                link(nc.vector.memset(carry_mask[:, :, 0], 0.0))
                dve.wait_ge(summed, 1)
                link(nc.vector.tensor_scalar(blocks_i[:, 0, :], psC[:, E:2 * E], float(P - 1), None, ALU.add))
                link(nc.vector.tensor_scalar(blocks_i[:, 1, :], blocks_i[:, 0, :], 7, None, ALU.arith_shift_right))
                link(nc.vector.tensor_copy(run[:, 1, :], blocks_i[:, 1, :]))
                link(nc.vector.tensor_tensor_scan(run[:, 2, :], ones[:, 0:E], run[:, 1, :], 0.0, ALU.mult, ALU.add))
                link(nc.vector.tensor_tensor(run[:, 3, :], run[:, 2, :], run[:, 1, :], ALU.subtract))
                link(nc.vector.scalar_tensor_tensor(run[:, 4, :], run[:, 3, :], float(P), psC[:, 0:E], ALU.mult, ALU.add))
                link(nc.vector.tensor_scalar(past[:, :], run[:, 2, :], block_no[:, :], None, ALU.is_le))
                link(nc.vector.tensor_reduce(eid_f[:, :], past[:, :], AX.X, ALU.add))
                nc.vector.tensor_scalar(eid_i[:, :], eid_f[:, :], float(E - 1), None, ALU.min).then_inc(eid_ready, 1)
                link(nc.vector.tensor_copy(run[:, 5, :], member[:, :, 0]))
                link(nc.vector.tensor_tensor(member[:, :, 0], member[:, :, 0], run[:, 4, :], ALU.add))
                link(nc.vector.tensor_tensor_scan(ranks[:, :, :].rearrange("p e t -> p (e t)"),
                                                  carry_mask[:, :, :].rearrange("p e t -> p (e t)"),
                                                  member[:, :, :].rearrange("p e t -> p (e t)"), 0.0,
                                                  ALU.mult, ALU.add))
                link(nc.vector.tensor_copy(member[:, :, 0], run[:, 5, :]))
                link(nc.vector.tensor_tensor(member[:, :, :], member[:, :, :], ranks[:, :, :], ALU.mult))
                link(nc.vector.tensor_reduce(ranks[:, 0, :], member[:, :, :].rearrange("p e t -> p t e"), AX.X, ALU.add))
                link(nc.vector.tensor_scalar(pos[:, :], ranks[:, 0, :], -1.0, None, ALU.add))

            @block.scalar
            def _(act):
                act.wait_ge(var_ready, 1)
                nc.scalar.activation(mr[:, :, 1], mr[:, :, 1], ACT.Sqrt).then_inc(dev_ready, 1)
                if hidden:
                    act.wait_ge(w_in, 16 * NW)

                def turned(i, s):
                    act.wait_ge(x_turned, i * LOT + (s + 1))
                    after(act, h_summed if hidden else l_summed, i * LOT + (s + 1 - LOT))
                    nc.scalar.activation(xT[:, s, :, :], psT[s % RT], ACT.Copy).then_inc(xT_ready, 1)

                def relu(i, s):
                    q = s % LOT
                    act.wait_ge(h_summed, i * LOT + (s + 1))
                    after(act, l_summed, i * LOT + (s + 1 - LOT))
                    nc.scalar.activation(rh[:, q, :], psH[q % RH], ACT.Relu, bias=b1[:, 0:1]).then_inc(rh_ready, 1)

                each_tile(act, [(turned, 0)] + [(relu, H_LAG)] * hidden)
                for n in range(2 if m["softmax"] else 1):
                    act.wait_ge(exp_asked, n + 1)
                    t = tmp[:, :, :] if n == 0 and m["softmax"] else top[:, 2, :]
                    nc.scalar.activation(t, t, ACT.Exp).then_inc(exp_ready, 1)

            @block.tensor
            def _(pe):
                pe.wait_ge(w_in, 16 * NW)

                def bank_free(sm, i, s, ring):
                    after(pe, sm, i * LOT + (s + 1 - s % LOT + before(s % LOT, ring)))

                def turn_x(i, s):
                    pe.wait_ge(xn_ready, i * LOT + (s + 1))
                    bank_free(xT_ready, i, s, RT)
                    for k in range(KD):
                        last = nc.tensor.transpose(psT[s % RT][:, k, :], xn[:, s, k * P:(k + 1) * P], ident[:, :])
                    last.then_inc(x_turned, 1)

                def sum_h(i, s):
                    q = s % LOT
                    pe.wait_ge(xT_ready, i * LOT + (s + 1))
                    bank_free(rh_ready, i, s, RH)
                    for k in range(KD):
                        last = nc.tensor.matmul(psH[q % RH], w1[:, k, :], xT[:, q, k, :], start=(k == 0),
                                                stop=(k == KD - 1))
                    last.then_inc(h_summed, 1)

                def sum_l(i, s):
                    q = s % LOT
                    pe.wait_ge(rh_ready if hidden else xT_ready, i * LOT + (s + 1))
                    bank_free(l_ready, i, s, RH)
                    if hidden:
                        nc.tensor.matmul(psL[q % RH], rh[:, q, :], w2[:, 0, :], start=True,
                                         stop=True).then_inc(l_summed, 1)
                    else:
                        for k in range(KD):
                            last = nc.tensor.matmul(psL[q % RH], xT[:, q, k, :], w2[:, k, :], start=(k == 0),
                                                    stop=(k == KD - 1))
                        last.then_inc(l_summed, 1)

                each_tile(pe, [(turn_x, 0)] + [(sum_h, H_LAG)] * hidden + [(sum_l, LOGIT_LAG)])
                pe.wait_ge(counted, 1)
                nc.tensor.matmul(psC[:, 0:E], tri[:, :], run[:, 0, :], start=True, stop=True)
                nc.tensor.matmul(psC[:, E:2 * E], ones[:, :], run[:, 0, :], start=True,
                                 stop=True).then_inc(summed, 1)


def experts(nc, sem, bank, c, a, dram, layer, m):
    E, widths = m["E"], m["widths"]
    NL = len(widths) - 1
    L = layer
    BLOCKS = m["blocks"]
    BR = m["ring"]
    with ExitStack() as ctx, stage(nc, sem) as (sem, pool_sem):
        sb = lambda n, s, d: ctx.enter_context(nc.sbuf_tensor(f"e{L}_{n}", s, d))
        ident, pos, eid = c["ident"], m["pos"], m["eid"]
        W = [sb(f"W{n}", [P, E, widths[n] // P, widths[n + 1]], F32) for n in range(NL)]
        B = [sb(f"B{n}", [P, E, widths[n + 1] // P], F32) for n in range(NL - 1)]
        NB = [E * widths[n + 1] // P for n in range(NL - 1)]
        brow = [sb(f"brow{n}", [NB[n], P], F32) for n in range(NL - 1)]
        xr = sb("xr", [P, max(LOT, 2 * BR), D], F32)
        pos_ring = sb("pos_ring", [P, LOT, 2], I32)
        xb, y = xr[:, 0:BR, :], xr[:, BR:2 * BR, :]
        widest = max(widths)
        hT = sb("hT", [P, BR, widest // P, P], F32)
        z = sb("z", [P, BR, max(widths[1:-1])], F32)

        w_in = [sem(f"e{L}_w_in{n}") for n in range(NL)]
        b_in = sem(f"e{L}_b_in")
        b_turned = sem(f"e{L}_b_turned")
        b_ready = sem(f"e{L}_b_ready")
        xr_in = [sem(f"e{L}_xr_in{s}") for s in range(LOT)]
        pos_ready = sem(f"e{L}_pos_ready")
        sent = [pool_sem(f"e{L}_sent{s}") for s in range(LOT)]
        all_sent = sem(f"e{L}_all_sent")
        xb_in = [sem(f"e{L}_xb_in{s}") for s in range(BR)]
        turned = sem(f"e{L}_turned")
        hT_ready = sem(f"e{L}_hT_ready")
        summed = sem(f"e{L}_summed")
        z_ready = sem(f"e{L}_z_ready")
        y_out = [sem(f"e{L}_y_out{s}") for s in range(BR)]
        turn = sem(f"e{L}_turn")
        psT = [bank[s] for s in range(BR)]
        psZ = [bank[BR + s] for s in range(BR)]
        psB = [psZ[n] for n in range(NL - 1)]
        ITER = BLOCKS // BR
        UNITS = [(n, s) for n in range(NL) for s in range(BR)]
        U = len(UNITS)
        AHEAD = m["ahead"]

        with nc.Block() as block:

            @block.sync
            def _(sp):
                for n in range(NL - 1):
                    sp.dma_start(brow[n][:, :], a[m["b"][n]].rearrange("e (k p) -> (e k) p", p=P)).then_inc(b_in, 16)
                with sp.Fori(0, NLOT) as i:
                    for s in range(LOT):
                        sp.wait_ge(pos_ready, i * LOT + (s + 1))
                        sp.dma_start(xr[:, s, :], tile_rows(dram["xn"], i * LOT + s)).then_inc(xr_in[s], 16)
                sp.wait_ge(all_sent, 1)

                def load(b, s):
                    sp.dma_start(xb[:, s, :], tile_rows(dram["sent"], b)).then_inc(xb_in[s], 16)

                def store(i, s):
                    sp.wait_ge(z_ready, i * U + ((NL - 1) * BR + s + 1))
                    sp.dma_start(tile_rows(dram["made"], i * BR + s), y[:, s, :]).then_inc(y_out[s], 16)

                for s in range(BR):
                    load(s, s)
                with sp.Fori(0, ITER - 1) as i:
                    for s in range(BR):
                        sp.wait_ge(turned, i * U + (s + 1))
                        load(i * BR + (BR + s), s)
                    for s in range(BR):
                        store(i, s)
                for s in range(BR):
                    store(ITER - 1, s)
                for s in range(BR):
                    sp.wait_ge(y_out[s], 16 * ITER)

            @block.gpsimd
            def _(pool):
                with pool.Fori(0, NLOT) as i:
                    for s in range(LOT):
                        pool.wait_ge(xr_in[s], i * 16 + 16)
                        pool.sem_inc(turn, 1)
                        for k in range(2):
                            nc.gpsimd.indirect_dma_start(
                                dram["sent"][:, :], bass.IndirectOffsetOnAxis(pos_ring[:, s, k:k + 1], 0),
                                xr[:, s, :], None).then_inc(sent[s], 16)
                for s in range(LOT):
                    pool.wait_ge(sent[s], 32 * NLOT)
                pool.sem_inc(all_sent, 1)

            @block.vector
            def _(dve):
                pos_by_tile = pos[:, :].rearrange("p (k t) -> p t k", k=2)

                def places(i, first):
                    for s in range(LOT):
                        if not first:
                            dve.wait_ge(sent[s], i * 32)
                            dve.sem_inc(turn, 1)
                        nc.vector.tensor_copy(pos_ring[:, s, :], pos_by_tile[:, bass.ds(i * LOT + s, 1), :].rearrange(
                            "p a k -> p (a k)")).then_inc(pos_ready, 1)
                peeled(dve, NLOT, places)

                def body(i, first):
                    for u, (n, s) in enumerate(UNITS):
                        dve.wait_ge(summed, i * U + (u + 1))
                        if n == NL - 1 and not first:
                            dve.wait_ge(y_out[s], i * 16)
                        to = y[:, s, :] if n == NL - 1 else z[:, s, 0:widths[n + 1]]
                        nc.vector.tensor_copy(to, psZ[s][:, 0:widths[n + 1]]).then_inc(z_ready, 1)
                peeled(dve, ITER, body)

            @block.scalar
            def _(act):
                for n in range(NL):
                    act.dma_start(W[n][:, :, :, :], a[m["w"][n]].rearrange("e (k p) f -> p e k f", p=P)
                                  ).then_inc(w_in[n], 16)
                for n in range(NL - 1):
                    act.wait_ge(b_turned, n + 1)
                    nc.scalar.activation(B[n][:, :, :].rearrange("p e k -> p (e k)"), psB[n][:, 0:NB[n]],
                                         ACT.Copy).then_inc(b_ready, 1)
                act.wait_ge(b_ready, NL - 1)

                def body(i, first):
                    es = []
                    for u, (n, s) in enumerate(UNITS):
                        act.wait_ge(turned, i * U + (u + 1))
                        if n == 0:
                            if not first:
                                act.wait_ge(summed, i * U + (u + 1 - BR))
                            nc.scalar.activation(hT[:, s, 0:KD, :], psT[s][:, 0:D].rearrange(
                                "p (k n) -> p k n", k=KD), ACT.Copy).then_inc(hT_ready, 1)
                            es.append(act.value_load(eid[0:1, bass.ds(i * BR + s, 1)], min_val=0, max_val=E - 1))
                        else:
                            act.sem_inc(turn, 1)
                            for k in range(widths[n] // P):
                                last = nc.scalar.activation(
                                    hT[:, s, k, :], psT[s][:, k * P:(k + 1) * P], ACT.Relu,
                                    bias=B[n - 1][:, bass.ds(es[s], 1), k])
                            last.then_inc(hT_ready, 1)
                peeled(act, ITER, body)

            @block.tensor
            def _(pe):
                pe.wait_ge(b_in, 16 * (NL - 1))
                for n in range(NL - 1):
                    nc.tensor.transpose(psB[n][:, 0:NB[n]], brow[n][:, :],
                                        ident[0:NB[n], 0:NB[n]]).then_inc(b_turned, 1)
                for n in range(NL):
                    pe.wait_ge(w_in[n], 16)

                pe.wait_ge(b_ready, NL - 1)

                def expert_of(i, s):
                    return pe.value_load(eid[0:1, bass.ds(i * BR + s, 1)], min_val=0, max_val=E - 1)

                def turn_rows(i, u):
                    n, s = UNITS[u]
                    if n == 0:
                        pe.wait_ge(xb_in[s], i * 16 + 16)
                    else:
                        pe.wait_ge(z_ready, i * U + (u + 1 - BR))
                    src = xb[:, s, :] if n == 0 else z[:, s, :]
                    for k in range(widths[n] // P):
                        last = nc.tensor.transpose(psT[s][:, k * P:(k + 1) * P], src[:, k * P:(k + 1) * P],
                                                   ident[:, :])
                    last.then_inc(turned, 1)

                def product(i, u, expert, first=False):
                    n, s = UNITS[u]
                    pe.wait_ge(hT_ready, i * U + (u + 1))
                    if n == 0 and not first:
                        pe.wait_ge(z_ready, i * U + (u + 1 - BR))
                    K = widths[n] // P
                    for k in range(K):
                        last = nc.tensor.matmul(psZ[s][:, 0:widths[n + 1]], hT[:, s, k, :],
                                                W[n][:, bass.ds(expert, 1), k, :].rearrange("p a f -> p (a f)"),
                                                start=(k == 0), stop=(k == K - 1))
                    last.then_inc(summed, 1)

                def body(i, first):
                    es = []
                    for u in range(U):
                        turn_rows(i, u)
                        if u < BR:
                            es.append(expert_of(i, u))
                        if u >= AHEAD:
                            product(i, u - AHEAD, es[UNITS[u - AHEAD][1]], first)
                        elif not first:
                            product(i, u - AHEAD, expert_of(i, u - AHEAD))
                peeled(pe, ITER, body)
                for u in range(AHEAD):
                    product(ITER, u - AHEAD, expert_of(ITER, u - AHEAD))


def combine(nc, sem, bank, c, a, dram, layer, m, out=None):
    E = m["E"]
    L = layer
    final = out is not None
    with ExitStack() as ctx, stage(nc, sem) as (sem, pool_sem):
        sb = lambda n, s, d: ctx.enter_context(nc.sbuf_tensor(f"c{L}_{n}", s, d))
        X, ident = c["X"], c["ident"]
        gates, gates_by, pos = m["gates"], m["gates_by"], m["pos"]
        pos_ring = sb("pos_ring", [P, LOT, 2], I32)
        yr = sb("yr", [P, LOT, 2, D], F32)
        bl = sb("bl", [E, D], F32)
        gT = sb("gT", [E, LOT, P], F32)
        gs = sb("gs", [P, LOT, E], F32)
        if final:
            y = sb("y", [P, LOT, D], F32)
            gamma = sb("gamma", [P, D], F32)
            beta = sb("beta", [P, D], F32)
            stats = sb("stats", [P, LOT, 6], F32)
            moments = sb("moments", [P, LOT, 2], F32)
            rstd = sb("rstd", [P, LOT], F32)
        w_in = sem(f"c{L}_w_in")
        xn_in = sem(f"c{L}_xn_in")
        pos_ready = sem(f"c{L}_pos_ready")
        rows_in = [pool_sem(f"c{L}_rows_in{s}") for s in range(LOT)]
        gs_ready = sem(f"c{L}_gs_ready")
        turned = sem(f"c{L}_turned")
        gT_ready = sem(f"c{L}_gT_ready")
        summed = sem(f"c{L}_summed")
        added = sem(f"c{L}_added")
        var_ready = sem(f"c{L}_var_ready")
        dev_ready = sem(f"c{L}_dev_ready")
        dve_done = sem(f"c{L}_dve_done")
        lot_done = sem(f"c{L}_lot_done")
        stored = sem(f"c{L}_stored")
        turn = sem(f"c{L}_turn")
        psG = [bank[r] for r in range(2)]
        psB = [bank[2 + r][:, 0:D] for r in range(2)]

        with nc.Block() as block:

            @block.sync
            def _(sp):
                sp.dma_start(bl[:, :], a[m["b_last"]]).then_inc(w_in, 16)
                if final:
                    for t, name in ((gamma, "L1_ffn_gamma"), (beta, "L1_ffn_beta")):
                        sp.dma_start(t[:, :], a[name].rearrange("(o d) -> o d", o=1).to_broadcast([P, D])
                                     ).then_inc(w_in, 16)

                    def body(i, first):
                        if not first:
                            sp.wait_ge(lot_done, i * 1)
                        sp.dma_start(y[:, :, :], dram["xn"][bass.ds(i * (LOT * P), LOT * P), :].rearrange(
                            "(t p) d -> p t d", p=P)).then_inc(xn_in, 16)
                        if not first:
                            sp.dma_start(out[bass.ds((i - 1) * (LOT * P), LOT * P), :].rearrange(
                                "(t p) d -> p t d", p=P), X[:, bass.ds((i - 1) * LOT, LOT), :]).then_inc(stored, 16)
                    peeled(sp, NLOT, body)
                    sp.wait_ge(lot_done, NLOT)
                    start = (NT - LOT) * P
                    full = (NT - 1) * P
                    sp.dma_start(out[start:full, :].rearrange("(t p) d -> p t d", p=P),
                                 X[:, NT - LOT:NT - 1, :]).then_inc(stored, 16)
                    sp.dma_start(out[full:N, :], X[0:LAST, NT - 1, :]).then_inc(stored, 16)
                    sp.wait_ge(stored, 16 * (NLOT + 1))

            @block.gpsimd
            def _(pool):
                with pool.Fori(0, NLOT) as i:
                    for s in range(LOT):
                        pool.wait_ge(pos_ready, i * LOT + (s + 1))
                        pool.sem_inc(turn, 1)
                        for k in range(2):
                            nc.gpsimd.indirect_dma_start(
                                yr[:, s, k, :], None, dram["made"][:, :],
                                bass.IndirectOffsetOnAxis(pos_ring[:, s, k:k + 1], 0)).then_inc(rows_in[s], 16)

            @block.vector
            def _(dve):
                steps = Count()
                pos_by_tile = pos[:, :].rearrange("p (k t) -> p t k", k=2)

                def link(ins):
                    ins.then_inc(dve_done, 1)
                    dve.wait_ge(dve_done, steps.next())

                def place(t, s):
                    nc.vector.tensor_copy(pos_ring[:, s, :], pos_by_tile[:, bass.ds(t, 1), :].rearrange(
                        "p a k -> p (a k)")).then_inc(pos_ready, 1)

                for s in range(LOT):
                    place(s, s)
                if final:
                    dve.wait_ge(w_in, 48)

                def body(i, first, last_turn):
                    if final:
                        dve.wait_ge(xn_in, i * 16 + 16)
                    for s in range(LOT):
                        t = i * LOT + s
                        x = y[:, s, :] if final else X[:, bass.ds(t, 1), :].rearrange("p a d -> p (a d)")
                        dve.wait_ge(rows_in[s], i * 32 + 32)
                        dve.sem_inc(turn, 1)
                        for k in range(2):
                            link(nc.vector.scalar_tensor_tensor(x, yr[:, s, k, :], gates[:, k, bass.ds(t, 1)], x,
                                                                ALU.mult, ALU.add))
                            dve.sem_inc(turn, 1)
                        if not last_turn:
                            place(t + LOT, s)
                        dve.wait_ge(summed, t + 1)
                        nc.vector.tensor_tensor(x, psB[s % 2], x, ALU.add).then_inc(added, 1)
                    if final:
                        dve.wait_ge(added, i * LOT + LOT)
                        for s in range(LOT):
                            ins = nc.vector.bn_stats(stats[:, s, :], y[:, s, :])
                        link(ins)
                        dve.sem_inc(turn, 1)
                        for s in range(LOT):
                            ins = nc.vector.bn_aggr(moments[:, s, :], stats[:, s, :])
                        link(ins)
                        nc.vector.tensor_scalar(rstd[:, :], moments[:, :, 1], EPS, None,
                                                ALU.add).then_inc(var_ready, 1)
                        dve.wait_ge(dev_ready, i * 1 + 1)
                        link(nc.vector.reciprocal(rstd[:, :], rstd[:, :]))
                        for s in range(LOT):
                            ins = nc.vector.tensor_scalar(y[:, s, :], y[:, s, :], moments[:, s, 0:1],
                                                          rstd[:, s:s + 1], ALU.subtract, ALU.mult)
                        link(ins)
                        link(nc.vector.tensor_tensor(y[:, :, :], y[:, :, :], spread(gamma[:, :], LOT), ALU.mult))
                        link(nc.vector.tensor_tensor(y[:, :, :], y[:, :, :], spread(beta[:, :], LOT), ALU.add))
                        dve.sem_inc(turn, 1)
                        xs = X[:, bass.ds(i * LOT, LOT), :]
                        nc.vector.tensor_tensor(xs, y[:, :, :], xs, ALU.add).then_inc(lot_done, 1)

                PER = 2 * LOT + (6 if final else 0)
                steps.enter(0, PER)
                body(0, True, False)
                steps.leave(1)
                with dve.Fori(1, NLOT - 1) as i:
                    steps.enter(i, PER, 1)
                    body(i, False, False)
                steps.leave(NLOT - 2)
                body(NLOT - 1, False, True)

            @block.scalar
            def _(act):
                def body(i, first):
                    nc.scalar.activation(gs[:, :, :], gates_by[:, bass.ds(i * LOT, LOT), :],
                                         ACT.Copy).then_inc(gs_ready, 1)
                    for s in range(LOT):
                        act.wait_ge(turned, i * LOT + (s + 1))
                        if not first:
                            act.wait_ge(summed, i * LOT + (s + 1 - LOT))
                        nc.scalar.activation(gT[:, s, :], psG[s % 2][0:E, 0:P], ACT.Copy).then_inc(gT_ready, 1)
                    if final:
                        act.wait_ge(var_ready, i * 1 + 1)
                        nc.scalar.activation(rstd[:, :], rstd[:, :], ACT.Sqrt).then_inc(dev_ready, 1)
                peeled(act, NLOT, body)

            @block.tensor
            def _(pe):
                pe.wait_ge(w_in, 48 if final else 16)

                def body(i, first):
                    pe.wait_ge(gs_ready, i * 1 + 1)
                    for s in range(LOT):
                        q = before(s, 2)
                        if q >= 0 or not first:
                            pe.wait_ge(gT_ready, i * LOT + (q + 1))
                        nc.tensor.transpose(psG[s % 2][0:E, 0:P], gs[:, s, :], ident[:, :]).then_inc(turned, 1)
                        pe.wait_ge(gT_ready, i * LOT + (s + 1))
                        if q >= 0 or not first:
                            pe.wait_ge(added, i * LOT + (q + 1))
                        nc.tensor.matmul(psB[s % 2], gT[:, s, :], bl[:, :], start=True, stop=True).then_inc(summed, 1)
                peeled(pe, NLOT, body)


def project_heads(nc, sem, bank, c, a, dram):
    with ExitStack() as ctx, stage(nc, sem) as (sem, pool_sem):
        sb = lambda n, s, d: ctx.enter_context(nc.sbuf_tensor(f"h_{n}", s, d))
        X, ident, ones = c["X"], c["ident"], c["ones"]
        W = sb("W", [HD, 2, D], F32)
        arow = sb("arow", [4, HD], F32)
        aT = sb("aT", [HD, 4], F32)
        brow = sb("brow", [2, HD], F32)
        bT = sb("bT", [HD, 2], F32)
        WIDE = ROW1 + 2
        WX = sb("WX", [P, KD, WIDE], F32)
        bias = sb("bias", [1, WIDE], F32)
        stats = sb("stats", [P, LOT, 6], F32)
        moments = sb("moments", [P, LOT, 2], F32)
        mr = sb("mr", [P, NT, 2], F32)
        xn = sb("xn", [P, LOT, D], F32)
        xT = sb("xT", [P, LOT, KD, P], F32)
        row = sb("row", [P, LOT, ROW1], F32)
        ss = sb("ss", [2, LOT, P], F32)
        w_in = sem("h_w_in")
        b_set = sem("h_b_set")
        a_turned = sem("h_a_turned")
        b_turned = sem("h_b_turned")
        w_turned = sem("h_w_turned")
        a_ready = sem("h_a_ready")
        ab_summed = sem("h_ab_summed")
        w_ready = sem("h_w_ready")
        dve_done = sem("h_dve_done")
        turn = sem("h_turn")
        var_ready = sem("h_var_ready")
        dev_ready = sem("h_dev_ready")
        xn_ready = sem("h_xn_ready")
        x_turned = sem("h_x_turned")
        xT_ready = sem("h_xT_ready")
        summed = sem("h_summed")
        row_ready = sem("h_row_ready")
        s_summed = sem("h_s_summed")
        ss_ready = sem("h_ss_ready")
        row_out = [sem(f"h_row_out{s}") for s in range(LOT)]
        psT = [bank[r][:, 0:D].rearrange("p (k n) -> p k n", k=KD) for r in range(3)]
        psR = [bank[3 + r][:, 0:WIDE] for r in range(2)]
        psS = [bank[5 + r][0:2, 0:P] for r in range(2)]
        psX = bank[7]

        with nc.Block() as block:

            @block.sync
            def _(sp):
                sp.dma_start(W[:, :, :], a["L1_gnn_W"].rearrange("h d f -> d h f")).then_inc(w_in, 16)
                sp.dma_start(arow[:, :], a["L1_gnn_a"].rearrange("h (s d) -> (h s) d", s=2)).then_inc(w_in, 16)
                sp.dma_start(brow[:, :], a["L1_gnn_b"]).then_inc(w_in, 16)
                sp.wait_ge(b_set, 1)
                for h in range(2):
                    sp.dma_start(bias[0:1, h * HW:h * HW + HD], a["L1_gnn_b"][h:h + 1, :]).then_inc(w_in, 16)

                def body(i, first):
                    for s in range(LOT):
                        sp.wait_ge(row_ready, i * LOT + (s + 1))
                        sp.dma_start(tile_rows(dram["table1"], i * LOT + s), row[:, s, :]).then_inc(row_out[s], 16)
                        sp.wait_ge(ss_ready, i * LOT + (s + 1))
                        sp.dma_start(dram["source_score"][bass.ds(i * LOT + s, 1), :].rearrange(
                            "t (h n) -> (t h) n", h=2), ss[:, s, :]).then_inc(row_out[s], 16)
                peeled(sp, NLOT, body)
                for s in range(LOT):
                    sp.wait_ge(row_out[s], 32 * NLOT)

            @block.vector
            def _(dve):
                steps = Count()

                def link(ins):
                    ins.then_inc(dve_done, 1)
                    dve.wait_ge(dve_done, steps.next())

                nc.vector.memset(bias[:, :], 1.0).then_inc(b_set, 1)
                link(nc.vector.memset(WX[:, :, :], 0.0))
                dve.wait_ge(a_turned, 1)
                nc.vector.tensor_copy(aT[:, :], psX[:, 0:4]).then_inc(a_ready, 1)
                dve.wait_ge(b_turned, 1)
                nc.vector.tensor_copy(bT[:, :], psX[:, 0:2]).then_inc(a_ready, 1)
                dve.wait_ge(w_in, 16 * 5)
                for h in range(2):
                    dve.wait_ge(ab_summed, h + 1)
                    for which, col in ((1, ROW1 - 2), (0, ROW1)):
                        nc.vector.tensor_copy(bias[0:1, col + h:col + h + 1], psX[0:1, which:which + 1])
                        for k in range(KD):
                            last = nc.vector.tensor_copy(WX[:, k, col + h:col + h + 1],
                                                         psX[:, 16 * (k + 1) + which:16 * (k + 1) + which + 1])
                    last.then_inc(w_ready, 1)
                for h in range(2):
                    dve.wait_ge(w_turned, h + 1)
                    nc.vector.tensor_copy(WX[:, :, h * HW:h * HW + HD], psX[:, 0:D].rearrange(
                        "p (k n) -> p k n", k=KD)).then_inc(w_ready, 1)
                norm_all(nc, dve, link, steps, turn, X, stats, moments, mr, var_ready, dev_ready)

                def norm(i, s):
                    after(dve, x_turned, i * LOT + (s + 1 - LOT))
                    dve.sem_inc(turn, 1)
                    nc.vector.tensor_scalar(xn[:, s, :], X[:, i * LOT + s, :], mr[:, bass.ds(i * LOT + s, 1), 0],
                                            mr[:, bass.ds(i * LOT + s, 1), 1], ALU.subtract,
                                            ALU.mult).then_inc(xn_ready, 1)

                def source_scores(i, s):
                    q = s % LOT
                    dve.wait_ge(s_summed, i * LOT + (s + 1))
                    after(dve, row_out[q], (i - 1 if s < 0 else i) * 32)
                    nc.vector.tensor_copy(ss[:, q, :], psS[q % 2]).then_inc(ss_ready, 1)

                each_tile(dve, [(norm, 0), (source_scores, 3)])

            @block.scalar
            def _(act):
                act.wait_ge(var_ready, 1)
                nc.scalar.activation(mr[:, :, 1], mr[:, :, 1], ACT.Sqrt).then_inc(dev_ready, 1)

                def turned(i, s):
                    act.wait_ge(x_turned, i * LOT + (s + 1))
                    after(act, s_summed, i * LOT + (s + 1 - LOT))
                    nc.scalar.activation(xT[:, s, :, :], psT[s % 3], ACT.Copy).then_inc(xT_ready, 1)

                def rows(i, s):
                    q = s % LOT
                    act.wait_ge(summed, i * LOT + (s + 1))
                    after(act, row_out[q], (i - 1 if s < 0 else i) * 32)
                    nc.scalar.activation(row[:, q, :], psR[q % 2][:, 0:ROW1], ACT.Copy).then_inc(row_ready, 1)

                each_tile(act, [(turned, 0), (rows, 1)])

            @block.tensor
            def _(pe):
                pe.wait_ge(w_in, 16 * 5)
                nc.tensor.transpose(psX[:, 0:4], arow[:, :], ident[0:4, 0:4]).then_inc(a_turned, 1)
                pe.wait_ge(a_ready, 1)
                nc.tensor.transpose(psX[:, 0:2], brow[:, :], ident[0:2, 0:2]).then_inc(b_turned, 1)
                pe.wait_ge(a_ready, 2)
                for h in range(2):
                    if h:
                        pe.wait_ge(w_ready, h)
                    nc.tensor.matmul(psX[0:1, 0:2], bT[:, h:h + 1], aT[:, 2 * h:2 * h + 2], start=True, stop=True)
                    for k in range(KD):
                        last = nc.tensor.matmul(psX[:, 16 * (k + 1):16 * (k + 1) + 2], W[:, h, k * P:(k + 1) * P],
                                                aT[:, 2 * h:2 * h + 2], start=True, stop=True)
                    last.then_inc(ab_summed, 1)
                for h in range(2):
                    pe.wait_ge(w_ready, 2 + h)
                    for k in range(KD):
                        last = nc.tensor.transpose(psX[:, k * P:(k + 1) * P], W[:, h, k * P:(k + 1) * P], ident[:, :])
                    last.then_inc(w_turned, 1)
                pe.wait_ge(w_ready, 4)

                def bank_free(sm, i, s, ring):
                    after(pe, sm, i * LOT + (s + 1 - s % LOT + before(s % LOT, ring)))

                def turn_x(i, s):
                    pe.wait_ge(xn_ready, i * LOT + (s + 1))
                    bank_free(xT_ready, i, s, 3)
                    for k in range(KD):
                        last = nc.tensor.transpose(psT[s % 3][:, k, :], xn[:, s, k * P:(k + 1) * P], ident[:, :])
                    last.then_inc(x_turned, 1)

                def project(i, s):
                    q = s % LOT
                    pe.wait_ge(xT_ready, i * LOT + (s + 1))
                    bank_free(row_ready, i, s, 2)
                    for k in range(KD):
                        nc.tensor.matmul(psR[q % 2], xT[:, q, k, :], WX[:, k, :], start=(k == 0), stop=False)
                    nc.tensor.matmul(psR[q % 2], ones[0:1, :], bias[0:1, :], start=False,
                                     stop=True).then_inc(summed, 1)
                    bank_free(ss_ready, i, s, 2)
                    for k in range(KD):
                        nc.tensor.matmul(psS[q % 2], WX[:, k, ROW1:WIDE], xT[:, q, k, :], start=(k == 0), stop=False)
                    nc.tensor.matmul(psS[q % 2], bias[0:1, ROW1:WIDE], ones[0:1, :], start=False,
                                     stop=True).then_inc(s_summed, 1)

                each_tile(pe, [(turn_x, 0), (project, 2)])


def gather_heads(nc, sem, bank, c, dram, acc):
    with ExitStack() as ctx, stage(nc, sem) as (sem, pool_sem):
        sb = lambda n, s, d: ctx.enter_context(nc.sbuf_tensor(f"g_{n}", s, d))
        iota, tid = c["iota"], c["tid"]
        rec = sb("rec", [P, RING, GB, REC], I32)
        rec_f = rec[:, :, :, :].bitcast(F32)
        rows = sb("rows", [P, RING, GB, ROW1], F32)
        spot = sb("spot", [P, RING, GB, P], F32)
        scaled = sb("scaled", [P, RING, GB, 2, P], F32)
        ss = sb("ss", [P, RING, 2, P], F32)
        picked = sb("picked", [P, GB, 2, P], F32)
        own = sb("own", [P, RING, GB, 2], F32)
        score = sb("score", [P, RING, GB, 2], F32)
        leaky = sb("leaky", [P, RING, GB, 2], F32)
        e_ = sb("e", [P, RING, GB, 2], F32)
        last_rows = sb("last_rows", [P, 1], F32)
        rec_in = [sem(f"g_rec_in{k}") for k in range(RING)]
        ss_in = [sem(f"g_ss_in{k}") for k in range(RING)]
        rows_in = [pool_sem(f"g_rows_in{k}") for k in range(RING)]
        pad_set = sem("g_pad_set")
        acc_set = sem("g_acc_set")
        spot_ready = sem("g_spot_ready")
        own_ready = sem("g_own_ready")
        score_ready = sem("g_score_ready")
        leaky_ready = sem("g_leaky_ready")
        e_ready = sem("g_e_ready")
        scaled_ready = sem("g_scaled_ready")
        summed = sem("g_summed")
        added = sem("g_added")
        turn = sem("g_turn")
        SCORE_LAG, ADD_LAG = 2, 5

        with nc.Block() as block:

            @block.sync
            def _(sp):
                def load(i, k, first):
                    if not first:
                        sp.wait_ge(summed, i * RING + (k + 1 - RING))
                    sp.dma_start(rec[:, k, :, :].rearrange("p e c -> p (e c)"),
                                 dram["sorted_edges"][bass.ds((i * RING + k) * GROUP, GROUP), :].rearrange(
                                     "(p e) c -> p (e c)", p=P)).then_inc(rec_in[k], 16)
                    t = sp.value_load(tid[0:1, bass.ds(i * RING + k, 1)], min_val=0, max_val=NT - 1)
                    sp.dma_start(ss[:, k, :, :].rearrange("p h n -> p (h n)"),
                                 dram["source_score"][bass.ds(t, 1), :].to_broadcast([P, 2 * P])
                                 ).then_inc(ss_in[k], 16)
                each_group(sp, load)

            @block.gpsimd
            def _(pool):
                nc.gpsimd.memset(last_rows[:, :], 1.0).then_inc(pad_set, 1)
                pool.wait_ge(pad_set, 1)
                nc.gpsimd.affine_select(out=last_rows[:, :], in_=last_rows[:, :], compare_op=ALU.is_ge, fill=0.0,
                                        base=-LAST, pattern=[[0, 1]], channel_multiplier=1).then_inc(pad_set, 1)

                def gather(i, k, first):
                    pool.wait_ge(rec_in[k], i * 16 + 16)
                    pool.sem_inc(turn, 1)
                    for e in range(GB):
                        nc.gpsimd.indirect_dma_start(
                            rows[:, k, e, :], None, dram["table1"][:, :],
                            bass.IndirectOffsetOnAxis(rec[:, k, e, 2:3], 0)).then_inc(rows_in[k], 16)
                each_group(pool, gather)

            @block.vector
            def _(dve):
                nc.vector.memset(acc[:, :, :], 0.0).then_inc(acc_set, 1)
                dve.wait_ge(pad_set, 2)
                dve.wait_ge(acc_set, 1)
                for h in range(2):
                    nc.vector.tensor_copy(acc[:, NT - 1, h * HW + HD:h * HW + HW],
                                          last_rows[:, :]).then_inc(acc_set, 1)
                dve.wait_ge(acc_set, 3)

                def build(i, k):
                    dve.wait_ge(rec_in[k], i * 16 + 16)
                    for e in range(GB):
                        last = nc.vector.tensor_scalar(spot[:, k, e, :], iota[:, :], rec_f[:, k, e, 0:1], None,
                                                       ALU.is_equal)
                    last.then_inc(spot_ready, 1)

                def pick(i, k, very_first):
                    dve.wait_ge(ss_in[k], i * 16 + 16)
                    if not very_first:
                        dve.wait_ge(own_ready, i * RING + k)
                    for e in range(GB):
                        for h in range(2):
                            last = nc.vector.scalar_tensor_tensor(picked[:, e, h, :], iota[:, :],
                                                                  rec_f[:, k, e, 0:1], ss[:, k, h, :], ALU.is_equal,
                                                                  ALU.mult, accum_out=own[:, k, e, h:h + 1])
                    last.then_inc(own_ready, 1)

                def rate(i, k):
                    q = k % RING
                    dve.wait_ge(own_ready, i * RING + (k + 1))
                    dve.wait_ge(rows_in[q], (i + (0 if k < 0 else 1)) * (16 * GB))
                    nc.vector.tensor_tensor(score[:, q, :, :], own[:, q, :, :],
                                            rows[:, q, :, ROW1 - 2:ROW1], ALU.add).then_inc(score_ready, 1)

                def leak(i, k):
                    q = k % RING
                    dve.wait_ge(score_ready, i * RING + (k + 1))
                    nc.vector.scalar_tensor_tensor(leaky[:, q, :, :], score[:, q, :, :], SLOPE, score[:, q, :, :],
                                                   ALU.mult, ALU.max).then_inc(leaky_ready, 1)

                def add(i, k, very_first=False):
                    dve.wait_ge(summed, i * RING + (k + 1))
                    if not very_first:
                        dve.wait_ge(added, i * RING + k)
                    dve.sem_inc(turn, 1)
                    t = dve.value_load(tid[0:1, bass.ds(i * RING + k, 1)], min_val=0, max_val=NT - 1)
                    at = acc[:, bass.ds(t, 1), :].rearrange("p a d -> p (a d)")
                    nc.vector.tensor_tensor(at, at, bank[k % RING][:, 0:2 * HW], ALU.add).then_inc(added, 1)

                def step(i, k, first):
                    scored = not first or k >= SCORE_LAG
                    build(i, k)
                    if scored:
                        rate(i, k - SCORE_LAG)
                    pick(i, k, first and k == 0)
                    if scored:
                        leak(i, k - SCORE_LAG)
                    if not first or k >= ADD_LAG:
                        add(i, k - ADD_LAG, first and k == ADD_LAG)
                each_group(dve, step)
                done = NGROUP % RING
                for k in range(done - SCORE_LAG, done):
                    rate(NGROUP // RING, k)
                    leak(NGROUP // RING, k)
                for k in range(done - ADD_LAG, done):
                    add(NGROUP // RING, k)

            @block.scalar
            def _(act):
                def scale(i, k, first):
                    act.wait_ge(leaky_ready, i * RING + (k + 1))
                    nc.scalar.activation(e_[:, k, :, :], leaky[:, k, :, :], ACT.Exp, scale=-1.0).then_inc(e_ready, 1)
                    act.wait_ge(e_ready, i * RING + (k + 1))
                    act.wait_ge(spot_ready, i * RING + (k + 1))
                    for e in range(GB):
                        for h in range(2):
                            last = nc.scalar.activation(scaled[:, k, e, h, :], spot[:, k, e, :], ACT.Copy,
                                                        scale=e_[:, k, e, h:h + 1])
                    last.then_inc(scaled_ready, 1)
                each_group(act, scale)

            @block.tensor
            def _(pe):
                def total(i, k, first):
                    pe.wait_ge(scaled_ready, i * RING + (k + 1))
                    if not first:
                        pe.wait_ge(added, i * RING + (k + 1 - RING))
                    pe.wait_ge(rows_in[k], (i + 1) * (16 * GB))
                    for e in range(GB):
                        for h in range(2):
                            last = nc.tensor.matmul(bank[k][:, h * HW:(h + 1) * HW], scaled[:, k, e, h, :],
                                                    rows[:, k, e, h * HW:(h + 1) * HW], start=(e == 0 and h == 0),
                                                    stop=(e == GB - 1), skip_group_check=True)
                    last.then_inc(summed, 1)
                each_group(pe, total)


def finish_heads(nc, sem, c, acc):
    with ExitStack() as ctx, stage(nc, sem) as (sem, pool_sem):
        sb = lambda n, s, d: ctx.enter_context(nc.sbuf_tensor(f"f_{n}", s, d))
        X = c["X"]
        by_head = acc[:, :, :].rearrange("p t (h w) -> p t h w", h=2)
        inv = sb("inv", [P, LOT, 2], F32)
        mean = sb("mean", [P, 2, LOT, 2, HD], F32)
        low = sb("low", [P, 2, LOT, 2, HD], F32)
        dve_done = sem("f_dve_done")
        turn = sem("f_turn")
        low_ready = sem("f_low_ready")
        exp_ready = sem("f_exp_ready")

        with nc.Block() as block:

            @block.vector
            def _(dve):
                steps = Count()

                def link(ins):
                    ins.then_inc(dve_done, 1)
                    dve.wait_ge(dve_done, steps.next())

                def divide(i, s):
                    link(nc.vector.reciprocal(inv[:, :, :], by_head[:, bass.ds(i * LOT, LOT), :, HD]))
                    dve.sem_inc(turn, 1)
                    for t in range(LOT):
                        last = nc.vector.tensor_tensor(mean[:, s, t, :, :], by_head[:, i * LOT + t, :, 0:HD],
                                                       widen(inv[:, t, :], HD), ALU.mult)
                    link(last)
                    nc.vector.tensor_scalar(low[:, s, :, :, :], mean[:, s, :, :, :], 0.0, None,
                                            ALU.min).then_inc(low_ready, 1)

                def grow(i, s):
                    dve.wait_ge(exp_ready, i + 1)
                    link(nc.vector.scalar_tensor_tensor(mean[:, s, :, :, :].rearrange("p t h n -> p (t h n)"),
                                                        mean[:, s, :, :, :].rearrange("p t h n -> p (t h n)"), 0.0,
                                                        low[:, s, :, :, :].rearrange("p t h n -> p (t h n)"),
                                                        ALU.max, ALU.add))
                    dve.sem_inc(turn, 1)
                    xs = X[:, bass.ds(i * LOT, LOT), :].rearrange("p t d -> p (t d)")
                    link(nc.vector.scalar_tensor_tensor(xs, mean[:, s, :, :, :].rearrange("p t h n -> p (t h n)"), -1.0,
                                                        xs, ALU.add, ALU.add))

                for i in range(NLOT):
                    divide(i, i % 2)
                    if i:
                        grow(i - 1, (i - 1) % 2)
                grow(NLOT - 1, (NLOT - 1) % 2)

            @block.scalar
            def _(act):
                for i in range(NLOT):
                    act.wait_ge(low_ready, i + 1)
                    nc.scalar.activation(low[:, i % 2, :, :, :], low[:, i % 2, :, :, :], ACT.Exp).then_inc(exp_ready, 1)


def build(nc, a, out):
    with ExitStack() as ctx:
        def sb(name, shape, dt):
            return ctx.enter_context(nc.sbuf_tensor(name, shape, dt))

        def sem(name):
            return ctx.enter_context(nc.semaphore(name))

        bank = [ctx.enter_context(nc.psum_tensor(f"bank{b}", [P, 512], F32)) for b in range(8)]
        dram = {
            "sorted_edges": nc.dram_tensor("sorted_edges", (FILLS * P * FILL, REC), I32).ap(),
            "table0": nc.dram_tensor("table0", (NT * P, D), F32).ap(),
            "table1": nc.dram_tensor("table1", (NT * P, ROW1), F32).ap(),
            "source_score": nc.dram_tensor("source_score", (NT, 2 * P), F32).ap(),
            "xn": nc.dram_tensor("dram_xn", (NT * P, D), F32).ap(),
            "sent": nc.dram_tensor("dram_sent", (BLOCKS_MAX * P, D), F32).ap(),
            "eid": nc.dram_tensor("dram_eid", (P,), I32).ap(),
            "group_tile": nc.dram_tensor("group_tile", (-(-NGROUP // P) * P,), I32).ap(),
        }
        c = {
            "X": sb("X", [P, NT, D], F32),
            "ident": sb("ident", [P, P], F32),
            "tri": sb("tri", [P, P], F32),
            "ones": sb("ones", [P, P], F32),
            "iota": sb("iota", [P, P], F32),
            "tid": sb("tid", [1, NGROUP], I32),
        }
        sort_and_project(nc, sem, bank, c, a, dram)
        gather_sum0(nc, sem, bank, c, dram)
        for layer in range(2):
            if layer == 1:
                project_heads(nc, sem, bank, c, a, dram)
                with nc.sbuf_tensor("acc", [P, NT, 2 * HW], F32) as acc:
                    gather_heads(nc, sem, bank, c, dram, acc)
                    finish_heads(nc, sem, c, acc)
            with ExitStack() as inner:
                m = dict(MOE[layer])
                tensor = lambda n, s, d: inner.enter_context(nc.sbuf_tensor(f"m{layer}_{n}", s, d))
                dram["made"] = nc.dram_tensor(f"dram_made{layer}", (m["blocks"] * P, D), F32).ap()
                m["gates"] = tensor("gates", [P, 2, NT], F32)
                m["gates_by"] = tensor("gates_by", [P, NT, m["E"]], F32)
                m["pos"] = tensor("pos", [P, 2 * NT], I32)
                m["eid"] = tensor("eid", [1, P], I32)
                route(nc, sem, bank, c, a, dram, layer, m)
                experts(nc, sem, bank, c, a, dram, layer, m)
                combine(nc, sem, bank, c, a, dram, layer, m, out if layer == 1 else None)


_INS = ['x', 'src', 'dst', 'edge_weight', 'L0_gnn_W', 'L0_ffn_router_w1', 'L0_ffn_router_b1', 'L0_ffn_router_w2',
        'L0_ffn_router_b2', 'L0_ffn_expert_w1', 'L0_ffn_expert_b1', 'L0_ffn_expert_w2', 'L0_ffn_expert_b2',
        'L0_ffn_expert_w3', 'L0_ffn_expert_b3', 'L1_gnn_W', 'L1_gnn_b', 'L1_gnn_a', 'L1_ffn_gate_w',
        'L1_ffn_gate_b', 'L1_ffn_w1', 'L1_ffn_b1', 'L1_ffn_w2', 'L1_ffn_b2', 'L1_ffn_gamma', 'L1_ffn_beta']


def kernel(**inputs):
    import numpy as _np
    import concourse.bacc as _bacc
    from concourse import mybir as _mybir
    from concourse.bass_utils import run_bass_kernel_spmd as _run

    nc = _bacc.Bacc("TRN2", target_bir_lowering=False, num_devices=1)
    arrays, args = {}, {}
    for name in _INS:
        v = _np.ascontiguousarray(inputs[name])
        arrays[f"in_{name}_dram"] = v
        args[name] = nc.dram_tensor(f"in_{name}_dram", v.shape, _mybir.dt.from_np(v.dtype), kind="ExternalInput").ap()
    out = nc.dram_tensor("out_0_dram", (N, D), _mybir.dt.float32, kind="ExternalOutput").ap()
    build(nc, args, out)
    r = _run(nc, [arrays], core_ids=[0])
    return r.results[0]["out_0_dram"]
```

```python
from contextlib import ExitStack, contextmanager

import concourse.bass as bass
from concourse import mybir

ALU = mybir.AluOpType
ACT = mybir.ActivationFunctionType
AX = mybir.AxisListType
F32 = mybir.dt.float32
BF16 = mybir.dt.bfloat16
I32 = mybir.dt.int32

P = 128
EPS = 1e-5
SLOPE = 0.2

N, D, EDGES = 6250, 256, 206250
NT = -(-N // P)
LAST = N - (NT - 1) * P
KD = D // P

LANE = -(-EDGES // P)
LANE_LAST = EDGES - (P - 1) * LANE
CHUNK = 26
NCHUNK = LANE // CHUNK
BUCKETS = NT + 1
assert NCHUNK * CHUNK == LANE and NCHUNK % 2 == 0

GROUP = 256
GB = GROUP // P
RING = 8
NGROUP = (EDGES + NT * (GROUP - 1)) // GROUP
SLOTS = NGROUP * GROUP
FILLS = 8
FILL = -(-(SLOTS + P) // (FILLS * P))
REC = 3
assert P * LANE - EDGES <= P

HD = D // 2
HW = HD + 1
ROW1 = 2 * HW + 2


class Count:

    def __init__(self):
        self.n, self.i, self.k = 0, None, 0

    def enter(self, i, per, start=0):
        self.i, self.per, self.k, self.start = i, per, 0, start

    def next(self):
        if self.i is None:
            self.n += 1
            return self.n
        self.k += 1
        return self.i * self.per + (self.n + self.k - self.start * self.per)

    def leave(self, count):
        assert self.k == self.per, (self.k, self.per)
        self.n += self.per * count
        self.i = None


def peeled(engine, count, body):
    body(0, True)
    with engine.Fori(1, count) as i:
        body(i, False)


def each_group(engine, step):
    for k in range(RING):
        step(0, k, True)
    with engine.Fori(1, NGROUP // RING) as i:
        for k in range(RING):
            step(i, k, False)
    for k in range(NGROUP % RING):
        step(NGROUP // RING, k, False)


@contextmanager
def stage(nc, kept):
    own = []

    def sem(name):
        own.append(nc.alloc_semaphore(name=name))
        return own[-1]

    yield sem, kept
    nc.clear_and_free_semaphores(own)
    nc.all_engine_barrier()


def tile_rows(dram, t):
    return dram[bass.ds(t * P, P), :]


def spread(ap, n):
    return ap.unsqueeze(1).to_broadcast([ap.shape[0], n, ap.shape[1]])


def widen(ap, n):
    return ap.unsqueeze(2).to_broadcast([ap.shape[0], ap.shape[1], n])


def sort_and_project(nc, sem, bank, c, a, dram):
    with ExitStack() as ctx, stage(nc, sem) as (sem, pool_sem):
        sb = lambda n, s, d: ctx.enter_context(nc.sbuf_tensor(n, s, d))
        X, ident, tri, ones, iota = c["X"], c["ident"], c["tri"], c["ones"], c["iota"]
        lane_src = sb("lane_src", [P, LANE], I32)
        lane_dst = sb("lane_dst", [P, LANE], I32)
        lane_w = sb("lane_w", [P, LANE], F32)
        tile_i = sb("tile_i", [P, LANE], I32)
        place_i = sb("place_i", [P, LANE], I32)
        tile_f = sb("tile_f", [P, LANE], F32)
        rec = sb("rec", [P, LANE, REC], I32)
        rec_f = rec[:, :, :].bitcast(F32)
        tile_h = sb("tile_h", [P, LANE], BF16)
        hits = sb("hits", [P, LANE], BF16)
        fill = sb("fill", [P, FILL, REC], F32)
        bucket_iota = sb("bucket_iota", [P, BUCKETS, CHUNK], F32)
        carry_mask = sb("carry_mask", [P, BUCKETS, CHUNK], F32)
        member = sb("member", [P, BUCKETS, CHUNK], F32)
        ranks = sb("ranks", [P, BUCKETS, CHUNK], F32)
        own = sb("own", [P, BUCKETS, CHUNK], F32)
        first_col = sb("first_col", [P, BUCKETS], F32)
        run = sb("run", [P, BUCKETS], F32)
        lane_count = sb("lane_count", [P, BUCKETS], F32)
        groups_i = sb("groups_i", [P, 2, BUCKETS], I32)
        groups = sb("groups", [P, BUCKETS], F32)
        group_end = sb("group_end", [P, BUCKETS], F32)
        group_start = sb("group_start", [P, BUCKETS], F32)
        NQ = -(-NGROUP // P)
        group_no = sb("group_no", [P, NQ], F32)
        past = sb("past", [P, NQ, NT], F32)
        tid_f = sb("tid_f", [P, NQ], F32)
        tid_i = sb("tid_i", [P, NQ], I32)
        pos_f = sb("pos_f", [P, CHUNK], F32)
        pos_ring = sb("pos_ring", [P, 2, CHUNK], I32)
        rec_ring = sb("rec_ring", [P, 2, CHUNK, REC], I32)
        Wn = sb("Wn", [P, KD, D], F32)
        WT = sb("WT", [P, KD, D], F32)
        stats = sb("stats", [P, 2, 6], F32)
        moments = sb("moments", [P, 2, 2], F32)
        dev = sb("dev", [P, 2], F32)
        rstd = sb("rstd", [P, 2], F32)
        xn = sb("xn", [P, 2, D], F32)
        xT = sb("xT", [P, 2, KD, P], F32)
        xp = sb("xp", [P, 2, D], F32)

        zeros = sb("zeros", [P, D], F32)
        cleared = sem("a_cleared")
        pads_set = sem("a_pads_set")
        fill_set = sem("a_fill_set")
        consts_set = sem("a_consts_set")
        edges_in = sem("a_edges_in")
        x_in = sem("a_x_in")
        w_in = sem("a_w_in")
        filled = sem("a_filled")
        tile_ready = sem("a_tile_ready")
        place_ready = sem("a_place_ready")
        rec_ready = sem("a_rec_ready")
        w_turned = sem("a_w_turned")
        w_ready = sem("a_w_ready")
        dve_done = sem("a_dve_done")
        counted = sem("a_counted")
        summed = sem("a_summed")
        ranked = sem("a_ranked")
        scattered = [pool_sem(f"a_scattered{s}") for s in range(2)]
        var_ready = sem("a_var_ready")
        dev_ready = sem("a_dev_ready")
        xn_ready = sem("a_xn_ready")
        x_turned = sem("a_x_turned")
        xT_ready = sem("a_xT_ready")
        projected = sem("a_projected")
        xp_ready = sem("a_xp_ready")
        stored = [sem(f"a_stored{s}") for s in range(2)]
        tid_ready = sem("a_tid_ready")
        tid_out = sem("a_tid_out")
        tid_in = sem("a_tid_in")
        turn = sem("a_turn")
        pool_done = sem("a_pool_done")

        psW = bank[0][:, :].rearrange("p (k o) -> p k o", k=KD)
        psC = bank[1]
        psT = [bank[2 + s][:, 0:D].rearrange("p (k n) -> p k n", k=KD) for s in range(2)]
        psP = [bank[4 + s][:, 0:D] for s in range(2)]

        table = dram["table0"]
        sorted_edges = dram["sorted_edges"]

        with nc.Block() as block:

            @block.sync
            def _(sp):
                sp.wait_ge(pads_set, 4)
                cut = (P - 1) // 16 * 16
                for name, lanes in (("src", lane_src), ("dst", lane_dst), ("edge_weight", lane_w)):
                    flat = a[name]
                    for lo, hi in ((0, cut), (cut, P - 1)):
                        sp.dma_start(lanes[lo:hi, :], flat[lo * LANE:hi * LANE].rearrange(
                            "(p t) -> p t", t=LANE)).then_inc(edges_in, 16)
                    sp.dma_start(lanes[P - 1:P, 0:LANE_LAST], flat[(P - 1) * LANE:EDGES].rearrange(
                        "(p t) -> p t", p=1)).then_inc(edges_in, 16)
                full = (NT - 1) * P
                sp.dma_start(X[:, 0:NT - 1, :], a["x"][0:full, :].rearrange(
                    "(t p) d -> p t d", p=P)).then_inc(x_in, 16)
                sp.dma_start(X[0:LAST, NT - 1, :], a["x"][full:N, :]).then_inc(x_in, 16)
                sp.dma_start(Wn[:, :, :], a["L0_gnn_W"].rearrange("(k p) d -> p k d", p=P)).then_inc(w_in, 16)
                sp.wait_ge(fill_set, 3)
                for q in range(FILLS):
                    sp.dma_start(sorted_edges[q * P * FILL:(q + 1) * P * FILL, :].rearrange(
                        "(p s) c -> p s c", p=P), fill[:, :, :].bitcast(I32)).then_inc(filled, 16)
                sp.dma_start(dram["sent"].rearrange("(p r) d -> p r d", p=P),
                             zeros[:, :].unsqueeze(1).to_broadcast([P, BLOCKS_MAX, D])).then_inc(cleared, 16)
                sp.wait_ge(tid_ready, 1)
                sp.dma_start(dram["group_tile"][0:NQ * P].rearrange("(p q) -> p q", p=P),
                             tid_i[:, :]).then_inc(tid_out, 16)
                sp.wait_ge(tid_out, 16)
                sp.dma_start(c["tid"][0:1, :], dram["group_tile"][0:NGROUP].rearrange(
                    "(p g) -> p g", p=1)).then_inc(tid_in, 16)
                with sp.Fori(0, NT // 2) as i:
                    for s in range(2):
                        sp.wait_ge(xp_ready, i * 2 + s + 1)
                        sp.dma_start(tile_rows(table, i * 2 + s), xp[:, s, :]).then_inc(stored[s], 16)
                sp.wait_ge(xp_ready, NT)
                sp.dma_start(tile_rows(table, NT - 1), xp[:, 0, :]).then_inc(stored[0], 16)
                sp.wait_ge(stored[0], 16 * (NT - NT // 2))
                sp.wait_ge(stored[1], 16 * (NT // 2))
                sp.wait_ge(tid_in, 16)
                sp.wait_ge(cleared, 16)

            @block.gpsimd
            def _(pool):
                nc.gpsimd.iota(bucket_iota[:, :, :], pattern=[[1, BUCKETS], [0, CHUNK]], base=0,
                               channel_multiplier=0, allow_small_or_imprecise_dtypes=True).then_inc(consts_set, 1)
                nc.gpsimd.iota(group_no[:, :], pattern=[[1, NQ]], base=0, channel_multiplier=NQ,
                               allow_small_or_imprecise_dtypes=True).then_inc(consts_set, 1)
                nc.gpsimd.iota(iota[:, :], pattern=[[1, P]], base=0, channel_multiplier=0,
                               allow_small_or_imprecise_dtypes=True).then_inc(consts_set, 1)
                nc.gpsimd.memset(ident[:, :], 0.0).then_inc(pool_done, 1)
                nc.gpsimd.memset(tri[:, :], 1.0).then_inc(pool_done, 1)
                nc.gpsimd.memset(ones[:, :], 1.0).then_inc(consts_set, 1)
                pool.wait_ge(pool_done, 2)
                nc.gpsimd.affine_select(out=ident[:, :], in_=ident[:, :], compare_op=ALU.not_equal, fill=1.0,
                                        base=0, pattern=[[-1, P]], channel_multiplier=1).then_inc(consts_set, 1)
                nc.gpsimd.affine_select(out=tri[:, :], in_=tri[:, :], compare_op=ALU.is_gt, fill=0.0,
                                        base=0, pattern=[[1, P]], channel_multiplier=-1).then_inc(consts_set, 1)
                pool.wait_ge(filled, 16 * FILLS)

                with pool.Fori(0, NCHUNK // 2) as i:
                    for s in range(2):
                        pool.wait_ge(ranked, i * 2 + s + 1)
                        pool.sem_inc(turn, 1)
                        for t in range(CHUNK):
                            nc.gpsimd.indirect_dma_start(
                                sorted_edges[:, :], bass.IndirectOffsetOnAxis(pos_ring[:, s, t:t + 1], 0),
                                rec_ring[:, s, t, :], None).then_inc(scattered[s], 16)
                for s in range(2):
                    pool.wait_ge(scattered[s], NCHUNK // 2 * CHUNK * 16)

            @block.vector
            def _(dve):
                steps = Count()

                def link(ins):
                    ins.then_inc(dve_done, 1)
                    dve.wait_ge(dve_done, steps.next())

                nc.vector.memset(lane_src[96:P, LANE_LAST:LANE], NT * P).then_inc(pads_set, 1)
                nc.vector.memset(lane_dst[96:P, LANE_LAST:LANE], 0).then_inc(pads_set, 1)
                nc.vector.memset(lane_w[96:P, LANE_LAST:LANE], 0.0).then_inc(pads_set, 1)
                nc.vector.memset(X[:, NT - 1, :], 0.0).then_inc(pads_set, 1)
                nc.vector.memset(zeros[:, :], 0.0).then_inc(fill_set, 1)
                nc.vector.memset(fill[:, :, 0], -1.0).then_inc(fill_set, 1)
                nc.vector.memset(fill[:, :, 1:REC], 0.0).then_inc(fill_set, 1)
                link(nc.vector.memset(carry_mask[:, :, :], 1.0))
                nc.vector.memset(carry_mask[:, :, 0], 0.0)
                dve.wait_ge(edges_in, 16 * 9)
                link(nc.vector.tensor_scalar(tile_i[:, :], lane_src[:, :], 7, None, ALU.arith_shift_right))
                dve.sem_inc(tile_ready, 1)
                link(nc.vector.tensor_copy(tile_h[:, :], tile_i[:, :]))
                for b in range(BUCKETS):
                    link(nc.vector.tensor_scalar(hits[:, :], tile_h[:, :], float(b), None, ALU.is_equal,
                                                 ALU.add, accum_out=lane_count[:, b:b + 1]))
                dve.sem_inc(counted, 1)
                nc.vector.tensor_scalar(place_i[:, :], lane_src[:, :], P - 1, None,
                                        ALU.bitwise_and).then_inc(place_ready, 1)
                dve.wait_ge(summed, 1)
                link(nc.vector.tensor_scalar(groups_i[:, 0, :], psC[:, BUCKETS:2 * BUCKETS], float(GROUP - 1), None,
                                             ALU.add))
                link(nc.vector.tensor_scalar(groups_i[:, 1, :], groups_i[:, 0, :], GROUP.bit_length() - 1, None,
                                             ALU.arith_shift_right))
                link(nc.vector.tensor_copy(groups[:, :], groups_i[:, 1, :]))
                dve.wait_ge(consts_set, 6)
                link(nc.vector.tensor_tensor_scan(group_end[:, :], ones[:, 0:BUCKETS], groups[:, :], 0.0,
                                                  ALU.mult, ALU.add))
                link(nc.vector.tensor_tensor(group_start[:, :], group_end[:, :], groups[:, :], ALU.subtract))
                link(nc.vector.memset(group_start[:, NT:NT + 1], float(NGROUP)))
                link(nc.vector.scalar_tensor_tensor(run[:, :], group_start[:, :], float(GROUP), psC[:, 0:BUCKETS],
                                                    ALU.mult, ALU.add))
                link(nc.vector.tensor_tensor(past[:, :, :], spread(group_end[:, 0:NT], NQ),
                                             widen(group_no[:, :], NT), ALU.is_le))
                link(nc.vector.tensor_reduce(tid_f[:, :], past[:, :, :], AX.X, ALU.add))
                nc.vector.tensor_scalar(tid_i[:, :], tid_f[:, :], float(NT - 1), None, ALU.min).then_inc(tid_ready, 1)

                def rank(t0, s, wait_slot):
                    link(nc.vector.tensor_tensor(member[:, :, :], bucket_iota[:, :, :],
                                                 spread(tile_f[:, bass.ds(t0, CHUNK)], BUCKETS), ALU.is_equal))
                    link(nc.vector.tensor_copy(first_col[:, :], member[:, :, 0]))
                    link(nc.vector.tensor_tensor(member[:, :, 0], member[:, :, 0], run[:, :], ALU.add))
                    link(nc.vector.tensor_tensor_scan(ranks[:, :, :].rearrange("p b t -> p (b t)"),
                                                      carry_mask[:, :, :].rearrange("p b t -> p (b t)"),
                                                      member[:, :, :].rearrange("p b t -> p (b t)"), 0.0,
                                                      ALU.mult, ALU.add))
                    link(nc.vector.tensor_copy(member[:, :, 0], first_col[:, :]))
                    nc.vector.tensor_copy(run[:, :], ranks[:, :, CHUNK - 1])
                    link(nc.vector.tensor_tensor(own[:, :, :], member[:, :, :], ranks[:, :, :], ALU.mult))
                    link(nc.vector.tensor_reduce(pos_f[:, :], own[:, :, :].rearrange("p b t -> p t b"), AX.X,
                                                 ALU.add))
                    wait_slot()
                    nc.vector.tensor_scalar(pos_ring[:, s, :], pos_f[:, :], -1.0, None, ALU.add)
                    nc.vector.tensor_copy(rec_ring[:, s, :, :], rec[:, bass.ds(t0, CHUNK), :]).then_inc(ranked, 1)

                RANK_LINKS = 7

                dve.wait_ge(x_in, 32)
                dve.wait_ge(rec_ready, 4)

                def step(i, first):
                    steps.enter(i, 2 * RANK_LINKS + 2 * 3 + 2, 0 if first else 1)
                    for s in range(2):
                        def slot_free(s=s):
                            if not first:
                                dve.wait_ge(scattered[s], i * (16 * CHUNK))
                        rank((i * 2 + s) * CHUNK, s, slot_free)
                        link(nc.vector.bn_stats(stats[:, s, :], X[:, i * 2 + s, :]))
                        dve.sem_inc(turn, 1)
                        link(nc.vector.bn_aggr(moments[:, s, :], stats[:, s, :]))
                        link(nc.vector.tensor_scalar(moments[:, s, 1:2], moments[:, s, 1:2], EPS, None, ALU.add))
                        nc.vector.tensor_copy(dev[:, s:s + 1], moments[:, s, 1:2]).then_inc(var_ready, 1)
                        dve.wait_ge(dev_ready, i * 2 + s + 1)
                        link(nc.vector.reciprocal(rstd[:, s:s + 1], dev[:, s:s + 1]))
                        if not first:
                            dve.wait_ge(x_turned, i * 2 + s - 1)
                        nc.vector.tensor_scalar(xn[:, s, :], X[:, i * 2 + s, :], moments[:, s, 0:1],
                                                rstd[:, s:s + 1], ALU.subtract, ALU.mult).then_inc(xn_ready, 1)

                step(0, True)
                steps.leave(1)
                with dve.Fori(1, NT // 2) as i:
                    step(i, False)
                steps.leave(NT // 2 - 1)
                t = NT - 1
                link(nc.vector.bn_stats(stats[:, 0, :], X[:, t, :]))
                link(nc.vector.bn_aggr(moments[:, 0, :], stats[:, 0, :]))
                link(nc.vector.tensor_scalar(moments[:, 0, 1:2], moments[:, 0, 1:2], EPS, None, ALU.add))
                nc.vector.tensor_copy(dev[:, 0:1], moments[:, 0, 1:2]).then_inc(var_ready, 1)
                dve.wait_ge(dev_ready, NT)
                link(nc.vector.reciprocal(rstd[:, 0:1], dev[:, 0:1]))
                dve.wait_ge(x_turned, NT - 2)
                nc.vector.tensor_scalar(xn[:, 0, :], X[:, t, :], moments[:, 0, 0:1],
                                        rstd[:, 0:1], ALU.subtract, ALU.mult).then_inc(xn_ready, 1)
                with dve.Fori(NT // 2, NCHUNK // 2) as i:
                    steps.enter(i, 2 * RANK_LINKS, NT // 2)
                    for s in range(2):
                        rank((i * 2 + s) * CHUNK, s, lambda s=s: dve.wait_ge(scattered[s], i * (16 * CHUNK)))

            @block.scalar
            def _(act):
                act.wait_ge(w_turned, 1)
                nc.scalar.activation(WT[:, :, :], psW, ACT.Copy).then_inc(w_ready, 1)
                act.wait_ge(edges_in, 16 * 9)
                nc.scalar.activation(rec_f[:, :, 1], lane_w[:, :], ACT.Copy).then_inc(rec_ready, 1)
                nc.scalar.activation(rec[:, :, 2], lane_dst[:, :], ACT.Copy).then_inc(rec_ready, 1)
                act.wait_ge(tile_ready, 1)
                nc.scalar.activation(tile_f[:, :], tile_i[:, :], ACT.Copy).then_inc(rec_ready, 1)
                act.wait_ge(place_ready, 1)
                nc.scalar.activation(rec_f[:, :, 0], place_i[:, :], ACT.Copy).then_inc(rec_ready, 1)

                def step(t, s, first, i):
                    act.wait_ge(var_ready, t + 1)
                    nc.scalar.activation(dev[:, s:s + 1], dev[:, s:s + 1], ACT.Sqrt).then_inc(dev_ready, 1)
                    act.wait_ge(x_turned, t + 1)
                    if not first:
                        act.wait_ge(projected, t - 1)
                    nc.scalar.activation(xT[:, s, :, :], psT[s], ACT.Copy).then_inc(xT_ready, 1)
                    act.wait_ge(projected, t + 1)
                    if not first:
                        act.wait_ge(stored[s], i * 16)
                    nc.scalar.activation(xp[:, s, :], psP[s], ACT.Copy).then_inc(xp_ready, 1)

                for s in range(2):
                    step(s, s, True, 0)
                with act.Fori(1, NT // 2) as i:
                    for s in range(2):
                        step(i * 2 + s, s, False, i)
                step(NT - 1, 0, False, NT // 2)

            @block.tensor
            def _(pe):
                pe.wait_ge(consts_set, 6)
                pe.wait_ge(w_in, 16)
                for k in range(KD):
                    for o in range(KD):
                        last = nc.tensor.transpose(psW[:, k, o * P:(o + 1) * P], Wn[:, o, k * P:(k + 1) * P],
                                                   ident[:, :])
                last.then_inc(w_turned, 1)
                pe.wait_ge(counted, 1)
                nc.tensor.matmul(psC[:, 0:BUCKETS], tri[:, :], lane_count[:, :], start=True, stop=True)
                nc.tensor.matmul(psC[:, BUCKETS:2 * BUCKETS], ones[:, :], lane_count[:, :], start=True,
                                 stop=True).then_inc(summed, 1)
                pe.wait_ge(w_ready, 1)

                def step(t, s, first):
                    pe.wait_ge(xn_ready, t + 1)
                    if not first:
                        pe.wait_ge(xT_ready, t - 1)
                    for k in range(KD):
                        last = nc.tensor.transpose(psT[s][:, k, :], xn[:, s, k * P:(k + 1) * P], ident[:, :])
                    last.then_inc(x_turned, 1)
                    pe.wait_ge(xT_ready, t + 1)
                    if not first:
                        pe.wait_ge(xp_ready, t - 1)
                    for k in range(KD):
                        last = nc.tensor.matmul(psP[s], xT[:, s, k, :], WT[:, k, :], start=(k == 0),
                                                stop=(k == KD - 1))
                    last.then_inc(projected, 1)

                for s in range(2):
                    step(s, s, True)
                with pe.Fori(1, NT // 2) as i:
                    for s in range(2):
                        step(i * 2 + s, s, False)
                step(NT - 1, 0, False)


def gather_sum0(nc, sem, bank, c, dram):
    with ExitStack() as ctx, stage(nc, sem) as (sem, pool_sem):
        sb = lambda n, s, d: ctx.enter_context(nc.sbuf_tensor(n, s, d))
        X, iota, tid = c["X"], c["iota"], c["tid"]
        rec = sb("b_rec", [P, RING, GB, REC], I32)
        rec_f = rec[:, :, :, :].bitcast(F32)
        rows = sb("b_rows", [P, RING, GB, D], F32)
        spot = sb("b_spot", [P, RING, GB, P], F32)
        rec_in = [sem(f"b_rec_in{k}") for k in range(RING)]
        rows_in = [pool_sem(f"b_rows_in{k}") for k in range(RING)]
        spot_ready = sem("b_spot_ready")
        summed = sem("b_summed")
        added = sem("b_added")
        turn = sem("b_turn")
        LAG = 4

        with nc.Block() as block:

            @block.sync
            def _(sp):
                def load(i, k, first):
                    if not first:
                        sp.wait_ge(summed, i * RING + (k + 1 - RING))
                    sp.dma_start(rec[:, k, :, :].rearrange("p e c -> p (e c)"),
                                 dram["sorted_edges"][bass.ds((i * RING + k) * GROUP, GROUP), :].rearrange(
                                     "(p e) c -> p (e c)", p=P)).then_inc(rec_in[k], 16)
                each_group(sp, load)

            @block.gpsimd
            def _(pool):
                def gather(i, k, first):
                    pool.wait_ge(rec_in[k], i * 16 + 16)
                    pool.sem_inc(turn, 1)
                    for e in range(GB):
                        nc.gpsimd.indirect_dma_start(
                            rows[:, k, e, :], None, dram["table0"][:, :],
                            bass.IndirectOffsetOnAxis(rec[:, k, e, 2:3], 0)).then_inc(rows_in[k], 16)
                each_group(pool, gather)

            @block.vector
            def _(dve):
                def build(i, k):
                    dve.wait_ge(rec_in[k], i * 16 + 16)
                    for e in range(GB):
                        last = nc.vector.tensor_scalar(spot[:, k, e, :], iota[:, :], rec_f[:, k, e, 0:1],
                                                       rec_f[:, k, e, 1:2], ALU.is_equal, ALU.mult)
                    last.then_inc(spot_ready, 1)

                def add(i, k, very_first=False):
                    dve.wait_ge(summed, i * RING + (k + 1))
                    if not very_first:
                        dve.wait_ge(added, i * RING + k)
                    dve.sem_inc(turn, 1)
                    t = dve.value_load(tid[0:1, bass.ds(i * RING + k, 1)], min_val=0, max_val=NT - 1)
                    nc.vector.tensor_tensor(X[:, bass.ds(t, 1), :].rearrange("p a d -> p (a d)"),
                                            X[:, bass.ds(t, 1), :].rearrange("p a d -> p (a d)"),
                                            bank[k % RING][:, 0:D], ALU.add).then_inc(added, 1)

                def step(i, k, first):
                    build(i, k)
                    if not first or k >= LAG:
                        add(i, k - LAG, first and k == LAG)
                each_group(dve, step)
                for k in range(NGROUP % RING - LAG, NGROUP % RING):
                    add(NGROUP // RING, k)

            @block.tensor
            def _(pe):
                def total(i, k, first):
                    pe.wait_ge(spot_ready, i * RING + (k + 1))
                    if not first:
                        pe.wait_ge(added, i * RING + (k + 1 - RING))
                    pe.wait_ge(rows_in[k], (i + 1) * (16 * GB))
                    for e in range(GB):
                        last = nc.tensor.matmul(bank[k][:, 0:D], spot[:, k, e, :], rows[:, k, e, :],
                                                start=(e == 0), stop=(e == GB - 1))
                    last.then_inc(summed, 1)
                each_group(pe, total)


def blocks_of(experts, ring):
    n = (2 * NT * P + experts * (P - 1)) // P
    return -(-n // ring) * ring


MOE = [
    {"E": 6, "widths": [D, 256, 256, D], "ring": 4, "ahead": 2, "blocks": blocks_of(6, 4), "softmax": True,
     "router_w1": "L0_ffn_router_w1", "router_b1": "L0_ffn_router_b1", "router_w2": "L0_ffn_router_w2",
     "router_b2": "L0_ffn_router_b2", "w": ["L0_ffn_expert_w1", "L0_ffn_expert_w2", "L0_ffn_expert_w3"],
     "b": ["L0_ffn_expert_b1", "L0_ffn_expert_b2"], "b_last": "L0_ffn_expert_b3"},
    {"E": 16, "widths": [D, 512, D], "ring": 3, "ahead": 1, "blocks": blocks_of(16, 3), "softmax": False,
     "router_w2": "L1_ffn_gate_w", "router_b2": "L1_ffn_gate_b", "w": ["L1_ffn_w1", "L1_ffn_w2"],
     "b": ["L1_ffn_b1"], "b_last": "L1_ffn_b2"},
]
BLOCKS_MAX = max(m["blocks"] for m in MOE)
LOT = 7
NLOT = NT // LOT
assert NLOT * LOT == NT


def before(s, ring):
    same = [q for q in range(LOT) if q % ring == s % ring]
    return s - ring if s >= ring else same[-1] - LOT


def after(engine, sem, count):
    if not isinstance(count, int) or count > 0:
        engine.wait_ge(sem, count)


def each_tile(engine, jobs):
    longest = max(lag for _, lag in jobs)

    def lot(i):
        for s in range(LOT):
            for job, lag in jobs:
                if not isinstance(i, int) or i * LOT + s >= lag:
                    job(i, s - lag)
    peel = 1 + -(-longest // LOT)
    for i in range(peel):
        lot(i)
    with engine.Fori(peel, NLOT) as i:
        lot(i)
    for s in range(longest):
        for job, lag in jobs:
            if s < lag:
                job(NLOT, s - lag)


def norm_all(nc, dve, link, steps, turn, X, stats, moments, mr, var_ready, dev_ready):
    with dve.Fori(0, NLOT) as i:
        steps.enter(i, 3)
        for s in range(LOT):
            last = nc.vector.bn_stats(stats[:, s, :], X[:, i * LOT + s, :])
        link(last)
        dve.sem_inc(turn, 1)
        for s in range(LOT):
            last = nc.vector.bn_aggr(moments[:, s, :], stats[:, s, :])
        link(last)
        dve.sem_inc(turn, 1)
        link(nc.vector.tensor_copy(mr[:, bass.ds(i * LOT, LOT), :], moments[:, :, :]))
        dve.sem_inc(turn, 1)
    steps.leave(NLOT)
    nc.vector.tensor_scalar(mr[:, :, 1], mr[:, :, 1], EPS, None, ALU.add).then_inc(var_ready, 1)
    dve.wait_ge(dev_ready, 1)
    link(nc.vector.reciprocal(mr[:, :, 1], mr[:, :, 1]))


def route(nc, sem, bank, c, a, dram, layer, m):
    E = m["E"]
    L = layer
    hidden = "router_w1" in m
    with ExitStack() as ctx, stage(nc, sem) as (sem, pool_sem):
        sb = lambda n, s, d: ctx.enter_context(nc.sbuf_tensor(f"r{L}_{n}", s, d))
        X, ident, tri, ones = c["X"], c["ident"], c["tri"], c["ones"]
        gates, gates_by, pos, eid = m["gates"], m["gates_by"], m["pos"], m["eid"]
        stats = sb("stats", [P, LOT, 6], F32)
        moments = sb("moments", [P, LOT, 2], F32)
        mr = sb("mr", [P, NT, 2], F32)
        xn = sb("xn", [P, LOT, D], F32)
        xT = sb("xT", [P, LOT, KD, P], F32)
        w1 = sb("w1", [P, KD, P], F32)
        b1 = sb("b1", [P, 1], F32)
        w2 = sb("w2", [P, KD, E], F32)
        b2 = sb("b2", [P, E], F32)
        rh = sb("rh", [P, LOT, P], F32)
        logits = sb("logits", [P, NT, E], F32)
        tmp = sb("tmp", [P, NT, E], F32)
        hot = [sb(f"hot{k}", [P, NT, E], F32) for k in range(2)]
        eno = sb("eno", [P, NT, E], F32)
        top = sb("top", [P, 4, NT], F32)
        member = sb("member", [P, E, 2 * NT], F32)
        ranks = sb("ranks", [P, E, 2 * NT], F32)
        carry_mask = sb("carry_mask", [P, E, 2 * NT], F32)
        run = sb("run", [P, 6, E], F32)
        blocks_i = sb("blocks_i", [P, 2, E], I32)
        block_no = sb("block_no", [P, 1], F32)
        past = sb("past", [P, E], F32)
        eid_f = sb("eid_f", [P, 1], F32)
        eid_i = sb("eid_i", [P, 1], I32)

        consts_set = sem(f"r{L}_consts_set")
        w_in = sem(f"r{L}_w_in")
        W0_in = sem(f"r{L}_W0_in")
        var_ready = sem(f"r{L}_var_ready")
        dev_ready = sem(f"r{L}_dev_ready")
        dve_done = sem(f"r{L}_dve_done")
        turn = sem(f"r{L}_turn")
        xn_ready = sem(f"r{L}_xn_ready")
        xn_out = [sem(f"r{L}_xn_out{s}") for s in range(LOT)]
        x_turned = sem(f"r{L}_x_turned")
        xT_ready = sem(f"r{L}_xT_ready")
        h_summed = sem(f"r{L}_h_summed")
        rh_ready = sem(f"r{L}_rh_ready")
        l_summed = sem(f"r{L}_l_summed")
        l_ready = sem(f"r{L}_l_ready")
        exp_asked = sem(f"r{L}_exp_asked")
        exp_ready = sem(f"r{L}_exp_ready")
        counted = sem(f"r{L}_counted")
        summed = sem(f"r{L}_summed")
        eid_ready = sem(f"r{L}_eid_ready")
        eid_out = sem(f"r{L}_eid_out")
        eid_in = sem(f"r{L}_eid_in")

        RT, RH = 3, 2
        psT = [bank[r][:, 0:D].rearrange("p (k n) -> p k n", k=KD) for r in range(RT)]
        psH = [bank[3 + r][:, 0:P] for r in range(RH)]
        psL = [bank[5 + r][:, 0:E] for r in range(RH)]
        psC = bank[7]
        NW = 4 if hidden else 2
        H_LAG, LOGIT_LAG = 1, (3 if hidden else 2)

        with nc.Block() as block:

            @block.sync
            def _(sp):
                if hidden:
                    sp.dma_start(w1[:, :, :], a[m["router_w1"]].rearrange("(k p) h -> p k h", p=P)).then_inc(w_in, 16)
                    with nc.allow_non_contiguous_dma(reason="a bias of 128 features, one on each partition"):
                        sp.dma_start(b1[:, :], a[m["router_b1"]].rearrange("(p o) -> p o", o=1)).then_inc(w_in, 16)
                    sp.dma_start(w2[:, 0, :], a[m["router_w2"]]).then_inc(w_in, 16)
                else:
                    sp.dma_start(w2[:, :, :], a[m["router_w2"]].rearrange("(k p) e -> p k e", p=P)).then_inc(w_in, 16)
                sp.dma_start(b2[:, :], a[m["router_b2"]].rearrange("(o e) -> o e", o=1).to_broadcast([P, E])
                             ).then_inc(w_in, 16)
                with sp.Fori(0, NLOT) as i:
                    for s in range(LOT):
                        sp.wait_ge(xn_ready, i * LOT + (s + 1))
                        sp.dma_start(tile_rows(dram["xn"], i * LOT + s), xn[:, s, :]).then_inc(xn_out[s], 16)
                sp.wait_ge(eid_ready, 1)
                sp.dma_start(dram["eid"].rearrange("(p o) -> p o", o=1), eid_i[:, :]).then_inc(eid_out, 16)
                sp.wait_ge(eid_out, 16)
                sp.dma_start(eid[0:1, :], dram["eid"].rearrange("(o g) -> o g", o=1)).then_inc(eid_in, 16)
                sp.wait_ge(eid_in, 16)
                for s in range(LOT):
                    sp.wait_ge(xn_out[s], 16 * NLOT)

            @block.gpsimd
            def _(pool):
                nc.gpsimd.iota(eno[:, :, :], pattern=[[0, NT], [1, E]], base=-1000, channel_multiplier=0,
                               allow_small_or_imprecise_dtypes=True).then_inc(consts_set, 1)
                nc.gpsimd.iota(block_no[:, :], pattern=[[0, 1]], base=0, channel_multiplier=1,
                               allow_small_or_imprecise_dtypes=True).then_inc(consts_set, 1)

            @block.vector
            def _(dve):
                steps = Count()

                def link(ins):
                    ins.then_inc(dve_done, 1)
                    dve.wait_ge(dve_done, steps.next())

                norm_all(nc, dve, link, steps, turn, X, stats, moments, mr, var_ready, dev_ready)

                def norm(i, s):
                    after(dve, xn_out[s], i * 16)
                    after(dve, x_turned, i * LOT + (s + 1 - LOT))
                    dve.sem_inc(turn, 1)
                    nc.vector.tensor_scalar(xn[:, s, :], X[:, i * LOT + s, :], mr[:, bass.ds(i * LOT + s, 1), 0],
                                            mr[:, bass.ds(i * LOT + s, 1), 1], ALU.subtract,
                                            ALU.mult).then_inc(xn_ready, 1)

                def logit(i, s):
                    dve.wait_ge(l_summed, i * LOT + (s + 1))
                    dve.sem_inc(turn, 1)
                    nc.vector.tensor_tensor(logits[:, bass.ds(i * LOT + s, 1), :].rearrange("p a e -> p (a e)"),
                                            psL[s % LOT % RH], b2[:, :], ALU.add).then_inc(l_ready, 1)

                dve.wait_ge(w_in, 16 * NW)
                each_tile(dve, [(norm, 0), (logit, LOGIT_LAG + 1)])
                dve.wait_ge(l_ready, NT)
                dve.wait_ge(consts_set, 2)
                v = logits
                if m["softmax"]:
                    link(nc.vector.tensor_reduce(top[:, 0, :], logits[:, :, :], AX.X, ALU.max))
                    nc.vector.tensor_tensor(tmp[:, :, :], logits[:, :, :], widen(top[:, 0, :], E),
                                            ALU.subtract).then_inc(exp_asked, 1)
                    dve.wait_ge(exp_ready, 1)
                    link(nc.vector.tensor_reduce(top[:, 0, :], tmp[:, :, :], AX.X, ALU.add))
                    link(nc.vector.reciprocal(top[:, 1, :], top[:, 0, :]))
                    link(nc.vector.tensor_tensor(logits[:, :, :], tmp[:, :, :], widen(top[:, 1, :], E), ALU.mult))
                for k in range(2):
                    link(nc.vector.tensor_reduce(top[:, k, :], v[:, :, :], AX.X, ALU.max))
                    link(nc.vector.tensor_tensor(tmp[:, :, :], v[:, :, :], widen(top[:, k, :], E), ALU.is_equal))
                    link(nc.vector.tensor_tensor(tmp[:, :, :], tmp[:, :, :], eno[:, :, :], ALU.mult))
                    link(nc.vector.tensor_reduce(top[:, 2, :], tmp[:, :, :], AX.X, ALU.min))
                    link(nc.vector.tensor_tensor(hot[k][:, :, :], eno[:, :, :], widen(top[:, 2, :], E), ALU.is_equal))
                    if k == 0:
                        link(nc.vector.scalar_tensor_tensor(v[:, :, :], hot[0][:, :, :], -3.0e38, v[:, :, :],
                                                            ALU.mult, ALU.add))
                nc.vector.tensor_tensor(top[:, 2, :], top[:, 1, :], top[:, 0, :], ALU.subtract).then_inc(exp_asked, 1)
                dve.wait_ge(exp_ready, 2 if m["softmax"] else 1)
                link(nc.vector.tensor_scalar(top[:, 3, :], top[:, 2, :], 1.0, None, ALU.add))
                link(nc.vector.reciprocal(gates[:, 0, :], top[:, 3, :]))
                link(nc.vector.tensor_tensor(gates[:, 1, :], gates[:, 0, :], top[:, 2, :], ALU.mult))
                link(nc.vector.tensor_tensor(tmp[:, :, :], hot[0][:, :, :], widen(gates[:, 0, :], E), ALU.mult))
                link(nc.vector.tensor_tensor(gates_by[:, :, :], hot[1][:, :, :], widen(gates[:, 1, :], E), ALU.mult))
                link(nc.vector.tensor_tensor(gates_by[:, :, :], gates_by[:, :, :], tmp[:, :, :], ALU.add))
                for k in range(2):
                    link(nc.vector.tensor_copy(member[:, :, k * NT:(k + 1) * NT],
                                               hot[k][:, :, :].rearrange("p t e -> p e t")))
                link(nc.vector.tensor_reduce(run[:, 0, :], member[:, :, :], AX.X, ALU.add))
                dve.sem_inc(counted, 1)
                link(nc.vector.memset(carry_mask[:, :, :], 1.0))
                link(nc.vector.memset(carry_mask[:, :, 0], 0.0))
                dve.wait_ge(summed, 1)
                link(nc.vector.tensor_scalar(blocks_i[:, 0, :], psC[:, E:2 * E], float(P - 1), None, ALU.add))
                link(nc.vector.tensor_scalar(blocks_i[:, 1, :], blocks_i[:, 0, :], 7, None, ALU.arith_shift_right))
                link(nc.vector.tensor_copy(run[:, 1, :], blocks_i[:, 1, :]))
                link(nc.vector.tensor_tensor_scan(run[:, 2, :], ones[:, 0:E], run[:, 1, :], 0.0, ALU.mult, ALU.add))
                link(nc.vector.tensor_tensor(run[:, 3, :], run[:, 2, :], run[:, 1, :], ALU.subtract))
                link(nc.vector.scalar_tensor_tensor(run[:, 4, :], run[:, 3, :], float(P), psC[:, 0:E], ALU.mult,
                                                    ALU.add))
                link(nc.vector.tensor_scalar(past[:, :], run[:, 2, :], block_no[:, :], None, ALU.is_le))
                link(nc.vector.tensor_reduce(eid_f[:, :], past[:, :], AX.X, ALU.add))
                nc.vector.tensor_scalar(eid_i[:, :], eid_f[:, :], float(E - 1), None, ALU.min).then_inc(eid_ready, 1)
                link(nc.vector.tensor_copy(run[:, 5, :], member[:, :, 0]))
                link(nc.vector.tensor_tensor(member[:, :, 0], member[:, :, 0], run[:, 4, :], ALU.add))
                link(nc.vector.tensor_tensor_scan(ranks[:, :, :].rearrange("p e t -> p (e t)"),
                                                  carry_mask[:, :, :].rearrange("p e t -> p (e t)"),
                                                  member[:, :, :].rearrange("p e t -> p (e t)"), 0.0,
                                                  ALU.mult, ALU.add))
                link(nc.vector.tensor_copy(member[:, :, 0], run[:, 5, :]))
                link(nc.vector.tensor_tensor(member[:, :, :], member[:, :, :], ranks[:, :, :], ALU.mult))
                link(nc.vector.tensor_reduce(ranks[:, 0, :], member[:, :, :].rearrange("p e t -> p t e"), AX.X,
                                             ALU.add))
                link(nc.vector.memset(pos[:, :, :], 0))
                link(nc.vector.tensor_scalar(pos[:, :, 0:NT], ranks[:, 0, :].rearrange("p (k t) -> p k t", k=2), -1.0,
                                             None, ALU.add))

            @block.scalar
            def _(act):
                act.dma_start(m["W0"][:, :, :, :], a[m["w"][0]].rearrange("e (k p) f -> p e k f", p=P)
                              ).then_inc(W0_in, 16)
                act.wait_ge(var_ready, 1)
                nc.scalar.activation(mr[:, :, 1], mr[:, :, 1], ACT.Sqrt).then_inc(dev_ready, 1)
                if hidden:
                    act.wait_ge(w_in, 16 * NW)

                def turned(i, s):
                    act.wait_ge(x_turned, i * LOT + (s + 1))
                    after(act, h_summed if hidden else l_summed, i * LOT + (s + 1 - LOT))
                    nc.scalar.activation(xT[:, s, :, :], psT[s % RT], ACT.Copy).then_inc(xT_ready, 1)

                def relu(i, s):
                    q = s % LOT
                    act.wait_ge(h_summed, i * LOT + (s + 1))
                    after(act, l_summed, i * LOT + (s + 1 - LOT))
                    nc.scalar.activation(rh[:, q, :], psH[q % RH], ACT.Relu, bias=b1[:, 0:1]).then_inc(rh_ready, 1)

                each_tile(act, [(turned, 0)] + [(relu, H_LAG)] * hidden)
                for n in range(2 if m["softmax"] else 1):
                    act.wait_ge(exp_asked, n + 1)
                    t = tmp[:, :, :] if n == 0 and m["softmax"] else top[:, 2, :]
                    nc.scalar.activation(t, t, ACT.Exp).then_inc(exp_ready, 1)
                act.wait_ge(W0_in, 16)

            @block.tensor
            def _(pe):
                pe.wait_ge(w_in, 16 * NW)

                def bank_free(sm, i, s, ring):
                    after(pe, sm, i * LOT + (s + 1 - s % LOT + before(s % LOT, ring)))

                def turn_x(i, s):
                    pe.wait_ge(xn_ready, i * LOT + (s + 1))
                    bank_free(xT_ready, i, s, RT)
                    for k in range(KD):
                        last = nc.tensor.transpose(psT[s % RT][:, k, :], xn[:, s, k * P:(k + 1) * P], ident[:, :])
                    last.then_inc(x_turned, 1)

                def sum_h(i, s):
                    q = s % LOT
                    pe.wait_ge(xT_ready, i * LOT + (s + 1))
                    bank_free(rh_ready, i, s, RH)
                    for k in range(KD):
                        last = nc.tensor.matmul(psH[q % RH], w1[:, k, :], xT[:, q, k, :], start=(k == 0),
                                                stop=(k == KD - 1))
                    last.then_inc(h_summed, 1)

                def sum_l(i, s):
                    q = s % LOT
                    pe.wait_ge(rh_ready if hidden else xT_ready, i * LOT + (s + 1))
                    bank_free(l_ready, i, s, RH)
                    if hidden:
                        nc.tensor.matmul(psL[q % RH], rh[:, q, :], w2[:, 0, :], start=True,
                                         stop=True).then_inc(l_summed, 1)
                    else:
                        for k in range(KD):
                            last = nc.tensor.matmul(psL[q % RH], xT[:, q, k, :], w2[:, k, :], start=(k == 0),
                                                    stop=(k == KD - 1))
                        last.then_inc(l_summed, 1)

                each_tile(pe, [(turn_x, 0)] + [(sum_h, H_LAG)] * hidden + [(sum_l, LOGIT_LAG)])
                pe.wait_ge(counted, 1)
                nc.tensor.matmul(psC[:, 0:E], tri[:, :], run[:, 0, :], start=True, stop=True)
                nc.tensor.matmul(psC[:, E:2 * E], ones[:, :], run[:, 0, :], start=True,
                                 stop=True).then_inc(summed, 1)


def experts(nc, sem, bank, c, a, dram, layer, m):
    E, widths = m["E"], m["widths"]
    NL = len(widths) - 1
    L = layer
    BLOCKS = m["blocks"]
    BR = m["ring"]
    with ExitStack() as ctx, stage(nc, sem) as (sem, pool_sem):
        sb = lambda n, s, d: ctx.enter_context(nc.sbuf_tensor(f"e{L}_{n}", s, d))
        ident, pos, eid = c["ident"], m["pos"], m["eid"]
        W = [m["W0"]] + [sb(f"W{n}", [P, E, widths[n] // P, widths[n + 1]], F32) for n in range(1, NL)]
        B = [sb(f"B{n}", [P, E, widths[n + 1] // P], F32) for n in range(NL - 1)]
        NB = [E * widths[n + 1] // P for n in range(NL - 1)]
        brow = [sb(f"brow{n}", [NB[n], P], F32) for n in range(NL - 1)]
        xr = sb("xr", [P, max(LOT, 2 * BR), D], F32)
        pos_ring = sb("pos_ring", [P, LOT, 2], I32)
        xb, y = xr[:, 0:BR, :], xr[:, BR:2 * BR, :]
        widest = max(widths)
        hT = sb("hT", [P, BR, widest // P, P], F32)
        z = sb("z", [P, BR, max(widths[1:-1])], F32)

        w_in = [sem(f"e{L}_w_in{n}") for n in range(NL)]
        b_in = sem(f"e{L}_b_in")
        b_turned = sem(f"e{L}_b_turned")
        b_ready = sem(f"e{L}_b_ready")
        xr_in = [sem(f"e{L}_xr_in{s}") for s in range(LOT)]
        pos_ready = sem(f"e{L}_pos_ready")
        sent = [pool_sem(f"e{L}_sent{s}") for s in range(LOT)]
        all_sent = sem(f"e{L}_all_sent")
        xb_in = [sem(f"e{L}_xb_in{s}") for s in range(BR)]
        turned = sem(f"e{L}_turned")
        hT_ready = sem(f"e{L}_hT_ready")
        summed = sem(f"e{L}_summed")
        z_ready = sem(f"e{L}_z_ready")
        y_out = [sem(f"e{L}_y_out{s}") for s in range(BR)]
        turn = sem(f"e{L}_turn")
        psT = [bank[s] for s in range(BR)]
        psZ = [bank[BR + s] for s in range(BR)]
        psB = [psZ[n] for n in range(NL - 1)]
        ITER = BLOCKS // BR
        UNITS = [(n, s) for n in range(NL) for s in range(BR)]
        U = len(UNITS)
        AHEAD = m["ahead"]
        EPART = E // (4 // (NL - 1))
        WPARTS = [(n, e) for n in range(1, NL) for e in range(0, E, EPART)]
        assert len(WPARTS) < NLOT

        with nc.Block() as block:

            @block.sync
            def _(sp):
                for n in range(NL - 1):
                    sp.dma_start(brow[n][:, :], a[m["b"][n]].rearrange("e (k p) -> (e k) p", p=P)).then_inc(b_in, 16)
                with sp.Fori(0, NLOT) as i:
                    for s in range(LOT):
                        sp.wait_ge(pos_ready, i * LOT + (s + 1))
                        sp.dma_start(xr[:, s, :], tile_rows(dram["xn"], i * LOT + s)).then_inc(xr_in[s], 16)
                sp.wait_ge(all_sent, 1)

                def load(b, s):
                    sp.dma_start(xb[:, s, :], tile_rows(dram["sent"], b)).then_inc(xb_in[s], 16)

                def store(i, s):
                    sp.wait_ge(z_ready, i * U + ((NL - 1) * BR + s + 1))
                    sp.dma_start(tile_rows(dram["made"], i * BR + s), y[:, s, :]).then_inc(y_out[s], 16)

                for s in range(BR):
                    load(s, s)
                with sp.Fori(0, ITER - 1) as i:
                    for s in range(BR):
                        sp.wait_ge(turned, i * U + (s + 1))
                        load(i * BR + (BR + s), s)
                    for s in range(BR):
                        store(i, s)
                for s in range(BR):
                    store(ITER - 1, s)
                for s in range(BR):
                    sp.wait_ge(y_out[s], 16 * ITER)

            @block.gpsimd
            def _(pool):
                with pool.Fori(0, NLOT) as i:
                    for s in range(LOT):
                        pool.wait_ge(xr_in[s], i * 16 + 16)
                        pool.sem_inc(turn, 1)
                        for k in range(2):
                            nc.gpsimd.indirect_dma_start(
                                dram["sent"][:, :], bass.IndirectOffsetOnAxis(pos_ring[:, s, k:k + 1], 0),
                                xr[:, s, :], None).then_inc(sent[s], 16)
                for s in range(LOT):
                    pool.wait_ge(sent[s], 32 * NLOT)
                pool.sem_inc(all_sent, 1)

            @block.vector
            def _(dve):
                pos_by_tile = pos[:, :, :].rearrange("p k t -> p t k")

                def places(i, first):
                    for s in range(LOT):
                        if not first:
                            dve.wait_ge(sent[s], i * 32)
                            dve.sem_inc(turn, 1)
                        nc.vector.tensor_copy(pos_ring[:, s, :], pos_by_tile[:, bass.ds(i * LOT + s, 1), :].rearrange(
                            "p a k -> p (a k)")).then_inc(pos_ready, 1)
                peeled(dve, NLOT, places)

                def body(i, first):
                    for u, (n, s) in enumerate(UNITS):
                        dve.wait_ge(summed, i * U + (u + 1))
                        if n == NL - 1 and not first:
                            dve.wait_ge(y_out[s], i * 16)
                        to = y[:, s, :] if n == NL - 1 else z[:, s, 0:widths[n + 1]]
                        nc.vector.tensor_copy(to, psZ[s][:, 0:widths[n + 1]]).then_inc(z_ready, 1)
                peeled(dve, ITER, body)

            @block.scalar
            def _(act):
                for j, (n, e) in enumerate(WPARTS):
                    act.wait_ge(sent[LOT - 1], 32 * (j + 1))
                    act.dma_start(W[n][:, e:e + EPART, :, :], a[m["w"][n]][e:e + EPART].rearrange(
                        "e (k p) f -> p e k f", p=P)).then_inc(w_in[n], 16)
                for n in range(NL - 1):
                    act.wait_ge(b_turned, n + 1)
                    nc.scalar.activation(B[n][:, :, :].rearrange("p e k -> p (e k)"), psB[n][:, 0:NB[n]],
                                         ACT.Copy).then_inc(b_ready, 1)
                act.wait_ge(b_ready, NL - 1)

                def body(i, first):
                    es = []
                    for u, (n, s) in enumerate(UNITS):
                        act.wait_ge(turned, i * U + (u + 1))
                        if n == 0:
                            if not first:
                                act.wait_ge(summed, i * U + (u + 1 - BR))
                            nc.scalar.activation(hT[:, s, 0:KD, :], psT[s][:, 0:D].rearrange(
                                "p (k n) -> p k n", k=KD), ACT.Copy).then_inc(hT_ready, 1)
                            es.append(act.value_load(eid[0:1, bass.ds(i * BR + s, 1)], min_val=0, max_val=E - 1))
                        else:
                            act.sem_inc(turn, 1)
                            for k in range(widths[n] // P):
                                last = nc.scalar.activation(
                                    hT[:, s, k, :], psT[s][:, k * P:(k + 1) * P], ACT.Relu,
                                    bias=B[n - 1][:, bass.ds(es[s], 1), k])
                            last.then_inc(hT_ready, 1)
                peeled(act, ITER, body)

            @block.tensor
            def _(pe):
                pe.wait_ge(b_in, 16 * (NL - 1))
                for n in range(NL - 1):
                    nc.tensor.transpose(psB[n][:, 0:NB[n]], brow[n][:, :],
                                        ident[0:NB[n], 0:NB[n]]).then_inc(b_turned, 1)
                for n in range(1, NL):
                    pe.wait_ge(w_in[n], 16 * (E // EPART))

                pe.wait_ge(b_ready, NL - 1)

                def turn_rows(i, u):
                    n, s = UNITS[u]
                    if n == 0:
                        pe.wait_ge(xb_in[s], i * 16 + 16)
                    else:
                        pe.wait_ge(z_ready, i * U + (u + 1 - BR))
                    src = xb[:, s, :] if n == 0 else z[:, s, :]
                    for k in range(widths[n] // P):
                        last = nc.tensor.transpose(psT[s][:, k * P:(k + 1) * P], src[:, k * P:(k + 1) * P],
                                                   ident[:, :])
                    last.then_inc(turned, 1)

                def product(i, u, expert, first):
                    n, s = UNITS[u]
                    pe.wait_ge(hT_ready, i * U + (u + 1))
                    if n == 0 and not first:
                        pe.wait_ge(z_ready, i * U + (u + 1 - BR))
                    K = widths[n] // P
                    for k in range(K):
                        last = nc.tensor.matmul(psZ[s][:, 0:widths[n + 1]], hT[:, s, k, :],
                                                W[n][:, bass.ds(expert, 1), k, :].rearrange("p a f -> p (a f)"),
                                                start=(k == 0), stop=(k == K - 1))
                    last.then_inc(summed, 1)

                def body(i, first=False, last=False):
                    es = []
                    for u, (n, s) in enumerate(UNITS):
                        if u + AHEAD < U:
                            turn_rows(i, u + AHEAD)
                        elif not last:
                            turn_rows(i + 1, u + AHEAD - U)
                        if n == 0:
                            es.append(pe.value_load(eid[0:1, bass.ds(i * BR + s, 1)], min_val=0, max_val=E - 1))
                        product(i, u, es[s], first)

                for u in range(AHEAD):
                    turn_rows(0, u)
                body(0, first=True)
                with pe.Fori(1, ITER - 1) as i:
                    body(i)
                body(ITER - 1, last=True)


def combine(nc, sem, bank, c, a, dram, layer, m, out=None):
    E = m["E"]
    L = layer
    final = out is not None
    with ExitStack() as ctx, stage(nc, sem) as (sem, pool_sem):
        sb = lambda n, s, d: ctx.enter_context(nc.sbuf_tensor(f"c{L}_{n}", s, d))
        X, ident, ones = c["X"], c["ident"], c["ones"]
        gates, gates_by, pos = m["gates"], m["gates_by"], m["pos"]
        pos_ring = sb("pos_ring", [P, LOT, 2], I32)
        yr = sb("yr", [P, LOT, 2, D], F32)
        bl = sb("bl", [E, D], F32)
        gT = sb("gT", [E, LOT, P], F32)
        gs = sb("gs", [P, LOT, E], F32)
        diag = sb("diag", [P, LOT, 2, P], F32)
        eps = sb("eps", [P, 1], F32)
        stats = sb("stats", [P, LOT, 6], F32)
        moments = sb("moments", [P, LOT, 2], F32)
        dev = sb("dev", [P, LOT], F32)
        rstd = sb("rstd", [P, LOT], F32)
        eps_set = sem(f"c{L}_eps_set")
        w_in = sem(f"c{L}_w_in")
        pos_ready = sem(f"c{L}_pos_ready")
        rows_in = [pool_sem(f"c{L}_rows_in{s}") for s in range(LOT)]
        gs_ready = sem(f"c{L}_gs_ready")
        turned = sem(f"c{L}_turned")
        gT_ready = sem(f"c{L}_gT_ready")
        summed = sem(f"c{L}_summed")
        diag_ready = sem(f"c{L}_diag_ready")
        added = sem(f"c{L}_added")
        stats_ready = sem(f"c{L}_stats_ready")
        var_ready = sem(f"c{L}_var_ready")
        dev_ready = sem(f"c{L}_dev_ready")
        inv_ready = sem(f"c{L}_inv_ready")
        turn = sem(f"c{L}_turn")
        psG = bank[0]
        psB = [bank[1 + r][:, 0:D] for r in range(2)]
        if final:
            y = sb("y", [P, LOT, D], F32)
            w = sb("w", [P, LOT, D], F32)
            gamma = sb("gamma", [P, D], F32)
            beta = sb("beta", [P, D], F32)
            xn_in = [sem(f"c{L}_xn_in{s}") for s in range(LOT)]
            centered = sem(f"c{L}_centered")
            scaled = sem(f"c{L}_scaled")
            tile_done = sem(f"c{L}_tile_done")
            stored = sem(f"c{L}_stored")
        else:
            WIDE = ROW1 + 2
            W = sb("W", [HD, 2, D], F32)
            arow = sb("arow", [4, HD], F32)
            aT = sb("aT", [HD, 4], F32)
            brow = sb("brow", [2, HD], F32)
            bT = sb("bT", [HD, 2], F32)
            WX = sb("WX", [P, KD, WIDE], F32)
            bias = sb("bias", [1, WIDE], F32)
            bias_rows = sb("bias_rows", [P, WIDE], F32)
            xn = sb("xn", [P, LOT, D], F32)
            xT = sb("xT", [P, LOT, KD, P], F32)
            row = sb("row", [P, LOT, WIDE], F32)
            ss = sb("ss", [2, LOT, P], F32)
            b_set = sem(f"c{L}_b_set")
            wx_set = sem(f"c{L}_wx_set")
            a_turned = sem(f"c{L}_a_turned")
            b_turned = sem(f"c{L}_b_turned")
            a_ready = sem(f"c{L}_a_ready")
            ab_summed = sem(f"c{L}_ab_summed")
            w_turned = sem(f"c{L}_w_turned")
            w_ready = sem(f"c{L}_w_ready")
            xn_ready = sem(f"c{L}_xn_ready")
            x_turned = sem(f"c{L}_x_turned")
            xT_ready = sem(f"c{L}_xT_ready")
            projected = sem(f"c{L}_projected")
            row_ready = sem(f"c{L}_row_ready")
            s_turned = sem(f"c{L}_s_turned")
            ss_ready = sem(f"c{L}_ss_ready")
            row_out = [sem(f"c{L}_row_out{s}") for s in range(LOT)]
            psT = [bank[3 + r][:, 0:D].rearrange("p (k n) -> p k n", k=KD) for r in range(2)]
            psR = [bank[5 + r][:, 0:WIDE] for r in range(2)]
            psX = bank[7]
            psS = psX[0:2, 0:P]
        NW = 3 if final else 6

        def whole(i, s):
            return X[:, bass.ds(i * LOT + s, 1), :].rearrange("p a d -> p (a d)")

        def normed(i, s):
            return w[:, s % LOT, :] if final else whole(i, s)

        with nc.Block() as block:

            @block.sync
            def _(sp):
                sp.dma_start(bl[:, :], a[m["b_last"]]).then_inc(w_in, 16)
                if final:
                    for t, name in ((gamma, "L1_ffn_gamma"), (beta, "L1_ffn_beta")):
                        sp.dma_start(t[:, :], a[name].rearrange("(o d) -> o d", o=1).to_broadcast([P, D])
                                     ).then_inc(w_in, 16)

                    def load(i, s):
                        after(sp, added, i * LOT + (s + 1 - LOT))
                        sp.dma_start(y[:, s, :], tile_rows(dram["xn"], i * LOT + s)).then_inc(xn_in[s], 16)

                    def store(i, s):
                        sp.wait_ge(tile_done, i * LOT + (s + 1))
                        t = i * LOT + s
                        if isinstance(t, int) and t == NT - 1:
                            sp.dma_start(out[t * P:N, :], X[0:LAST, t, :]).then_inc(stored, 16)
                        else:
                            sp.dma_start(tile_rows(out, t), whole(i, s)).then_inc(stored, 16)
                    each_tile(sp, [(load, 0), (store, LOT)])
                    sp.wait_ge(stored, 16 * NT)
                else:
                    sp.dma_start(W[:, :, :], a["L1_gnn_W"].rearrange("h d f -> d h f")).then_inc(w_in, 16)
                    sp.dma_start(arow[:, :], a["L1_gnn_a"].rearrange("h (s d) -> (h s) d", s=2)).then_inc(w_in, 16)
                    sp.dma_start(brow[:, :], a["L1_gnn_b"]).then_inc(w_in, 16)
                    sp.wait_ge(b_set, 1)
                    for h in range(2):
                        sp.dma_start(bias[0:1, h * HW:h * HW + HD], a["L1_gnn_b"][h:h + 1, :]).then_inc(w_in, 16)

                    def store_row(i, s):
                        sp.wait_ge(row_ready, i * LOT + (s + 1))
                        sp.dma_start(tile_rows(dram["table1"], i * LOT + s), row[:, s % LOT, 0:ROW1]
                                     ).then_inc(row_out[s % LOT], 16)

                    def store_scores(i, s):
                        sp.wait_ge(ss_ready, i * LOT + (s + 1))
                        sp.dma_start(dram["source_score"][bass.ds(i * LOT + s, 1), :].rearrange(
                            "t (h n) -> (t h) n", h=2), ss[:, s % LOT, :]).then_inc(row_out[s % LOT], 16)
                    each_tile(sp, [(store_row, 0), (store_scores, 1)])
                    for s in range(LOT):
                        sp.wait_ge(row_out[s], 32 * NLOT)

            @block.gpsimd
            def _(pool):
                with pool.Fori(0, NLOT) as i:
                    for s in range(LOT):
                        pool.wait_ge(pos_ready, i * LOT + (s + 1))
                        pool.sem_inc(turn, 1)
                        for k in range(2):
                            nc.gpsimd.indirect_dma_start(
                                yr[:, s, k, :], None, dram["made"][:, :],
                                bass.IndirectOffsetOnAxis(pos_ring[:, s, k:k + 1], 0)).then_inc(rows_in[s], 16)

            @block.vector
            def _(dve):
                pos_by_tile = pos[:, :, :].rearrange("p k t -> p t k")

                def place(i, s):
                    nc.vector.tensor_copy(pos_ring[:, s % LOT, :], pos_by_tile[:, bass.ds(i * LOT + s, 1), :].rearrange(
                        "p a k -> p (a k)")).then_inc(pos_ready, 1)

                for s in range(LOT):
                    place(0, s)
                nc.vector.memset(eps[:, :], EPS).then_inc(eps_set, 1)
                if not final:
                    nc.vector.memset(bias[:, :], 1.0).then_inc(b_set, 1)
                    nc.vector.memset(WX[:, :, :], 0.0).then_inc(wx_set, 1)
                    dve.wait_ge(wx_set, 1)
                    dve.wait_ge(a_turned, 1)
                    nc.vector.tensor_copy(aT[:, :], psX[:, 0:4]).then_inc(a_ready, 1)
                    dve.wait_ge(b_turned, 1)
                    nc.vector.tensor_copy(bT[:, :], psX[:, 0:2]).then_inc(a_ready, 1)
                    dve.wait_ge(w_in, 16 * NW)
                    for h in range(2):
                        dve.wait_ge(ab_summed, h + 1)
                        for which, col in ((1, ROW1 - 2), (0, ROW1)):
                            nc.vector.tensor_copy(bias[0:1, col + h:col + h + 1], psX[0:1, which:which + 1])
                            for k in range(KD):
                                last = nc.vector.tensor_copy(WX[:, k, col + h:col + h + 1],
                                                             psX[:, 16 * (k + 1) + which:16 * (k + 1) + which + 1])
                        last.then_inc(w_ready, 1)
                    for h in range(2):
                        dve.wait_ge(w_turned, h + 1)
                        nc.vector.tensor_copy(WX[:, :, h * HW:h * HW + HD], psX[:, 0:D].rearrange(
                            "p (k n) -> p k n", k=KD)).then_inc(w_ready, 1)
                    dve.wait_ge(ab_summed, 3)
                    nc.vector.tensor_copy(bias_rows[:, :], psR[0]).then_inc(w_ready, 1)
                    dve.wait_ge(w_ready, 5)
                else:
                    dve.wait_ge(w_in, 16 * NW)

                def add(i, s):
                    q = s % LOT
                    dve.wait_ge(summed, i * LOT + (s + 1))
                    dve.sem_inc(turn, 1)
                    place(i, s + LOT)
                    if final:
                        dve.wait_ge(xn_in[q], (i + s // LOT) * 16 + 16)
                        after(dve, scaled, i * LOT + (s + 1 - LOT))
                    dve.sem_inc(turn, 1)
                    nc.vector.tensor_tensor(normed(i, s), psB[q % 2], y[:, q, :] if final else whole(i, s),
                                            ALU.add).then_inc(added, 1)

                def take_stats(i, s):
                    dve.wait_ge(added, i * LOT + (s + 1))
                    dve.sem_inc(turn, 1)
                    nc.vector.bn_stats(stats[:, s % LOT, :], normed(i, s)).then_inc(stats_ready, 1)

                def aggregate(i, s):
                    dve.wait_ge(stats_ready, i * LOT + (s + 1))
                    dve.sem_inc(turn, 1)
                    nc.vector.bn_aggr(moments[:, s % LOT, :], stats[:, s % LOT, :]).then_inc(var_ready, 1)

                def invert(i, s):
                    q = s % LOT
                    dve.wait_ge(dev_ready, i * LOT + (s + 1))
                    nc.vector.reciprocal(rstd[:, q:q + 1], dev[:, q:q + 1]).then_inc(inv_ready, 1)

                def norm(i, s):
                    q = s % LOT
                    dve.wait_ge(inv_ready, i * LOT + (s + 1))
                    after(dve, x_turned, i * LOT + (s + 1 - LOT))
                    dve.sem_inc(turn, 1)
                    nc.vector.tensor_scalar(xn[:, q, :], whole(i, s), moments[:, q, 0:1], rstd[:, q:q + 1],
                                            ALU.subtract, ALU.mult).then_inc(xn_ready, 1)

                def center(i, s):
                    q = s % LOT
                    nc.vector.scalar_tensor_tensor(w[:, q, :], w[:, q, :], moments[:, q, 0:1], gamma[:, :],
                                                   ALU.subtract, ALU.mult).then_inc(centered, 1)

                def scale(i, s):
                    q = s % LOT
                    dve.wait_ge(inv_ready, i * LOT + (s + 1))
                    dve.wait_ge(centered, i * LOT + (s + 1))
                    dve.sem_inc(turn, 1)
                    nc.vector.scalar_tensor_tensor(whole(i, s), w[:, q, :], rstd[:, q:q + 1], whole(i, s),
                                                   ALU.mult, ALU.add).then_inc(scaled, 1)

                def shift(i, s):
                    dve.wait_ge(scaled, i * LOT + (s + 1))
                    dve.sem_inc(turn, 1)
                    nc.vector.tensor_tensor(whole(i, s), whole(i, s), beta[:, :], ALU.add).then_inc(tile_done, 1)

                def rows(i, s):
                    q = s % LOT
                    dve.wait_ge(projected, i * LOT + (s + 1))
                    after(dve, row_out[q], (i + s // LOT) * 32)
                    nc.vector.tensor_tensor(row[:, q, :], psR[q % 2], bias_rows[:, :], ALU.add).then_inc(row_ready, 1)

                if final:
                    ends = [(shift, 9), (scale, 8), (invert, 7), (center, 7)]
                else:
                    ends = [(rows, 13), (norm, 9), (invert, 8)]
                each_tile(dve, ends + [(aggregate, 6), (take_stats, 5), (add, 4)])

            @block.scalar
            def _(act):
                act.wait_ge(eps_set, 1)

                def gates_of(i, s):
                    after(act, turned, i * LOT + (s + 1 - LOT))
                    act.sem_inc(turn, 1)
                    nc.scalar.activation(gs[:, s, :], gates_by[:, bass.ds(i * LOT + s, 1), :].rearrange(
                        "p a e -> p (a e)"), ACT.Copy).then_inc(gs_ready, 1)

                def spread_gates(i, s):
                    after(act, summed, i * LOT + (s + 1 - LOT))
                    act.sem_inc(turn, 1)
                    for k in range(2):
                        last = nc.scalar.activation(diag[:, s % LOT, k, :], ident[:, :], ACT.Copy,
                                                    scale=gates[:, k, bass.ds(i * LOT + s, 1)])
                    last.then_inc(diag_ready, 1)

                def gates_turned(i, s):
                    act.wait_ge(turned, i * LOT + (s + 1))
                    after(act, summed, i * LOT + (s + 1 - LOT))
                    nc.scalar.activation(gT[:, s % LOT, :], psG[0:E, 0:P], ACT.Copy).then_inc(gT_ready, 1)

                def root(i, s):
                    q = s % LOT
                    act.wait_ge(var_ready, i * LOT + (s + 1))
                    after(act, inv_ready, i * LOT + (s + 1 - LOT))
                    nc.scalar.activation(dev[:, q:q + 1], moments[:, q, 1:2], ACT.Sqrt,
                                         bias=eps[:, 0:1]).then_inc(dev_ready, 1)

                def x_copied(i, s):
                    act.wait_ge(x_turned, i * LOT + (s + 1))
                    after(act, projected, i * LOT + (s + 1 - LOT))
                    nc.scalar.activation(xT[:, s % LOT, :, :], psT[s % LOT % 2], ACT.Copy).then_inc(xT_ready, 1)

                def source_scores(i, s):
                    act.wait_ge(s_turned, i * LOT + (s + 1))
                    nc.scalar.activation(ss[:, s % LOT, :], psS, ACT.Copy).then_inc(ss_ready, 1)

                ends = [(root, 6)] if final else [(source_scores, 15), (x_copied, 11), (root, 7)]
                each_tile(act, ends + [(spread_gates, 2), (gates_turned, 2), (gates_of, 0)])

            @block.tensor
            def _(pe):
                pe.wait_ge(w_in, 16 * NW)
                if not final:
                    nc.tensor.transpose(psX[:, 0:4], arow[:, :], ident[0:4, 0:4]).then_inc(a_turned, 1)
                    pe.wait_ge(a_ready, 1)
                    nc.tensor.transpose(psX[:, 0:2], brow[:, :], ident[0:2, 0:2]).then_inc(b_turned, 1)
                    pe.wait_ge(a_ready, 2)
                    for h in range(2):
                        if h:
                            pe.wait_ge(w_ready, h)
                        nc.tensor.matmul(psX[0:1, 0:2], bT[:, h:h + 1], aT[:, 2 * h:2 * h + 2], start=True, stop=True)
                        for k in range(KD):
                            last = nc.tensor.matmul(psX[:, 16 * (k + 1):16 * (k + 1) + 2], W[:, h, k * P:(k + 1) * P],
                                                    aT[:, 2 * h:2 * h + 2], start=True, stop=True)
                        last.then_inc(ab_summed, 1)
                    for h in range(2):
                        pe.wait_ge(w_ready, 2 + h)
                        for k in range(KD):
                            last = nc.tensor.transpose(psX[:, k * P:(k + 1) * P], W[:, h, k * P:(k + 1) * P],
                                                       ident[:, :])
                        last.then_inc(w_turned, 1)
                    nc.tensor.matmul(psR[0], ones[0:1, :], bias[0:1, :], start=True, stop=True).then_inc(ab_summed, 1)
                    pe.wait_ge(w_ready, 5)

                def bank_free(sm, i, s, ring):
                    after(pe, sm, i * LOT + (s + 1 - s % LOT + before(s % LOT, ring)))

                def turn_gates(i, s):
                    pe.wait_ge(gs_ready, i * LOT + (s + 1))
                    bank_free(gT_ready, i, s, 1)
                    nc.tensor.transpose(psG[0:E, 0:P], gs[:, s % LOT, :], ident[:, :]).then_inc(turned, 1)

                def total(i, s):
                    q = s % LOT
                    pe.wait_ge(gT_ready, i * LOT + (s + 1))
                    bank_free(added, i, s, 2)
                    nc.tensor.matmul(psB[q % 2], gT[:, q, :], bl[:, :], start=True, stop=False)
                    pe.wait_ge(diag_ready, i * LOT + (s + 1))
                    pe.wait_ge(rows_in[q], (i + s // LOT) * 32 + 32)
                    for k in range(2):
                        last = nc.tensor.matmul(psB[q % 2], diag[:, q, k, :], yr[:, q, k, :], start=False,
                                                stop=(k == 1))
                    last.then_inc(summed, 1)

                def turn_x(i, s):
                    q = s % LOT
                    pe.wait_ge(xn_ready, i * LOT + (s + 1))
                    bank_free(xT_ready, i, s, 2)
                    for k in range(KD):
                        last = nc.tensor.transpose(psT[q % 2][:, k, :], xn[:, q, k * P:(k + 1) * P], ident[:, :])
                    last.then_inc(x_turned, 1)

                def project(i, s):
                    q = s % LOT
                    pe.wait_ge(xT_ready, i * LOT + (s + 1))
                    bank_free(row_ready, i, s, 2)
                    for k in range(KD):
                        last = nc.tensor.matmul(psR[q % 2], xT[:, q, k, :], WX[:, k, :], start=(k == 0),
                                                stop=(k == KD - 1))
                    last.then_inc(projected, 1)

                def turn_scores(i, s):
                    pe.wait_ge(row_ready, i * LOT + (s + 1))
                    bank_free(ss_ready, i, s, 1)
                    nc.tensor.transpose(psS, row[:, s % LOT, ROW1:WIDE], ident[:, :]).then_inc(s_turned, 1)

                ends = [] if final else [(turn_scores, 14), (project, 12), (turn_x, 10)]
                each_tile(pe, ends + [(total, 3), (turn_gates, 1)])


def gather_heads(nc, sem, bank, c, dram, acc):
    with ExitStack() as ctx, stage(nc, sem) as (sem, pool_sem):
        sb = lambda n, s, d: ctx.enter_context(nc.sbuf_tensor(f"g_{n}", s, d))
        iota, tid = c["iota"], c["tid"]
        rec = sb("rec", [P, RING, GB, REC], I32)
        rec_f = rec[:, :, :, :].bitcast(F32)
        rows = sb("rows", [P, RING, GB, ROW1], F32)
        spot = sb("spot", [P, RING, GB, P], F32)
        scaled = sb("scaled", [P, RING, GB, 2, P], F32)
        ss = sb("ss", [P, RING, 2, P], F32)
        picked = sb("picked", [P, GB, 2, P], F32)
        own = sb("own", [P, RING, GB, 2], F32)
        score = sb("score", [P, RING, GB, 2], F32)
        leaky = sb("leaky", [P, RING, GB, 2], F32)
        e_ = sb("e", [P, RING, GB, 2], F32)
        last_rows = sb("last_rows", [P, 1], F32)
        rec_in = [sem(f"g_rec_in{k}") for k in range(RING)]
        ss_in = [sem(f"g_ss_in{k}") for k in range(RING)]
        rows_in = [pool_sem(f"g_rows_in{k}") for k in range(RING)]
        pad_set = sem("g_pad_set")
        acc_set = sem("g_acc_set")
        spot_ready = sem("g_spot_ready")
        own_ready = sem("g_own_ready")
        score_ready = sem("g_score_ready")
        leaky_ready = sem("g_leaky_ready")
        e_ready = sem("g_e_ready")
        scaled_ready = sem("g_scaled_ready")
        summed = sem("g_summed")
        added = sem("g_added")
        turn = sem("g_turn")
        SCORE_LAG, ADD_LAG = 2, 5

        with nc.Block() as block:

            @block.sync
            def _(sp):
                def load(i, k, first):
                    if not first:
                        sp.wait_ge(summed, i * RING + (k + 1 - RING))
                    sp.dma_start(rec[:, k, :, :].rearrange("p e c -> p (e c)"),
                                 dram["sorted_edges"][bass.ds((i * RING + k) * GROUP, GROUP), :].rearrange(
                                     "(p e) c -> p (e c)", p=P)).then_inc(rec_in[k], 16)
                    t = sp.value_load(tid[0:1, bass.ds(i * RING + k, 1)], min_val=0, max_val=NT - 1)
                    sp.dma_start(ss[:, k, :, :].rearrange("p h n -> p (h n)"),
                                 dram["source_score"][bass.ds(t, 1), :].to_broadcast([P, 2 * P])
                                 ).then_inc(ss_in[k], 16)
                each_group(sp, load)

            @block.gpsimd
            def _(pool):
                nc.gpsimd.memset(last_rows[:, :], 1.0).then_inc(pad_set, 1)
                pool.wait_ge(pad_set, 1)
                nc.gpsimd.affine_select(out=last_rows[:, :], in_=last_rows[:, :], compare_op=ALU.is_ge, fill=0.0,
                                        base=-LAST, pattern=[[0, 1]], channel_multiplier=1).then_inc(pad_set, 1)

                def gather(i, k, first):
                    pool.wait_ge(rec_in[k], i * 16 + 16)
                    pool.sem_inc(turn, 1)
                    for e in range(GB):
                        nc.gpsimd.indirect_dma_start(
                            rows[:, k, e, :], None, dram["table1"][:, :],
                            bass.IndirectOffsetOnAxis(rec[:, k, e, 2:3], 0)).then_inc(rows_in[k], 16)
                each_group(pool, gather)

            @block.vector
            def _(dve):
                nc.vector.memset(acc[:, :, :], 0.0).then_inc(acc_set, 1)
                dve.wait_ge(pad_set, 2)
                dve.wait_ge(acc_set, 1)
                for h in range(2):
                    nc.vector.tensor_copy(acc[:, NT - 1, h * HW + HD:h * HW + HW],
                                          last_rows[:, :]).then_inc(acc_set, 1)
                dve.wait_ge(acc_set, 3)

                def build(i, k):
                    dve.wait_ge(rec_in[k], i * 16 + 16)
                    for e in range(GB):
                        last = nc.vector.tensor_scalar(spot[:, k, e, :], iota[:, :], rec_f[:, k, e, 0:1], None,
                                                       ALU.is_equal)
                    last.then_inc(spot_ready, 1)

                def pick(i, k, very_first):
                    dve.wait_ge(ss_in[k], i * 16 + 16)
                    if not very_first:
                        dve.wait_ge(own_ready, i * RING + k)
                    for e in range(GB):
                        for h in range(2):
                            last = nc.vector.scalar_tensor_tensor(picked[:, e, h, :], iota[:, :],
                                                                  rec_f[:, k, e, 0:1], ss[:, k, h, :], ALU.is_equal,
                                                                  ALU.mult, accum_out=own[:, k, e, h:h + 1])
                    last.then_inc(own_ready, 1)

                def rate(i, k):
                    q = k % RING
                    dve.wait_ge(own_ready, i * RING + (k + 1))
                    dve.wait_ge(rows_in[q], (i + (0 if k < 0 else 1)) * (16 * GB))
                    nc.vector.tensor_tensor(score[:, q, :, :], own[:, q, :, :],
                                            rows[:, q, :, ROW1 - 2:ROW1], ALU.add).then_inc(score_ready, 1)

                def leak(i, k):
                    q = k % RING
                    dve.wait_ge(score_ready, i * RING + (k + 1))
                    nc.vector.scalar_tensor_tensor(leaky[:, q, :, :], score[:, q, :, :], SLOPE, score[:, q, :, :],
                                                   ALU.mult, ALU.max).then_inc(leaky_ready, 1)

                def add(i, k, very_first=False):
                    dve.wait_ge(summed, i * RING + (k + 1))
                    if not very_first:
                        dve.wait_ge(added, i * RING + k)
                    dve.sem_inc(turn, 1)
                    t = dve.value_load(tid[0:1, bass.ds(i * RING + k, 1)], min_val=0, max_val=NT - 1)
                    at = acc[:, bass.ds(t, 1), :].rearrange("p a d -> p (a d)")
                    nc.vector.tensor_tensor(at, at, bank[k % RING][:, 0:2 * HW], ALU.add).then_inc(added, 1)

                def step(i, k, first):
                    scored = not first or k >= SCORE_LAG
                    build(i, k)
                    if scored:
                        rate(i, k - SCORE_LAG)
                    pick(i, k, first and k == 0)
                    if scored:
                        leak(i, k - SCORE_LAG)
                    if not first or k >= ADD_LAG:
                        add(i, k - ADD_LAG, first and k == ADD_LAG)
                each_group(dve, step)
                done = NGROUP % RING
                for k in range(done - SCORE_LAG, done):
                    rate(NGROUP // RING, k)
                    leak(NGROUP // RING, k)
                for k in range(done - ADD_LAG, done):
                    add(NGROUP // RING, k)

            @block.scalar
            def _(act):
                def scale(i, k, first):
                    act.wait_ge(leaky_ready, i * RING + (k + 1))
                    nc.scalar.activation(e_[:, k, :, :], leaky[:, k, :, :], ACT.Exp, scale=-1.0).then_inc(e_ready, 1)
                    act.wait_ge(e_ready, i * RING + (k + 1))
                    act.wait_ge(spot_ready, i * RING + (k + 1))
                    for e in range(GB):
                        for h in range(2):
                            last = nc.scalar.activation(scaled[:, k, e, h, :], spot[:, k, e, :], ACT.Copy,
                                                        scale=e_[:, k, e, h:h + 1])
                    last.then_inc(scaled_ready, 1)
                each_group(act, scale)

            @block.tensor
            def _(pe):
                def total(i, k, first):
                    pe.wait_ge(scaled_ready, i * RING + (k + 1))
                    if not first:
                        pe.wait_ge(added, i * RING + (k + 1 - RING))
                    pe.wait_ge(rows_in[k], (i + 1) * (16 * GB))
                    for e in range(GB):
                        for h in range(2):
                            last = nc.tensor.matmul(bank[k][:, h * HW:(h + 1) * HW], scaled[:, k, e, h, :],
                                                    rows[:, k, e, h * HW:(h + 1) * HW], start=(e == 0 and h == 0),
                                                    stop=(e == GB - 1), skip_group_check=True)
                    last.then_inc(summed, 1)
                each_group(pe, total)


def finish_heads(nc, sem, c, acc):
    with ExitStack() as ctx, stage(nc, sem) as (sem, pool_sem):
        sb = lambda n, s, d: ctx.enter_context(nc.sbuf_tensor(f"f_{n}", s, d))
        X = c["X"]
        by_head = acc[:, :, :].rearrange("p t (h w) -> p t h w", h=2)
        inv = sb("inv", [P, NT, 2], F32)
        mean = sb("mean", [P, 2, LOT, 2, HD], F32)
        grown_exp = sb("grown_exp", [P, 2, LOT, 2, HD], F32)
        inv_ready = sem("f_inv_ready")
        mean_ready = sem("f_mean_ready")
        dve_means = sem("f_dve_means")
        exp_ready = sem("f_exp_ready")
        relu_ready = sem("f_relu_ready")
        grown = sem("f_grown")
        added = sem("f_added")

        DVE_TILES = 2

        def flat(t):
            return t.rearrange("p t h n -> p (t h n)")

        with nc.Block() as block:

            @block.vector
            def _(dve):
                nc.vector.reciprocal(inv[:, :, :], by_head[:, :, :, HD]).then_inc(inv_ready, 1)
                dve.wait_ge(inv_ready, 1)

                def divide(i):
                    if i >= 2:
                        dve.wait_ge(added, i - 1)
                    for t in range(LOT - DVE_TILES, LOT):
                        nc.vector.tensor_tensor(mean[:, i % 2, t, :, :], by_head[:, i * LOT + t, :, 0:HD],
                                                widen(inv[:, i * LOT + t, :], HD), ALU.mult).then_inc(dve_means, 1)

                divide(0)
                for i in range(NLOT):
                    if i + 1 < NLOT:
                        divide(i + 1)
                    s = i % 2
                    e, r = flat(grown_exp[:, s, :, :, :]), flat(mean[:, s, :, :, :])
                    dve.wait_ge(relu_ready, i + 1)
                    nc.vector.scalar_tensor_tensor(r, e, 1.0, r, ALU.min, ALU.add).then_inc(grown, 1)
                    dve.wait_ge(grown, i + 1)
                    xs = X[:, i * LOT:(i + 1) * LOT, :].rearrange("p t d -> p (t d)")
                    nc.vector.scalar_tensor_tensor(xs, r, -1.0, xs, ALU.add, ALU.add).then_inc(added, 1)

            @block.scalar
            def _(act):
                act.wait_ge(inv_ready, 1)

                for i in range(NLOT):
                    s = i % 2
                    if i >= 2:
                        act.wait_ge(added, i - 1)
                    for t in range(LOT - DVE_TILES):
                        for h in range(2):
                            last = nc.scalar.activation(mean[:, s, t, h, :], by_head[:, i * LOT + t, h, 0:HD], ACT.Copy,
                                                        scale=inv[:, i * LOT + t, h:h + 1])
                    last.then_inc(mean_ready, 1)
                    act.wait_ge(mean_ready, i + 1)
                    act.wait_ge(dve_means, (i + 1) * DVE_TILES)
                    nc.scalar.activation(flat(grown_exp[:, s, :, :, :]), flat(mean[:, s, :, :, :]),
                                         ACT.Exp).then_inc(exp_ready, 1)
                    act.wait_ge(exp_ready, i + 1)
                    nc.scalar.activation(flat(mean[:, s, :, :, :]), flat(mean[:, s, :, :, :]),
                                         ACT.Relu).then_inc(relu_ready, 1)


def build(nc, a, out):
    with ExitStack() as ctx:
        def sb(name, shape, dt):
            return ctx.enter_context(nc.sbuf_tensor(name, shape, dt))

        def sem(name):
            return ctx.enter_context(nc.semaphore(name))

        bank = [ctx.enter_context(nc.psum_tensor(f"bank{b}", [P, 512], F32)) for b in range(8)]
        dram = {
            "sorted_edges": nc.dram_tensor("sorted_edges", (FILLS * P * FILL, REC), I32).ap(),
            "table0": nc.dram_tensor("table0", (NT * P, D), F32).ap(),
            "table1": nc.dram_tensor("table1", (NT * P, ROW1), F32).ap(),
            "source_score": nc.dram_tensor("source_score", (NT, 2 * P), F32).ap(),
            "xn": nc.dram_tensor("dram_xn", (NT * P, D), F32).ap(),
            "sent": nc.dram_tensor("dram_sent", (BLOCKS_MAX * P, D), F32).ap(),
            "eid": nc.dram_tensor("dram_eid", (P,), I32).ap(),
            "group_tile": nc.dram_tensor("group_tile", (-(-NGROUP // P) * P,), I32).ap(),
        }
        c = {
            "X": sb("X", [P, NT, D], F32),
            "ident": sb("ident", [P, P], F32),
            "tri": sb("tri", [P, P], F32),
            "ones": sb("ones", [P, P], F32),
            "iota": sb("iota", [P, P], F32),
            "tid": sb("tid", [1, NGROUP], I32),
        }
        sort_and_project(nc, sem, bank, c, a, dram)
        gather_sum0(nc, sem, bank, c, dram)
        for layer in range(2):
            if layer == 1:
                with nc.sbuf_tensor("acc", [P, NT, 2 * HW], F32) as acc:
                    gather_heads(nc, sem, bank, c, dram, acc)
                    finish_heads(nc, sem, c, acc)
            with ExitStack() as inner:
                m = dict(MOE[layer])
                tensor = lambda n, s, d: inner.enter_context(nc.sbuf_tensor(f"m{layer}_{n}", s, d))
                dram["made"] = nc.dram_tensor(f"dram_made{layer}", (m["blocks"] * P, D), F32).ap()
                m["gates"] = tensor("gates", [P, 2, NT], F32)
                m["gates_by"] = tensor("gates_by", [P, NT, m["E"]], F32)
                m["pos"] = tensor("pos", [P, 2, NT + LOT], I32)
                m["eid"] = tensor("eid", [1, P], I32)
                m["W0"] = tensor("W0", [P, m["E"], D // P, m["widths"][1]], F32)
                route(nc, sem, bank, c, a, dram, layer, m)
                experts(nc, sem, bank, c, a, dram, layer, m)
                combine(nc, sem, bank, c, a, dram, layer, m, out if layer == 1 else None)


_INS = ['x', 'src', 'dst', 'edge_weight', 'L0_gnn_W', 'L0_ffn_router_w1', 'L0_ffn_router_b1', 'L0_ffn_router_w2',
        'L0_ffn_router_b2', 'L0_ffn_expert_w1', 'L0_ffn_expert_b1', 'L0_ffn_expert_w2', 'L0_ffn_expert_b2',
        'L0_ffn_expert_w3', 'L0_ffn_expert_b3', 'L1_gnn_W', 'L1_gnn_b', 'L1_gnn_a', 'L1_ffn_gate_w',
        'L1_ffn_gate_b', 'L1_ffn_w1', 'L1_ffn_b1', 'L1_ffn_w2', 'L1_ffn_b2', 'L1_ffn_gamma', 'L1_ffn_beta']


def kernel(**inputs):
    import numpy as _np
    import concourse.bacc as _bacc
    from concourse import mybir as _mybir
    from concourse.bass_utils import run_bass_kernel_spmd as _run

    nc = _bacc.Bacc("TRN2", target_bir_lowering=False, num_devices=1)
    arrays, args = {}, {}
    for name in _INS:
        v = _np.ascontiguousarray(inputs[name])
        arrays[f"in_{name}_dram"] = v
        args[name] = nc.dram_tensor(f"in_{name}_dram", v.shape, _mybir.dt.from_np(v.dtype), kind="ExternalInput").ap()
    out = nc.dram_tensor("out_0_dram", (N, D), _mybir.dt.float32, kind="ExternalOutput").ap()
    build(nc, args, out)
    r = _run(nc, [arrays], core_ids=[0])
    return r.results[0]["out_0_dram"]
```
